# Optimizing a Trainium2 kernel written in Bass

```python
import numpy as np
import jax
import jax.numpy as jnp

def _softmax(x, axis=-1):
    return jax.nn.softmax(x, axis=axis)

def _gelu(x):
    return jax.nn.gelu(x, approximate=True)

def _silu(x):
    return jax.nn.silu(x)

def _sigmoid(x):
    return jax.nn.sigmoid(x)

def _layernorm(x, axis=-1, eps=1e-05):
    m = jnp.mean(x, axis=axis, keepdims=True)
    v = jnp.var(x, axis=axis, keepdims=True)
    return (x - m) / jnp.sqrt(v + eps)

def _scatter_add(tgt, idx, src, axis=0):
    return tgt.at[idx].add(src)

def _segment_sum(src, seg, n):
    return jax.ops.segment_sum(src, seg, n)
kernel_name = 'mk_conv_attn_hybrid_d2_conv_nhwc256_r2_6d79b2'

def setup_inputs(seed: int=0):
    np.random.seed(seed)
    _w = jnp.asarray

    def _rec_inputs():
        import jax
        import jax.numpy as jnp
        _gk = jax.random.key(seed)
        x = 7.22e-05 + 1 * jax.random.normal(jax.random.fold_in(_gk, 1), (8, 32, 32, 128), jnp.float32)
        return x
    x = _rec_inputs()

    def _L0_conv_setup():
        import jax, jax.numpy as jnp
        import numpy as np
        K = 3
        FILTERS = 128
        GC = 16
        G = FILTERS // GC
        key = jax.random.key(seed)
        ks = jax.random.split(key, 5)
        B, H, W, C = (8, 32, 32, FILTERS)
        red = FILTERS // 4
        x = jax.random.normal(ks[0], (B, H, W, C), dtype=jnp.float32)
        W1 = jax.random.normal(ks[1], (C, red), dtype=jnp.float32) * 0.05
        b1 = jnp.zeros((red,), dtype=jnp.float32)
        W2 = jax.random.normal(ks[2], (red, K * K * G), dtype=jnp.float32) * 0.05
        b2 = jnp.zeros((K * K * G,), dtype=jnp.float32)
        return {'x': x, 'W1': W1, 'b1': b1, 'W2': W2, 'b2': b2}
    _L0_conv_all = _L0_conv_setup()
    _L0_conv_in = {k: v for k, v in _L0_conv_all.items() if k in ('W1', 'b1', 'W2', 'b2')}
    del _L0_conv_all

    def _L1_attn_setup():
        import jax, jax.numpy as jnp
        import numpy as np
        B, N, DIM = (8, 4096, 128)
        HEADS, LOCAL_HEADS, WINDOW = (8, 1, 32)
        HD = DIM // HEADS
        MLP_HIDDEN = 512
        EPS = 1e-05

        def layer_norm(x, g, b):
            mu = jnp.mean(x, axis=-1, keepdims=True)
            var = jnp.var(x, axis=-1, keepdims=True)
            return (x - mu) * jax.lax.rsqrt(var + EPS) * g + b

        def look_around(t, pad_value=0.0):
            nw = t.shape[1]
            pads = [(0, 0), (1, 1)] + [(0, 0)] * (t.ndim - 2)
            p = jnp.pad(t, pads, constant_values=pad_value)
            return jnp.concatenate([p[:, i:i + nw] for i in range(3)], axis=2)

        def local_attn(q, k, v):
            b, n, d = q.shape
            nw = n // WINDOW
            scale = d ** (-0.5)
            bq = q.reshape(b, nw, WINDOW, d) * scale
            bk = look_around(k.reshape(b, nw, WINDOW, d))
            bv = look_around(v.reshape(b, nw, WINDOW, d))
            ticker = jnp.arange(n).reshape(1, nw, WINDOW)
            bq_k = look_around(ticker, pad_value=-1)
            pad_mask = (bq_k == -1)[:, :, None, :]
            dots = jnp.einsum('bnie,bnje->bnij', bq, bk)
            dots = jnp.where(pad_mask, -1000000000.0, dots)
            attn = jax.nn.softmax(dots, axis=-1)
            out = jnp.einsum('bnij,bnje->bnie', attn, bv)
            return out.reshape(b, n, d)

        def linear_attn(q, k, v):
            d = q.shape[-1]
            qs = jax.nn.softmax(q, axis=-1) * d ** (-0.5)
            ks = jax.nn.softmax(k, axis=-2)
            ctx = jnp.einsum('bhnd,bhne->bhde', ks, v)
            return jnp.einsum('bhnd,bhde->bhne', qs, ctx)
        key = jax.random.key(seed)
        ks = jax.random.split(key, 8)
        s = 0.02
        return {'x': jax.random.normal(ks[0], (B, N, DIM), jnp.float32), 'norm1_g': jnp.ones((DIM,), jnp.float32), 'norm1_b': jnp.zeros((DIM,), jnp.float32), 'Wq': jax.random.normal(ks[1], (DIM, DIM), jnp.float32) * s, 'Wkv': jax.random.normal(ks[2], (DIM, DIM), jnp.float32) * s, 'Wproj': jax.random.normal(ks[3], (DIM, DIM), jnp.float32) * s, 'bproj': jnp.zeros((DIM,), jnp.float32), 'norm2_g': jnp.ones((DIM,), jnp.float32), 'norm2_b': jnp.zeros((DIM,), jnp.float32), 'W1': jax.random.normal(ks[4], (MLP_HIDDEN, DIM), jnp.float32) * s, 'b1': jnp.zeros((MLP_HIDDEN,), jnp.float32), 'W2': jax.random.normal(ks[5], (DIM, MLP_HIDDEN), jnp.float32) * s, 'b2': jnp.zeros((DIM,), jnp.float32)}
    _L1_attn_all = _L1_attn_setup()
    _L1_attn_in = {k: v for k, v in _L1_attn_all.items() if k in ('norm1_g', 'norm1_b', 'Wq', 'Wkv', 'Wproj', 'bproj', 'norm2_g', 'norm2_b', 'W1', 'b1', 'W2', 'b2')}
    del _L1_attn_all

    def _L1_ffn_setup():
        import jax, jax.numpy as jnp
        import numpy as np
        N_EXPERTS = 8
        TOP_K = 2
        key = jax.random.key(seed)
        ks = jax.random.split(key, 5)
        B, T, C, E, H = (8, 1024, 128, 8, 341)
        scale = 1.0 / np.sqrt(C)
        return {'x': jax.random.normal(ks[0], (B, T, C), dtype=jnp.float32), 'router_w': jax.random.normal(ks[1], (E, C), dtype=jnp.float32) * scale, 'w1': jax.random.normal(ks[2], (E, H, C), dtype=jnp.float32) * scale, 'w2': jax.random.normal(ks[3], (E, C, H), dtype=jnp.float32) * (1.0 / np.sqrt(H)), 'w3': jax.random.normal(ks[4], (E, H, C), dtype=jnp.float32) * scale}
    _L1_ffn_all = _L1_ffn_setup()
    _L1_ffn_in = {k: v for k, v in _L1_ffn_all.items() if k in ('router_w', 'w1', 'w2', 'w3')}
    del _L1_ffn_all
    return {'x': x, 'L0_conv_W1': _L0_conv_in['W1'], 'L0_conv_b1': _L0_conv_in['b1'], 'L0_conv_W2': _L0_conv_in['W2'], 'L0_conv_b2': _L0_conv_in['b2'], 'L1_attn_norm1_g': _L1_attn_in['norm1_g'], 'L1_attn_norm1_b': _L1_attn_in['norm1_b'], 'L1_attn_Wq': _L1_attn_in['Wq'], 'L1_attn_Wkv': _L1_attn_in['Wkv'], 'L1_attn_Wproj': _L1_attn_in['Wproj'], 'L1_attn_bproj': _L1_attn_in['bproj'], 'L1_attn_norm2_g': _L1_attn_in['norm2_g'], 'L1_attn_norm2_b': _L1_attn_in['norm2_b'], 'L1_attn_W1': _L1_attn_in['W1'], 'L1_attn_b1': _L1_attn_in['b1'], 'L1_attn_W2': _L1_attn_in['W2'], 'L1_attn_b2': _L1_attn_in['b2'], 'L1_ffn_router_w': _L1_ffn_in['router_w'], 'L1_ffn_w1': _L1_ffn_in['w1'], 'L1_ffn_w2': _L1_ffn_in['w2'], 'L1_ffn_w3': _L1_ffn_in['w3']}

def reference(x, L0_conv_W1, L0_conv_b1, L0_conv_W2, L0_conv_b2, L1_attn_norm1_g, L1_attn_norm1_b, L1_attn_Wq, L1_attn_Wkv, L1_attn_Wproj, L1_attn_bproj, L1_attn_norm2_g, L1_attn_norm2_b, L1_attn_W1, L1_attn_b1, L1_attn_W2, L1_attn_b2, L1_ffn_router_w, L1_ffn_w1, L1_ffn_w2, L1_ffn_w3):
    import jax
    import jax.numpy as jnp

    def _L0_conv_ref(x, W1, b1, W2, b2):
        import jax, jax.numpy as jnp
        import numpy as np
        K = 3
        FILTERS = 128
        GC = 16
        G = FILTERS // GC
        b, h, w, c = x.shape
        kk = K * K
        wgt = jnp.einsum('bhwc,cd->bhwd', x, W1) + b1
        wgt = jnp.einsum('bhwd,de->bhwe', wgt, W2) + b2
        wgt = wgt.transpose(0, 3, 1, 2).reshape(b, G, 1, kk, h, w)
        pad = (K - 1) // 2
        xp = jnp.pad(x, ((0, 0), (pad, K - 1 - pad), (pad, K - 1 - pad), (0, 0)))
        patches = jnp.stack([xp[:, i:i + h, j:j + w, :] for i in range(K) for j in range(K)], axis=3)
        out = patches.reshape(b, h, w, kk * c).transpose(0, 3, 1, 2).reshape(b, G, GC, kk, h, w)
        out = jnp.einsum('bgokhw,bgckhw->bgchw', wgt, out)
        out = out.reshape(b, FILTERS, h, w).transpose(0, 2, 3, 1)
        return out

    def _L1_attn_ref(x, norm1_g, norm1_b, Wq, Wkv, Wproj, bproj, norm2_g, norm2_b, W1, b1, W2, b2):
        import jax, jax.numpy as jnp
        import numpy as np
        B, N, DIM = (8, 4096, 128)
        HEADS, LOCAL_HEADS, WINDOW = (8, 1, 32)
        HD = DIM // HEADS
        MLP_HIDDEN = 512
        EPS = 1e-05

        def layer_norm(x, g, b):
            mu = jnp.mean(x, axis=-1, keepdims=True)
            var = jnp.var(x, axis=-1, keepdims=True)
            return (x - mu) * jax.lax.rsqrt(var + EPS) * g + b

        def look_around(t, pad_value=0.0):
            nw = t.shape[1]
            pads = [(0, 0), (1, 1)] + [(0, 0)] * (t.ndim - 2)
            p = jnp.pad(t, pads, constant_values=pad_value)
            return jnp.concatenate([p[:, i:i + nw] for i in range(3)], axis=2)

        def local_attn(q, k, v):
            b, n, d = q.shape
            nw = n // WINDOW
            scale = d ** (-0.5)
            bq = q.reshape(b, nw, WINDOW, d) * scale
            bk = look_around(k.reshape(b, nw, WINDOW, d))
            bv = look_around(v.reshape(b, nw, WINDOW, d))
            ticker = jnp.arange(n).reshape(1, nw, WINDOW)
            bq_k = look_around(ticker, pad_value=-1)
            pad_mask = (bq_k == -1)[:, :, None, :]
            dots = jnp.einsum('bnie,bnje->bnij', bq, bk)
            dots = jnp.where(pad_mask, -1000000000.0, dots)
            attn = jax.nn.softmax(dots, axis=-1)
            out = jnp.einsum('bnij,bnje->bnie', attn, bv)
            return out.reshape(b, n, d)

        def linear_attn(q, k, v):
            d = q.shape[-1]
            qs = jax.nn.softmax(q, axis=-1) * d ** (-0.5)
            ks = jax.nn.softmax(k, axis=-2)
            ctx = jnp.einsum('bhnd,bhne->bhde', ks, v)
            return jnp.einsum('bhnd,bhde->bhne', qs, ctx)
        b, n, c = x.shape
        h = layer_norm(x, norm1_g, norm1_b)
        q = h @ Wq.T
        kv = h @ Wkv.T
        split_heads = lambda t: t.reshape(b, n, HEADS, HD).transpose(0, 2, 1, 3)
        q, k, v = (split_heads(q), split_heads(kv), split_heads(kv))
        lq, gq = (q[:, :LOCAL_HEADS], q[:, LOCAL_HEADS:])
        lk, gk = (k[:, :LOCAL_HEADS], k[:, LOCAL_HEADS:])
        lv, gv = (v[:, :LOCAL_HEADS], v[:, LOCAL_HEADS:])
        lout = local_attn(lq.reshape(b * LOCAL_HEADS, n, HD), lk.reshape(b * LOCAL_HEADS, n, HD), lv.reshape(b * LOCAL_HEADS, n, HD)).reshape(b, LOCAL_HEADS, n, HD)
        gout = linear_attn(gq, gk, gv)
        attn = jnp.concatenate([lout, gout], axis=1)
        y = attn.transpose(0, 2, 1, 3).reshape(b, n, c) @ Wproj.T + bproj
        x = x + y
        h2 = layer_norm(x, norm2_g, norm2_b)
        m = jax.nn.gelu(h2 @ W1.T + b1, approximate=False) @ W2.T + b2
        return x + m

    def _L1_ffn_ref(x, router_w, w1, w2, w3):
        import jax, jax.numpy as jnp
        import numpy as np
        N_EXPERTS = 8
        TOP_K = 2
        B, T, C = x.shape
        flat = x.reshape(-1, C)
        logits = flat @ router_w.T
        probs = jax.nn.softmax(logits, axis=-1)
        topk_probs, topk_idx = jax.lax.top_k(probs, TOP_K)
        topk_probs = topk_probs / (jnp.sum(topk_probs, axis=-1, keepdims=True) + 1e-09)
        onehot = jax.nn.one_hot(topk_idx, N_EXPERTS, dtype=flat.dtype)
        gates = jnp.einsum('nk,nke->ne', topk_probs, onehot)
        h1 = jnp.einsum('nc,ehc->neh', flat, w1)
        h3 = jnp.einsum('nc,ehc->neh', flat, w3)
        h = jax.nn.silu(h1) * h3
        y = jnp.einsum('neh,ech->nec', h, w2)
        out = jnp.einsum('ne,nec->nc', gates, y)
        return out.reshape(B, T, C)

    def _gn(v, G=32, eps=1e-05):
        B_, H_, W_, C_ = v.shape
        g = v.reshape(B_, H_, W_, G, C_ // G)
        m = jnp.mean(g, axis=(1, 2, 4), keepdims=True)
        s = jnp.var(g, axis=(1, 2, 4), keepdims=True)
        return ((g - m) / jnp.sqrt(s + eps)).reshape(v.shape)

    def _ln_c(v, eps=1e-06):
        m = jnp.mean(v, axis=-1, keepdims=True)
        s = jnp.var(v, axis=-1, keepdims=True)
        return (v - m) / jnp.sqrt(s + eps)

    def _ln_t(v, eps=1e-05):
        m = jnp.mean(v, axis=-1, keepdims=True)
        s = jnp.var(v, axis=-1, keepdims=True)
        return (v - m) / jnp.sqrt(s + eps)

    def _to_tokens(v):
        B_, H_, W_, C_ = v.shape
        return v.reshape(B_, H_ * W_, C_)

    def _from_tokens(t, like):
        return t.reshape(like.shape)
    x = x + _L0_conv_ref(_gn(x), L0_conv_W1, L0_conv_b1, L0_conv_W2, L0_conv_b2)
    t = _to_tokens(x)
    t = t + _L1_attn_ref(_ln_t(t), L1_attn_norm1_g, L1_attn_norm1_b, L1_attn_Wq, L1_attn_Wkv, L1_attn_Wproj, L1_attn_bproj, L1_attn_norm2_g, L1_attn_norm2_b, L1_attn_W1, L1_attn_b1, L1_attn_W2, L1_attn_b2)
    t = t + _L1_ffn_ref(_ln_t(t), L1_ffn_router_w, L1_ffn_w1, L1_ffn_w2, L1_ffn_w3)
    x = _from_tokens(t, x)
    return x

_drawn_inputs = setup_inputs


def setup_inputs(seed=0):
    import zlib

    import numpy as np

    out = dict(_drawn_inputs(seed))
    spreads = {'L0_conv_b1': (0.0, 0.1),
     'L0_conv_b2': (0.0, 0.1),
     'L1_attn_norm1_g': (1.0, 0.6),
     'L1_attn_norm1_b': (0.0, 0.8),
     'L1_attn_bproj': (0.0, 0.1),
     'L1_attn_norm2_g': (1.0, 0.6),
     'L1_attn_norm2_b': (0.0, 2.0),
     'L1_attn_b1': (0.0, 0.341),
     'L1_attn_b2': (0.0, 0.1)}
    factors = {'L1_attn_Wq': 8.0, 'L1_attn_Wkv': 8.0, 'L1_attn_Wproj': 8.0}
    for name, (base, spread) in spreads.items():
        noise = np.random.default_rng([zlib.crc32(name.encode()), seed]).standard_normal(out[name].shape)
        drawn = base * np.exp(spread * noise) if base else spread * noise
        out[name] = jnp.asarray(drawn.astype(out[name].dtype))
    for name, factor in factors.items():
        out[name] = (out[name] * factor).astype(out[name].dtype)
    return out
```

```python
from contextlib import ExitStack

import numpy as np

import concourse.bass as bass
from concourse import mybir

F32 = mybir.dt.float32
F32R = mybir.dt.float32r
ALU = mybir.AluOpType
ACT = mybir.ActivationFunctionType
AX = mybir.AxisListType

P = 128
BATCH, SIDE = 8, 32
PIX = SIDE * SIDE
TOK = BATCH * PIX
TILES = TOK // P
BT = PIX // P
CHUNK = 512
CT = CHUNK // P
TAPS, GROUPS, GCH = 9, 8, 16
RED = P // 4
CONV_W = 16
HEADS, HD, WIN = 8, 16, 32
SPAN = P + 2 * WIN
MLP = 512
EXPERTS, HID = 8, 341
HT = [(k * P, min(P, HID - k * P)) for k in range((HID + P - 1) // P)]
PADI = SIDE + 2
NEG = -1.0e30

C_ID, C_GN, C_SEL, C_HEAD, C_MASK = 0, P, 2 * P, 2 * P + TAPS * CONV_W, 3 * P + TAPS * CONV_W
C_HI, C_LO = C_MASK + 3 * SPAN, C_MASK + 3 * SPAN + 1
C_IOTA = C_LO + 1
C_GATE = C_IOTA + EXPERTS
C_END = C_GATE + EXPERTS * P


def first_channel(tap):
    return tap * P // TAPS


def constants():
    c = np.zeros((P, C_END), np.float32)
    p = np.arange(P)
    c[p, C_ID + p] = 1.0
    c[:, C_GN:C_GN + P] = (p[:, None] // 4 == p[None, :] // 4) * 0.25
    for t in range(TAPS):
        c[p, C_SEL + t * CONV_W + (t * P + p) // TAPS - first_channel(t)] = 1.0
    head = p // HD
    c[:, C_HEAD:C_HEAD + P] = (head[:, None] == head[None, :]) & (head[:, None] > 0)
    key = np.arange(SPAN)[None, :] // WIN
    query = p[:, None] // WIN
    near = (key >= query) & (key <= query + 2)
    for n, inside in enumerate((key >= 1, key >= 0, key < SPAN // WIN - 1)):
        c[:, C_MASK + n * SPAN:C_MASK + (n + 1) * SPAN] = np.where(near & inside, 0.0, NEG)
    c[:, C_HI] = (p < 2 * RED) | (p == 3 * RED)
    c[:, C_LO] = ((p >= 2 * RED) & (p < 3 * RED)) | (p == 3 * RED + 1)
    c[:, C_IOTA:C_IOTA + EXPERTS] = np.arange(EXPERTS)[None, :]
    for e in range(EXPERTS):
        c[e, C_GATE + e * P:C_GATE + (e + 1) * P] = 1.0
    return c


class Signal:

    def __init__(self, sem, each):
        self.sem, self.each = sem, each

    def at(self, i, n):
        return i * self.each + n


def conv_attn_moe(nc, x, w_red, b_red, w_tap, b_tap, n1g, n1b, wq, wkv, wproj, bproj,
                  n2g, n2b, w_up, b_up, w_down, b_down, router, w1, w2, w3, consts, out,
                  last_phase=9, dbg=None):
    x_t = x.rearrange("b h w c -> (b h w) c").rearrange("(n p) c -> p n c", p=P)
    out_t = out.rearrange("b h w c -> (b h w) c").rearrange("(n p) c -> p n c", p=P)

    with ExitStack() as ctx:
        def sb(name, shape, dt=F32, scope=ctx):
            return scope.enter_context(nc.sbuf_tensor(name, shape, dt))

        def ps(name, shape, scope=ctx):
            return scope.enter_context(nc.psum_tensor(name, shape, F32))

        def sem(name, scope=ctx):
            return scope.enter_context(nc.semaphore(name))

        cst = sb("cst", [P, C_END])
        ident = cst[:, C_ID:C_ID + P]
        eps5 = sb("eps5", [P, 1])
        tok = sb("tok", [P, TILES, P])
        res = sb("res", [P, TILES, P])
        bst = sb("bst", [P, TILES, 6])
        sc_a = sb("sc_a", [P, TILES])
        sc_b = sb("sc_b", [P, TILES])
        sc_c = sb("sc_c", [P, TILES])
        sc_d = sb("sc_d", [P, TILES])
        col = sb("col", [P, 12])
        N1G, N1B, N2G, N2B, BRED, BUP = 0, 1, 2, 3, 4, 5
        bproj_row = sb("bproj_row", [P, P])
        bdown_row = sb("bdown_row", [P, P])
        w_redT = sb("w_redT", [P, 3 * RED])
        w_taps = sb("w_taps", [P, TAPS * P], F32R)
        wqkvT = sb("wqkvT", [P, 2 * P])
        wkeyT = sb("wkeyT", [P, P])
        wprojT = sb("wprojT", [P, P])
        upH = sb("upH", [P, MLP], F32R)
        upL = sb("upL", [P, MLP], F32R)
        downH = sb("downH", [P, CT, P], F32R)
        downL = sb("downL", [P, CT, P], F32R)
        routerT = sb("routerT", [P, EXPERTS])
        w1T = sb("w1T", [P, EXPERTS * HID])
        w3T = sb("w3T", [P, EXPERTS * HID])
        w2T = sb("w2T", [P, EXPERTS, len(HT), P])
        banks = [ps(f"bank{n}", [P, CHUNK]) for n in range(8)]

        with ExitStack() as ph:
            raw1 = sb("raw1", [P, EXPERTS, len(HT), P], scope=ph)
            raw3 = sb("raw3", [P, EXPERTS, len(HT), P], scope=ph)
            raw2 = sb("raw2", [P, EXPERTS, HID], scope=ph)
            rawq = sb("rawq", [P, 3, P], scope=ph)
            rawu = sb("rawu", [P, CT, P], scope=ph)
            rawd = sb("rawd", [P, MLP], scope=ph)
            rawr = sb("rawr", [EXPERTS, P], scope=ph)
            rawt = sb("rawt", [P, TAPS * GROUPS], scope=ph)
            hi_t = sb("hi_t", [P, TAPS * GROUPS], F32R, scope=ph)
            lo_t = sb("lo_t", [P, TAPS * GROUPS], F32, scope=ph)
            cleared = sem("cleared", ph)
            loaded = sem("loaded", ph)
            turned = sem("turned", ph)
            high = sem("high", ph)
            emptied = sem("emptied", ph)
            tap_step = sem("tap_step", ph)
            vec_done = sem("vec_done", ph)
            groups = []
            for raw, dst in ((raw1, w1T), (raw3, w3T)):
                for e in range(EXPERTS):
                    groups.append(([(raw[0:m, e, k, :], m, P, a) for k, (a, m) in enumerate(HT)],
                                   [((P, 0, HID), dst[:, e * HID:(e + 1) * HID], None)]))
            for e in range(EXPERTS):
                tail = HT[-1][1]
                groups.append(([(raw2[:, e, a:a + m], P, m, k * P) for k, (a, m) in enumerate(HT)],
                               [((P, 0, 2 * P), w2T[:, e, 0:2, :], None),
                                ((tail, 2 * P, 3 * P), w2T[0:tail, e, 2, :], None)]))
            groups.append(([(rawq[:, k, :], P, P, k * P) for k in range(3)],
                           [((P, 0, 2 * P), wqkvT[:, :], None), ((P, 2 * P, 3 * P), wprojT[:, :], None),
                            ((P, 0, HD), wkeyT[:, 0:HD], None), ((P, P + HD, 2 * P), wkeyT[:, HD:P], None)]))
            groups.append(([(rawu[:, k, :], P, P, k * P) for k in range(CT)],
                           [((P, 0, MLP), upH[:, :], upL[:, :])]))
            groups.append(([(rawd[:, k * P:(k + 1) * P], P, P, k * P) for k in range(CT)],
                           [((P, 0, MLP), downH[:, :, :], downL[:, :, :])]))
            groups.append(([(rawr[:, :], EXPERTS, P, 0)], [((P, 0, EXPERTS), routerT[:, :], None)]))

            with nc.Block() as block:
                @block.sync
                def _(sp):
                    sp.dma_start(cst[:, :], consts).then_inc(loaded, 16)
                    for e in range(EXPERTS):
                        for raw, w in ((raw1, w1), (raw3, w3)):
                            sp.dma_start(raw[:, e, 0:2, :], w[e, 0:2 * P, :].rearrange("(k p) c -> p k c", p=P)).then_inc(loaded, 16)
                            sp.dma_start(raw[0:HT[2][1], e, 2, :], w[e, 2 * P:HID, :]).then_inc(loaded, 16)
                    sp.dma_start(raw2[:, :, :], w2.rearrange("e c h -> c e h")).then_inc(loaded, 16)
                    for k, w in enumerate((wq, wkv, wproj)):
                        sp.dma_start(rawq[:, k, :], w).then_inc(loaded, 16)
                    sp.dma_start(rawu[:, :, :], w_up.rearrange("(k p) c -> p k c", p=P)).then_inc(loaded, 16)
                    sp.dma_start(rawd[:, :], w_down).then_inc(loaded, 16)
                    sp.dma_start(rawr[:, :], router).then_inc(loaded, 16)

                @block.scalar
                def _(act):
                    with nc.allow_non_contiguous_dma(reason="vectors with one value per partition"):
                        for n, v in ((N1G, n1g), (N1B, n1b), (N2G, n2g), (N2B, n2b)):
                            act.dma_start(col[:, n:n + 1], v.rearrange("(p a) -> p a", a=1)).then_inc(loaded, 16)
                        for k in range(3):
                            act.dma_start(col[k * RED:(k + 1) * RED, BRED:BRED + 1], b_red.rearrange("(p a) -> p a", a=1)).then_inc(loaded, 16)
                        act.dma_start(col[:, BUP:BUP + CT], b_up.rearrange("(k p) -> p k", p=P)).then_inc(loaded, 16)
                    act.dma_start(bproj_row[:, :], bproj.rearrange("(a c) -> a c", a=1).to_broadcast([P, P])).then_inc(loaded, 16)
                    act.dma_start(bdown_row[:, :], b_down.rearrange("(a c) -> a c", a=1).to_broadcast([P, P])).then_inc(loaded, 16)
                    for k in range(3):
                        act.dma_start(w_redT[:, k * RED:(k + 1) * RED], w_red).then_inc(loaded, 16)
                    act.wait_ge(cleared, 1)
                    for k in range(3):
                        act.dma_start(rawt[k * RED:(k + 1) * RED, :], w_tap).then_inc(loaded, 16)
                    for k in range(2):
                        act.dma_start(rawt[3 * RED + k:3 * RED + k + 1, :], b_tap.rearrange("(a e) -> a e", a=1)).then_inc(loaded, 16)
                    for g, (_, pieces) in enumerate(groups):
                        act.wait_ge(turned, g + 1)
                        for (rows, a, b), dst, low in pieces:
                            ins = nc.scalar.activation(dst, banks[g % 8][0:rows, a:b] if len(dst.shape) == 2 else
                                                       banks[g % 8][0:rows, a:b].rearrange("p (k c) -> p k c", c=P), ACT.Copy)
                        ins.then_inc(high, 1)

                n_loads = 1 + 4 * EXPERTS + 1 + 3 + 3 + 4 + 3 + 1 + 2 + 3 + 3 + 2

                @block.tensor
                def _(pe):
                    pe.wait_ge(loaded, 16 * n_loads)
                    for g, (turns, pieces) in enumerate(groups):
                        if g >= 8:
                            pe.wait_ge(emptied, g - 7)
                        for src, rows, cols, at in turns:
                            ins = pe.transpose(banks[g % 8][0:cols, at:at + rows], src, ident[0:rows, 0:rows])
                        ins.then_inc(turned, 1)

                @block.vector
                def _(dve):
                    dve.memset(rawt[:, :], 0.0).then_inc(cleared, 1)
                    dve.memset(eps5[:, :], 1e-5)
                    dve.wait_ge(loaded, 16 * n_loads)
                    dve.tensor_copy(hi_t[:, :], rawt[:, :]).then_inc(tap_step, 1)
                    dve.wait_ge(tap_step, 1)
                    dve.tensor_tensor(lo_t[:, :], rawt[:, :], hi_t[:, :].bitcast(F32), ALU.subtract).then_inc(tap_step, 1)
                    dve.wait_ge(tap_step, 2)
                    dve.tensor_scalar(lo_t[:, :], lo_t[:, :], cst[:, C_LO:C_LO + 1], None, ALU.mult).then_inc(tap_step, 1)
                    dve.wait_ge(tap_step, 3)
                    dve.scalar_tensor_tensor(rawt[:, :], hi_t[:, :].bitcast(F32), cst[:, C_HI:C_HI + 1], lo_t[:, :],
                                             ALU.mult, ALU.add).then_inc(tap_step, 1)
                    dve.wait_ge(tap_step, 4)
                    dve.tensor_copy(w_taps[:, :].rearrange("p (g c k) -> p g c k", g=GROUPS, k=TAPS),
                                    rawt[:, :].rearrange("p (g a k) -> p g a k", g=GROUPS, a=1)
                                    .to_broadcast([P, GROUPS, GCH, TAPS]))
                    for g, (_, pieces) in enumerate(groups):
                        dve.wait_ge(high, g + 1)
                        ins = None
                        for (rows, a, b), dst, low in pieces:
                            if low is not None:
                                src = banks[g % 8][0:rows, a:b]
                                if len(dst.shape) == 3:
                                    src = src.rearrange("p (k c) -> p k c", c=P)
                                ins = dve.tensor_tensor(low, src, dst.bitcast(F32), ALU.subtract)
                        if ins is None:
                            dve.sem_inc(emptied, 1)
                        else:
                            ins.then_inc(emptied, 1)
        if last_phase < 1:
            return

        with ExitStack() as ph:
            stage = [sb(f"stage{s}", [P, BT, P], scope=ph) for s in range(2)]
            norm = [sb(f"norm{s}", [P, PADI, PADI], scope=ph) for s in range(2)]
            redu = [sb(f"redu{s}", [P, CHUNK], F32R, scope=ph) for s in range(2)]
            prod = [sb(f"prod{s}", [P, CHUNK], scope=ph) for s in range(3)]
            bnst = sb("bnst", [P, 2, 6], scope=ph)
            cstat = sb("cstat", [P, 2], scope=ph)
            dev4 = sb("dev4", [P, 2, 2], scope=ph)
            gmean = sb("gmean", [P, 1], scope=ph)
            dev = sb("dev", [P, 2], scope=ph)
            gsd = sb("gsd", [P, 1], scope=ph)
            grstd = sb("grstd", [P, 1], scope=ph)
            gshift = sb("gshift", [P, 1], scope=ph)
            tbn = sb("tbn", [P, 2 * BT, 6], scope=ph)
            S = {name: Signal(sem(name, ph), each) for name, each in {
                "x_loaded": 32, "stage_free": 4, "x_turned": 2, "cmean": 4, "gavg": 4, "gvec": 18, "gsd_set": 2,
                "gsd_ready": 2, "normed": 4, "norm_free": 2, "reduced": 4, "redu_ready": 4, "redu_step": 4,
                "taps": 4 * TAPS, "products": 4 * TAPS, "prod_used": 4 * TAPS, "summed": 4,
                "t0": 4, "tstat": 2, "halo": 0}.items()}
            NB = 2

            def w(eng, name, i, n):
                eng.wait_ge(S[name].sem, S[name].at(i, n))

            xcm = banks[0:2]
            tapb = banks[2:5]
            misc = banks[5]
            outb = banks[6:8]
            with nc.Block() as block:
                @block.sync
                def _(sp):
                    for b in range(BATCH):
                        sp.wait_ge(S["stage_free"].sem, 2 * b + 2)
                        sp.dma_start(stage[b % NB][:, :, :], x_t[:, b * BT:(b + 1) * BT, :]).then_inc(S["x_loaded"].sem, 16)
                        sp.wait_ge(S["x_loaded"].sem, 16 * (b + 1))

                @block.tensor
                def _(pe):
                    with pe.Fori(0, BATCH // NB) as i:
                        for s in range(NB):
                            w(pe, "x_loaded", i, 16 * (s + 1))
                            w(pe, "normed", i, 2 * s) if s else pe.wait_ge(S["normed"].sem, S["normed"].at(i, 0))
                            for n in range(2):
                                for j in range(CT):
                                    ins = pe.transpose(xcm[n][:, j * P:(j + 1) * P], stage[s][:, n * CT + j, :], ident)
                                ins.then_inc(S["x_turned"].sem, 0) if False else None
                            ins.then_inc(S["x_turned"].sem, 1)
                            w(pe, "cmean", i, 2 * s + 1)
                            pe.matmul(misc[:, 0:1], cst[:, C_GN:C_GN + P], cstat[:, 0:1], start=True, stop=True).then_inc(S["gavg"].sem, 1)
                            w(pe, "cmean", i, 2 * s + 2)
                            pe.matmul(misc[:, 0:1], cst[:, C_GN:C_GN + P], dev[:, 1:2], start=True, stop=True).then_inc(S["gavg"].sem, 1)
                            for n in range(2):
                                w(pe, "normed", i, 2 * s + 2)
                                w(pe, "redu_ready", i, 2 * s + n)
                                pe.matmul(misc[0:3 * RED, :], w_redT[:, :],
                                          norm[s][:, 1 + 16 * n:17 + 16 * n, 1:1 + SIDE], start=True, stop=True).then_inc(S["reduced"].sem, 1)
                                w(pe, "redu_ready", i, 2 * s + n + 1)
                                q = 2 * s + n
                                w(pe, "t0", i, q)

                                def sums(t):
                                    w(pe, "products", i, q * TAPS + t + 1)
                                    c0 = first_channel(t)
                                    width = min(CONV_W, P - c0)
                                    for j in range(CT):
                                        ins = pe.matmul(outb[n][:, j * P + c0:j * P + c0 + width],
                                                        prod[(q * TAPS + t) % 3][:, j * P:(j + 1) * P],
                                                        cst[:, C_SEL + t * CONV_W:C_SEL + t * CONV_W + width],
                                                        start=(t == 0 and j == 0), stop=(t == TAPS - 1), skip_group_check=True)
                                    ins.then_inc(S["prod_used"].sem, 1)
                                    return ins
                                for t in range(TAPS):
                                    if q * TAPS + t >= 3:
                                        w(pe, "products", i, q * TAPS + t - 2)
                                    pe.matmul(tapb[(q * TAPS + t) % 3][:, :], w_taps[:, t * P:(t + 1) * P], redu[n][:, :],
                                              start=True, stop=True).then_inc(S["taps"].sem, 1)
                                    if t >= 2:
                                        sums(t - 2)
                                sums(TAPS - 2)
                                sums(TAPS - 1)
                                pe.wait_ge(S["prod_used"].sem, S["prod_used"].at(i, (q + 1) * TAPS))
                                pe.sem_inc(S["summed"].sem, 1)

                @block.scalar
                def _(act):
                    with act.Fori(0, BATCH // NB) as i:
                        for s in range(NB):
                            w(act, "gsd_set", i, s + 1)
                            nc.scalar.activation(gsd[:, :], dev[:, 0:1], ACT.Sqrt, bias=eps5[:, 0:1]).then_inc(S["gsd_ready"].sem, 1)
                            w(act, "gvec", i, 9 * s + 9)
                            if s == 0:
                                act.wait_ge(S["summed"].sem, S["summed"].at(i, 0))
                            for n in range(2):
                                nc.scalar.activation(norm[s][:, 1 + 16 * n:17 + 16 * n, 1:1 + SIDE],
                                                     xcm[n][:, :].rearrange("p (h w) -> p h w", w=SIDE), ACT.Identity,
                                                     bias=gshift[:, 0:1], scale=grstd[:, 0:1]).then_inc(S["normed"].sem, 1)
                            w(act, "t0", i, 2 * s + 2)
                            act.activation(tok[:, bass.ds((i * NB + s) * BT, BT), :], stage[s][:, :, :], ACT.Copy
                                           ).then_inc(S["stage_free"].sem, 1)

                @block.vector
                def _(dve):
                    for s in range(2):
                        dve.memset(norm[s][:, :, :], 0.0)
                        dve.memset(redu[s][96:128, :].bitcast(F32), 1.0)
                    dve.drain()
                    dve.sem_inc(S["stage_free"].sem, 4)
                    with dve.Fori(0, BATCH // NB) as i:
                        for s in range(NB):
                            gv = 9 * s

                            def g_step(ins, n):
                                ins.then_inc(S["gvec"].sem, 1)
                                w(dve, "gvec", i, gv + n)
                            w(dve, "x_turned", i, s + 1) if False else dve.wait_ge(S["x_turned"].sem, i * 2 + s + 1)
                            for n in range(2):
                                ins = dve.bn_stats(bnst[:, n, :], xcm[n][:, :])
                            g_step(ins, 1)
                            dve.tensor_reduce(cstat[:, 0:1], bnst[:, :, 1::3], AX.XY, ALU.add).then_inc(S["cmean"].sem, 1)
                            w(dve, "gavg", i, 2 * s + 1)
                            g_step(dve.tensor_scalar(gmean[:, :], misc[:, 0:1], 0.25, None, ALU.mult), 2)
                            g_step(dve.tensor_scalar(dev4[:, :, :], bnst[:, :, 1::3], gmean[:, 0:1], None, ALU.subtract), 3)
                            g_step(dve.tensor_tensor(dev4[:, :, :], dev4[:, :, :], dev4[:, :, :], ALU.mult), 4)
                            g_step(dve.scalar_tensor_tensor(dev4[:, :, :], bnst[:, :, 2::3], 4.0 / PIX, dev4[:, :, :], ALU.mult, ALU.add), 5)
                            dve.tensor_reduce(dev[:, 1:2], dev4[:, :, :], AX.XY, ALU.add).then_inc(S["cmean"].sem, 1)
                            w(dve, "gavg", i, 2 * s + 2)
                            g_step(dve.tensor_scalar(dev[:, 0:1], misc[:, 0:1], 0.25, None, ALU.mult), 6)
                            dve.sem_inc(S["gsd_set"].sem, 1)
                            w(dve, "gsd_ready", i, s + 1)
                            g_step(dve.reciprocal(grstd[:, :], gsd[:, :]), 7)
                            g_step(dve.scalar_tensor_tensor(gshift[:, :], gmean[:, :], -1.0, grstd[:, :], ALU.mult, ALU.mult), 8)
                            dve.sem_inc(S["gvec"].sem, 1)
                            for n in range(2):
                                q = 2 * s + n
                                w(dve, "reduced", i, q + 1)
                                dve.tensor_scalar(redu[n][0:3 * RED, :], misc[0:3 * RED, :], col[0:3 * RED, BRED:BRED + 1],
                                                  None, ALU.add).then_inc(S["redu_step"].sem, 1)
                                w(dve, "redu_step", i, q + 1)
                                dve.scalar_tensor_tensor(redu[n][RED:2 * RED, :], misc[RED:2 * RED, :], col[RED:2 * RED, BRED:BRED + 1],
                                                         redu[n][RED:2 * RED, :].bitcast(F32), ALU.add,
                                                         ALU.subtract).then_inc(S["redu_ready"].sem, 1)
                                for t in range(TAPS):
                                    dy, dx = t // 3, t % 3
                                    g = q * TAPS + t
                                    w(dve, "taps", i, g + 1)
                                    if g >= 3:
                                        w(dve, "prod_used", i, g - 2)
                                    dve.tensor_tensor(prod[g % 3][:, :].rearrange("p (h w) -> p h w", w=SIDE),
                                                      tapb[g % 3][:, :].rearrange("p (h w) -> p h w", w=SIDE),
                                                      norm[s][:, 16 * n + dy:16 * n + dy + 16, dx:dx + SIDE],
                                                      ALU.mult).then_inc(S["products"].sem, 1)
                                w(dve, "summed", i, q + 1)
                                t0 = stage[s][:, n * CT:(n + 1) * CT, :]
                                dve.tensor_tensor(t0, outb[n][:, :].rearrange("p (j c) -> p j c", c=P), t0,
                                                  ALU.add).then_inc(S["t0"].sem, 1)
                                w(dve, "t0", i, q + 1)
                                for j in range(CT):
                                    ins = dve.bn_stats(tbn[:, s * BT + n * CT + j, :], stage[s][:, n * CT + j, :])
                            ins.then_inc(S["tstat"].sem, 1)
                            w(dve, "tstat", i, s + 1)
                            dve.tensor_copy(bst[:, bass.ds((i * NB + s) * BT, BT), :], tbn[:, s * BT:(s + 1) * BT, :]
                                            ).then_inc(S["stage_free"].sem, 1)
                    dve.drain()
        if dbg is not None and last_phase == 1:
            with nc.Block() as block, nc.semaphore("dbgs") as ds:
                @block.sync
                def _(sp):
                    sp.dma_start(out_t, tok[:, :, :]).then_inc(ds, 16)
                    sp.wait_ge(ds, 16)
            return

        def norm_scales(first, n=[0]):
            n[0] += 1
            tag = f"_{n[0]}"
            with ExitStack() as ph:
                sd = sb("sd" + tag, [P, TILES], scope=ph)
                v2 = sb("v2" + tag, [P, TILES], scope=ph)
                step, rooted = sem("step" + tag, ph), sem("rooted" + tag, ph)
                mean = sb("mean" + tag, [P, TILES], scope=ph)
                var = sb("var" + tag, [P, TILES], scope=ph)
                half = sb("half" + tag, [P, TILES], scope=ph)
                folded = sem("folded" + tag, ph)
                with nc.Block() as block:
                    @block.scalar
                    def _(act):
                        act.wait_ge(folded, 7)
                        nc.scalar.activation(sd[:, :], var[:, :], ACT.Sqrt, bias=eps5[:, 0:1]).then_inc(rooted, 1)
                        if first:
                            act.wait_ge(step, 4)
                            nc.scalar.activation(sd[:, :], v2[:, :], ACT.Sqrt, bias=eps5[:, 0:1]).then_inc(rooted, 1)

                    @block.vector
                    def _(dve):
                        me, mo = bst[:, :, 1], bst[:, :, 4]
                        fold = [
                            lambda: dve.tensor_tensor(mean[:, :], me, mo, ALU.add),
                            lambda: dve.tensor_tensor(half[:, :], me, mo, ALU.subtract),
                            lambda: dve.tensor_tensor(var[:, :], bst[:, :, 2], bst[:, :, 5], ALU.add),
                            lambda: dve.tensor_scalar(mean[:, :], mean[:, :], 0.5, None, ALU.mult),
                            lambda: dve.scalar_tensor_tensor(half[:, :], half[:, :], 0.25, half[:, :], ALU.mult, ALU.mult),
                            lambda: dve.tensor_scalar(var[:, :], var[:, :], 1.0 / P, None, ALU.mult),
                            lambda: dve.tensor_tensor(var[:, :], var[:, :], half[:, :], ALU.add),
                        ]
                        for n, part in enumerate(fold):
                            part().then_inc(folded, 1)
                            dve.wait_ge(folded, n + 1)
                        dve.wait_ge(rooted, 1)
                        dve.reciprocal(sc_a[:, :], sd[:, :]).then_inc(step, 1)
                        dve.wait_ge(step, 1)
                        dve.scalar_tensor_tensor(sc_b[:, :], mean[:, :], -1.0, sc_a[:, :], ALU.mult, ALU.mult).then_inc(step, 1)
                        if first:
                            dve.tensor_tensor(v2[:, :], var[:, :], sc_a[:, :], ALU.mult).then_inc(step, 1)
                            dve.wait_ge(step, 3)
                            dve.tensor_tensor(v2[:, :], v2[:, :], sc_a[:, :], ALU.mult).then_inc(step, 1)
                            dve.wait_ge(rooted, 2)
                            dve.reciprocal(sc_c[:, :], sd[:, :]).then_inc(step, 1)
                            dve.wait_ge(step, 5)
                            dve.tensor_tensor(sc_c[:, :], sc_c[:, :], sc_a[:, :], ALU.mult).then_inc(step, 1)
                            dve.wait_ge(step, 6)
                            dve.scalar_tensor_tensor(sc_d[:, :], mean[:, :], -1.0, sc_c[:, :], ALU.mult, ALU.mult).then_inc(step, 1)

        norm_scales(True)

        with ExitStack() as ph:
            ht = [sb(f"ht{s}", [P, BT, P], scope=ph) for s in range(2)]
            hcm = [sb(f"hcm{s}", [P, PIX + 2 * WIN], scope=ph) for s in range(2)]
            u = [sb(f"u{s}", [P, BT, P], scope=ph) for s in range(2)]
            kvt = sb("kvt", [P, BT, P], scope=ph)
            qs = sb("qs", [P, BT, P], scope=ph)
            qcm = sb("qcm", [P, PIX], scope=ph)
            ek = sb("ek", [P, PIX], scope=ph)
            ekt = sb("ekt", [P, BT, P], scope=ph)
            q0 = sb("q0", [HD, PIX], scope=ph)
            k0 = sb("k0", [HD, PIX + 2 * WIN], scope=ph)
            va = sb("va", [P, BT, HD], scope=ph)
            vb = sb("vb", [SPAN - P, BT, HD], scope=ph)
            sm = [sb(f"sm{m}", [P, 2, SPAN], scope=ph) for m in range(2)]
            pta = sb("pta", [P, BT, P], scope=ph)
            ptb = sb("ptb", [SPAN - P, BT, P], scope=ph)
            ctxs = sb("ctxs", [P, P], scope=ph)
            acm = sb("acm", [P, PIX], scope=ph)
            qmax = sb("qmax", [P, 2 * HEADS], scope=ph)
            qsum = sb("qsum", [P, BT * HEADS], scope=ph)
            kmax = sb("kmax", [P, 2], scope=ph)
            nkmax = sb("nkmax", [P, 1], scope=ph)
            ksum = sb("ksum", [P, 2], scope=ph)
            kinv = sb("kinv", [P, 1], scope=ph)
            nmax = sb("nmax", [P, BT], scope=ph)
            lsum = sb("lsum", [P, BT], scope=ph)
            linv = sb("linv", [P, BT], scope=ph)
            tbn = sb("rbn", [P, BT, 6], scope=ph)
            NB, JOBS = 2, 28
            J_HT, J_QKV, J_KEY, J_K0, J_V, J_S, J_EKT, J_QST, J_CTX, J_PT, J_OUT, J_Y = 0, 2, 6, 8, 10, 11, 15, 17, 19, 20, 24, 26
            BY_ACT = [0, 1, 6, 7, 8, 9, 10, 15, 16, 17, 18, 20, 21, 22, 23, 24, 25]
            BY_DVE = [2, 3, 4, 5, 11, 12, 13, 14, 19, 26, 27]
            V_STEPS = 200
            S = {name: Signal(sem(name, ph), each) for name, each in {
                "done": NB * JOBS, "act_read": NB * len(BY_ACT), "dve_read": NB * len(BY_DVE),
                "ht_ready": 2 * NB, "hcm_ready": 2 * NB, "kv_ready": 4 * NB, "kmax_ready": NB, "ek_ready": NB,
                "u_raw": NB, "u_ready": NB, "u_free": NB, "q_shift": 4 * NB, "q_exp": 4 * NB, "qs_ready": 4 * NB,
                "s_shift": 4 * NB, "s_exp": 4 * NB, "s_ready": 4 * NB, "ctx_ready": NB,
                "vec": NB * 23}.items()}

            def w(eng, name, i, n):
                eng.wait_ge(S[name].sem, S[name].at(i, n))

            def bank(s, k):
                return banks[(s * JOBS + k) % 8]

            def read_out(eng, i, s, k):
                g = s * JOBS + k - 8
                i_, g = (i, g + NB * JOBS) if g < 0 else (i + 1, g)
                s_, k_ = divmod(g, JOBS)
                name, order = ("act_read", BY_ACT) if k_ in BY_ACT else ("dve_read", BY_DVE)
                w(eng, name, i_, s_ * len(order) + order.index(k_) + 1)

            with nc.Block() as block:
                @block.tensor
                def _(pe):
                    with pe.Fori(0, BATCH // NB) as i:
                        for s in range(NB):
                            def job_done(ins):
                                ins.then_inc(S["done"].sem, 1)

                            for n in range(2):
                                read_out(pe, i, s, J_HT + n)
                                w(pe, "ht_ready", i, 2 * s + n + 1)
                                for j in range(CT):
                                    ins = pe.transpose(bank(s, J_HT + n)[:, j * P:(j + 1) * P], ht[s][:, n * CT + j, :], ident)
                                job_done(ins)
                            for m in range(4):
                                w(pe, "hcm_ready", i, 2 * s + m // 2 + 1)
                                read_out(pe, i, s, J_QKV + m)
                                for h in range(2):
                                    a = WIN + (2 * m + h) * P
                                    ins = pe.matmul(bank(s, J_QKV + m)[:, h * 2 * P:(h + 1) * 2 * P], hcm[s][:, a:a + P], wqkvT[:, :],
                                                    start=True, stop=True)
                                job_done(ins)
                            for n in range(2):
                                read_out(pe, i, s, J_KEY + n)
                                a = WIN + n * CHUNK
                                job_done(pe.matmul(bank(s, J_KEY + n)[:, :], wkeyT[:, :], hcm[s][:, a:a + CHUNK], start=True, stop=True))
                            for n in range(2):
                                read_out(pe, i, s, J_K0 + n)
                                a = WIN + n * CHUNK
                                job_done(pe.matmul(bank(s, J_K0 + n)[0:HD, :], wqkvT[:, P:P + HD], hcm[s][:, a:a + CHUNK], start=True, stop=True))
                            read_out(pe, i, s, J_V)
                            for j in range(BT):
                                pe.matmul(bank(s, J_V)[:, j * 2 * HD:j * 2 * HD + HD], hcm[s][:, j * P:(j + 1) * P],
                                          wqkvT[:, P:P + HD], start=True, stop=True)
                                ins = pe.matmul(bank(s, J_V)[0:SPAN - P, j * 2 * HD + HD:(j + 1) * 2 * HD],
                                                hcm[s][:, (j + 1) * P:j * P + SPAN], wqkvT[:, P:P + HD], start=True, stop=True)
                            job_done(ins)
                            w(pe, "act_read", i + 1, s * len(BY_ACT) + BY_ACT.index(J_K0 + 1) + 1)
                            for m in range(4):
                                read_out(pe, i, s, J_S + m)
                                for h in range(2):
                                    j = 2 * m + h
                                    ins = pe.matmul(bank(s, J_S + m)[:, h * SPAN:(h + 1) * SPAN], q0[:, j * P:(j + 1) * P],
                                                    k0[:, j * P:j * P + SPAN], start=True, stop=True)
                                job_done(ins)
                            for n in range(2):
                                w(pe, "ek_ready", i, s + 1)
                                read_out(pe, i, s, J_EKT + n)
                                for j in range(CT):
                                    a = (n * CT + j) * P
                                    ins = pe.transpose(bank(s, J_EKT + n)[:, j * P:(j + 1) * P], ek[:, a:a + P], ident)
                                job_done(ins)
                            for n in range(2):
                                w(pe, "qs_ready", i, 4 * s + 2 * n + 2)
                                read_out(pe, i, s, J_QST + n)
                                for j in range(CT):
                                    ins = pe.transpose(bank(s, J_QST + n)[:, j * P:(j + 1) * P], qs[:, n * CT + j, :], ident)
                                job_done(ins)
                            w(pe, "act_read", i + 1, s * len(BY_ACT) + BY_ACT.index(J_EKT + 1) + 1)
                            w(pe, "kv_ready", i, 4 * s + 4)
                            read_out(pe, i, s, J_CTX)
                            for j in range(BT):
                                ins = pe.matmul(bank(s, J_CTX)[:, 0:P], ekt[:, j, :], kvt[:, j, :], start=(j == 0), stop=(j == BT - 1))
                            job_done(ins)
                            for m in range(4):
                                w(pe, "s_ready", i, 4 * s + m + 1)
                                read_out(pe, i, s, J_PT + m)
                                for h in range(2):
                                    a = 2 * h * P
                                    pe.transpose(bank(s, J_PT + m)[:, a:a + P], sm[m % 2][:, h, 0:P], ident)
                                    ins = pe.transpose(bank(s, J_PT + m)[0:SPAN - P, a + P:a + 2 * P], sm[m % 2][:, h, P:SPAN], ident)
                                job_done(ins)
                            for n in range(2):
                                w(pe, "ctx_ready", i, s + 1)
                                w(pe, "act_read", i + 1, s * len(BY_ACT) + BY_ACT.index(J_PT + 2 * n + 1) + 1)
                                read_out(pe, i, s, J_OUT + n)
                                pe.matmul(bank(s, J_OUT + n)[:, :], ctxs[:, :], qcm[:, n * CHUNK:(n + 1) * CHUNK],
                                          start=True, stop=False, skip_group_check=True)
                                for t in range(CT):
                                    j = n * CT + t
                                    o = bank(s, J_OUT + n)[0:HD, t * P:(t + 1) * P]
                                    pe.matmul(o, va[:, j, :], pta[:, j, :], start=False, stop=False, skip_group_check=True)
                                    ins = pe.matmul(o, vb[:, j, :], ptb[:, j, :], start=False, stop=True, skip_group_check=True)
                                job_done(ins)
                            for n in range(2):
                                w(pe, "act_read", i + 1, s * len(BY_ACT) + BY_ACT.index(J_OUT + n) + 1)
                                read_out(pe, i, s, J_Y + n)
                                for t in range(CT):
                                    j = n * CT + t
                                    ins = pe.matmul(bank(s, J_Y + n)[:, t * P:(t + 1) * P], acm[:, j * P:(j + 1) * P], wprojT[:, :],
                                                    start=True, stop=True)
                                job_done(ins)

                def pt_out(act, i, s, m, job, read):
                    job(J_PT + m)
                    pv = bank(s, J_PT + m)[:, :].rearrange("p (h k c) -> p h k c", h=2, k=2)
                    act.activation(pta[:, 2 * m:2 * m + 2, :], pv[:, :, 0, :], ACT.Copy)
                    read(act.activation(ptb[:, 2 * m:2 * m + 2, :], pv[0:SPAN - P, :, 1, :], ACT.Copy))

                @block.scalar
                def _(act):
                    act.sem_inc(S["act_read"].sem, S["act_read"].each)
                    with act.Fori(0, BATCH // NB) as i:
                        for s in range(NB):
                            def job(k):
                                w(act, "done", i, s * JOBS + k + 1)

                            def read(ins):
                                ins.then_inc(S["act_read"].sem, 1)

                            for j in range(BT):
                                t = (i * NB + s) * BT + j
                                ins = act.activation(u[s][:, j, :], tok[:, bass.ds(t, 1), :].rearrange("p a c -> p (a c)"),
                                                     ACT.Identity, bias=sc_b[:, bass.ds(t, 1)], scale=sc_a[:, bass.ds(t, 1)])
                            ins.then_inc(S["u_raw"].sem, 1)
                            for n in range(2):
                                job(J_HT + n)
                                ins = act.activation(hcm[s][:, WIN + n * CHUNK:WIN + (n + 1) * CHUNK], bank(s, J_HT + n)[:, :], ACT.Identity,
                                                     bias=col[:, N1B:N1B + 1], scale=col[:, N1G:N1G + 1])
                                read(ins)
                                act.wait_ge(S["act_read"].sem, S["act_read"].at(i + 1, s * len(BY_ACT) + n + 1))
                                act.sem_inc(S["hcm_ready"].sem, 1)
                            for m in range(4):
                                job(J_QKV + m)
                                if m == 0:
                                    w(act, "done", i, s * JOBS)
                                act.activation(kvt[:, 2 * m:2 * m + 2, :],
                                               bank(s, J_QKV + m)[:, :].rearrange("p (h c) -> p h c", h=2)[:, :, P:2 * P],
                                               ACT.Copy).then_inc(S["kv_ready"].sem, 1)
                            w(act, "kmax_ready", i, s + 1)
                            for n in range(2):
                                job(J_KEY + n)
                                act.activation(q0[:, n * CHUNK:(n + 1) * CHUNK], bank(s, J_KEY + n)[0:HD, :], ACT.Copy)
                                read(act.activation(ek[:, n * CHUNK:(n + 1) * CHUNK], bank(s, J_KEY + n)[:, :], ACT.Exp,
                                                    bias=nkmax[:, 0:1], accum_out=ksum[:, n:n + 1]))
                            act.wait_ge(S["act_read"].sem, S["act_read"].at(i + 1, s * len(BY_ACT) + BY_ACT.index(J_KEY + 1) + 1))
                            act.sem_inc(S["ek_ready"].sem, 1)
                            for n in range(2):
                                job(J_K0 + n)
                                read(act.activation(k0[:, WIN + n * CHUNK:WIN + (n + 1) * CHUNK], bank(s, J_K0 + n)[0:HD, :], ACT.Copy))
                            job(J_V)
                            vv = bank(s, J_V)[:, 0:BT * 2 * HD].rearrange("p (j k e) -> p j k e", j=BT, k=2)
                            act.activation(va[:, :, :], vv[:, :, 0, :], ACT.Copy)
                            read(act.activation(vb[:, :, :], vv[0:SPAN - P, :, 1, :], ACT.Copy))
                            for m in range(4):
                                w(act, "q_shift", i, 4 * s + m + 1)
                                act.activation(qs[:, 2 * m:2 * m + 2, :], qs[:, 2 * m:2 * m + 2, :], ACT.Exp).then_inc(S["q_exp"].sem, 1)
                            for n in range(2):
                                job(J_EKT + n)
                                read(act.activation(ekt[:, n * CT:(n + 1) * CT, :], bank(s, J_EKT + n)[:, :].rearrange("p (j c) -> p j c", c=P), ACT.Copy))
                            for n in range(2):
                                job(J_QST + n)
                                read(act.activation(qcm[:, n * CHUNK:(n + 1) * CHUNK], bank(s, J_QST + n)[:, :], ACT.Copy))
                            for m in range(4):
                                w(act, "s_shift", i, 4 * s + m + 1)
                                for h in range(2):
                                    j = 2 * m + h
                                    ins = act.activation(sm[m % 2][:, h, :], sm[m % 2][:, h, :], ACT.Exp, bias=nmax[:, j:j + 1],
                                                         accum_out=lsum[:, j:j + 1])
                                ins.then_inc(S["s_exp"].sem, 1)
                                if m >= 1:
                                    pt_out(act, i, s, m - 1, job, read)
                            pt_out(act, i, s, 3, job, read)
                            for n in range(2):
                                job(J_OUT + n)
                                read(act.activation(acm[:, n * CHUNK:(n + 1) * CHUNK], bank(s, J_OUT + n)[:, :], ACT.Copy))
                            act.wait_ge(S["dve_read"].sem, S["dve_read"].at(i + 1, (s + 1) * len(BY_DVE)))
                            act.activation(res[:, bass.ds((i * NB + s) * BT, BT), :], u[s][:, :, :], ACT.Copy).then_inc(S["u_free"].sem, 1)
                            w(act, "u_free", i, s + 1)

                @block.gpsimd
                def _(pool):
                    with pool.Fori(0, BATCH // NB) as i:
                        for s in range(NB):
                            w(pool, "u_raw", i, s + 1)
                            pool.tensor_tensor(u[s][:, :, :], u[s][:, :, :],
                                               bproj_row[:, :].rearrange("p (a c) -> p a c", a=1).to_broadcast([P, BT, P]),
                                               ALU.add).then_inc(S["u_ready"].sem, 1)

                @block.vector
                def _(dve):
                    for s in range(2):
                        dve.memset(hcm[s][:, :], 0.0)
                    dve.memset(k0[:, :], 0.0)
                    dve.drain()
                    dve.sem_inc(S["dve_read"].sem, S["dve_read"].each)
                    with dve.Fori(0, BATCH // NB) as i:
                        count = [0]

                        def step(ins):
                            ins.then_inc(S["vec"].sem, 1)
                            count[0] += 1
                            w(dve, "vec", i, count[0])

                        for s in range(NB):
                            def job(k):
                                w(dve, "done", i, s * JOBS + k + 1)

                            def read(ins):
                                ins.then_inc(S["dve_read"].sem, 1)

                            for j in range(BT):
                                t = (i * NB + s) * BT + j
                                ins = dve.tensor_scalar(ht[s][:, j, :], tok[:, bass.ds(t, 1), :].rearrange("p a c -> p (a c)"),
                                                        sc_c[:, bass.ds(t, 1)], sc_d[:, bass.ds(t, 1)], ALU.mult, ALU.add)
                                if j % CT == CT - 1:
                                    ins.then_inc(S["ht_ready"].sem, 1)
                            for m in range(4):
                                w(dve, "kv_ready", i, 4 * s + m + 1)
                                q4 = bank(s, J_QKV + m)[:, :].rearrange("p (h c) -> p h c", h=2)[:, :, 0:P].rearrange("p h (g d) -> p h g d", d=HD)
                                step(dve.tensor_reduce(qmax[:, :].rearrange("p (h g) -> p h g", h=2), q4, AX.X, ALU.max))
                                ins = dve.tensor_tensor(qs[:, 2 * m:2 * m + 2, :].rearrange("p h (g d) -> p h g d", d=HD), q4,
                                                        qmax[:, :].rearrange("p (h g a) -> p h g a", h=2, a=1).to_broadcast([P, 2, HEADS, HD]),
                                                        ALU.subtract)
                                read(ins)
                                dve.wait_ge(S["dve_read"].sem, S["dve_read"].at(i + 1, s * len(BY_DVE) + m + 1))
                                dve.sem_inc(S["q_shift"].sem, 1)
                            for n in range(2):
                                job(J_KEY + n)
                                ins = dve.tensor_reduce(kmax[:, n:n + 1], bank(s, J_KEY + n)[:, :], AX.X, ALU.max)
                            step(ins)
                            dve.tensor_reduce(nkmax[:, :], kmax[:, :], AX.X, ALU.max, negate=True).then_inc(S["kmax_ready"].sem, 1)

                            def scores_in(m):
                                job(J_S + m)
                                for h in range(2):
                                    j = 2 * m + h
                                    kind = 0 if j == 0 else 2 if j == BT - 1 else 1
                                    ins = dve.scalar_tensor_tensor(sm[m % 2][:, h, :], bank(s, J_S + m)[:, h * SPAN:(h + 1) * SPAN], HD ** -0.5,
                                                                   cst[:, C_MASK + kind * SPAN:C_MASK + (kind + 1) * SPAN], ALU.mult, ALU.add)
                                read(ins)
                                dve.wait_ge(S["dve_read"].sem, S["dve_read"].at(i + 1, s * len(BY_DVE) + 4 + m + 1))
                                dve.tensor_reduce(nmax[:, 2 * m:2 * m + 2], sm[m % 2][:, :, :], AX.X, ALU.max, negate=True).then_inc(S["s_shift"].sem, 1)

                            def scores_out(m):
                                w(dve, "s_exp", i, 4 * s + m + 1)
                                step(dve.reciprocal(linv[:, 2 * m:2 * m + 2], lsum[:, 2 * m:2 * m + 2]))
                                for h in range(2):
                                    ins = dve.tensor_scalar(sm[m % 2][:, h, :], sm[m % 2][:, h, :], linv[:, 2 * m + h:2 * m + h + 1], None, ALU.mult)
                                ins.then_inc(S["s_ready"].sem, 1)

                            def q_out(m):
                                w(dve, "q_exp", i, 4 * s + m + 1)
                                q4 = qs[:, 2 * m:2 * m + 2, :].rearrange("p h (g d) -> p h g d", d=HD)
                                r = qsum[:, 2 * m * HEADS:(2 * m + 2) * HEADS]
                                step(dve.tensor_reduce(r.rearrange("p (h g) -> p h g", h=2), q4, AX.X, ALU.add))
                                step(dve.reciprocal(r, r))
                                dve.tensor_tensor(q4, q4, r.rearrange("p (h g a) -> p h g a", h=2, a=1).to_broadcast([P, 2, HEADS, HD]),
                                                  ALU.mult).then_inc(S["qs_ready"].sem, 1)

                            scores_in(0)
                            scores_in(1)
                            for m in range(4):
                                q_out(m)
                            w(dve, "ek_ready", i, s + 1)
                            step(dve.tensor_tensor(kinv[:, :], ksum[:, 0:1], ksum[:, 1:2], ALU.add))
                            step(dve.reciprocal(kinv[:, :], kinv[:, :]))
                            step(dve.tensor_scalar(kinv[:, :], kinv[:, :], HD ** -0.5, None, ALU.mult))
                            scores_out(0)
                            scores_out(1)
                            for m in range(2, 4):
                                job(J_PT + m - 2)
                                if m == 2:
                                    job(J_CTX)
                                    ins = dve.scalar_tensor_tensor(ctxs[:, :], bank(s, J_CTX)[:, 0:P], kinv[:, 0:1], cst[:, C_HEAD:C_HEAD + P],
                                                                   ALU.mult, ALU.mult)
                                    step(ins)
                                    dve.sem_inc(S["ctx_ready"].sem, 1)
                                scores_in(m)
                                scores_out(m)
                            dve.sem_inc(S["dve_read"].sem, 1)
                            w(dve, "u_ready", i, s + 1)
                            for n in range(2):
                                job(J_Y + n)
                                read(dve.tensor_tensor(u[s][:, n * CT:(n + 1) * CT, :], bank(s, J_Y + n)[:, :].rearrange("p (j c) -> p j c", c=P),
                                                       u[s][:, n * CT:(n + 1) * CT, :], ALU.add))
                                dve.wait_ge(S["dve_read"].sem, S["dve_read"].at(i + 1, s * len(BY_DVE) + 9 + n + 1))
                                for j in range(CT):
                                    ins = dve.bn_stats(tbn[:, n * CT + j, :], u[s][:, n * CT + j, :])
                            step(ins)
                            step(dve.tensor_copy(bst[:, bass.ds((i * NB + s) * BT, BT), :], tbn[:, :, :]))
                        assert count[0] == S["vec"].each, count
                    dve.drain()
        if dbg is not None and last_phase == 2:
            with nc.Block() as block, nc.semaphore("dbgs") as ds:
                @block.sync
                def _(sp):
                    sp.dma_start(out_t, res[:, :, :]).then_inc(ds, 16)
                    sp.wait_ge(ds, 16)
            return

        norm_scales(False)

        with ExitStack() as ph:
            ht = [sb(f"mht{s}", [P, CT, P], scope=ph) for s in range(2)]
            hv = [sb(f"mhv{s}", [P, CHUNK], scope=ph) for s in range(2)]
            hh = [sb(f"mhh{s}", [P, CHUNK], F32R, scope=ph) for s in range(2)]
            hl = [sb(f"mhl{s}", [P, CHUNK], F32R, scope=ph) for s in range(2)]
            gv = [sb(f"mgv{r}", [P, CHUNK], scope=ph) for r in range(2)]
            gh = [sb(f"mgh{s}", [P, CT, CHUNK], F32R, scope=ph) for s in range(2)]
            gl = [sb(f"mgl{s}", [P, CT, CHUNK], F32R, scope=ph) for s in range(2)]
            acc = [sb(f"macc{s}", [P, CT, P], scope=ph) for s in range(2)]
            tbn = sb("mbn", [P, CT, 6], scope=ph)
            NB, UPS = 2, MLP // P
            S = {name: Signal(sem("m_" + name, ph), each) for name, each in {
                "ht_ready": NB, "ht_turned": NB, "h_high": NB, "h_full": NB, "h_low": NB, "h_used": NB, "up": NB * UPS, "gelu": NB * UPS,
                "g_high": NB * UPS, "g_low": NB * UPS, "down": NB, "base": NB, "base_ready": NB, "t1": NB, "t1_kept": NB, "vec": NB * 2}.items()}

            def w(eng, name, i, n):
                eng.wait_ge(S[name].sem, S[name].at(i, n))

            turnb, upb, downb = banks[0:2], banks[2:6], banks[6:8]
            with nc.Block() as block:
                @block.tensor
                def _(pe):
                    with pe.Fori(0, TOK // CHUNK // NB) as i:
                        for s in range(NB):
                            w(pe, "ht_ready", i, s + 1)
                            w(pe, "h_full", i, s)
                            for j in range(CT):
                                ins = pe.transpose(turnb[s][:, j * P:(j + 1) * P], ht[s][:, j, :], ident)
                            ins.then_inc(S["ht_turned"].sem, 1)
                            w(pe, "h_low", i, s + 1)
                            for k in range(UPS):
                                w(pe, "gelu", i, UPS * s + k)
                                c = slice(k * P, (k + 1) * P)
                                pe.matmul(upb[k][:, :], upH[:, c], hh[s][:, :], start=True, stop=False)
                                pe.matmul(upb[k][:, :], upH[:, c], hl[s][:, :], start=False, stop=False)
                                pe.matmul(upb[k][:, :], upL[:, c], hh[s][:, :], start=False, stop=True).then_inc(S["up"].sem, 1)
                            w(pe, "t1", i, s)
                            w(pe, "g_low", i, UPS * (s + 1))
                            for j in range(CT):
                                c = slice(j * P, (j + 1) * P)
                                for k in range(UPS):
                                    o = downb[s][:, c]
                                    pe.matmul(o, gh[s][:, k, c], downH[:, k, :], start=(k == 0), stop=False)
                                    pe.matmul(o, gh[s][:, k, c], downL[:, k, :], start=False, stop=False)
                                    ins = pe.matmul(o, gl[s][:, k, c], downH[:, k, :], start=False, stop=(k == UPS - 1))
                            ins.then_inc(S["down"].sem, 1)

                @block.scalar
                def _(act):
                    with act.Fori(0, TOK // CHUNK // NB) as i:
                        for s in range(NB):
                            w(act, "ht_turned", i, s + 1)
                            w(act, "down", i, s)
                            act.activation(hv[s][:, :], turnb[s][:, :], ACT.Identity, bias=col[:, N2B:N2B + 1],
                                           scale=col[:, N2G:N2G + 1]).then_inc(S["h_full"].sem, 1)
                            for k in range(UPS):
                                w(act, "up", i, UPS * s + k + 1)
                                if UPS * s + k >= 2:
                                    w(act, "g_low", i, UPS * s + k - 1)
                                act.activation(gv[k % 2][:, :], upb[k][:, :], ACT.Gelu,
                                               bias=col[:, BUP + k:BUP + k + 1]).then_inc(S["gelu"].sem, 1)
                            w(act, "t1", i, s + 1)
                            act.activation(tok[:, bass.ds((i * NB + s) * CT, CT), :], acc[s][:, :, :], ACT.Copy
                                           ).then_inc(S["t1_kept"].sem, 1)

                @block.gpsimd
                def _(pool):
                    with pool.Fori(0, TOK // CHUNK // NB) as i:
                        for s in range(NB):
                            w(pool, "base", i, s + 1)
                            pool.tensor_tensor(acc[s][:, :, :], acc[s][:, :, :],
                                               bdown_row[:, :].rearrange("p (a c) -> p a c", a=1).to_broadcast([P, CT, P]),
                                               ALU.add).then_inc(S["base_ready"].sem, 1)

                @block.vector
                def _(dve):
                    with dve.Fori(0, TOK // CHUNK // NB) as i:
                        count = [0]

                        def step(ins):
                            ins.then_inc(S["vec"].sem, 1)
                            count[0] += 1
                            w(dve, "vec", i, count[0])

                        for s in range(NB):
                            t = (i * NB + s) * CT
                            for j in range(CT):
                                ins = dve.tensor_scalar(ht[s][:, j, :], res[:, bass.ds(t + j, 1), :].rearrange("p a c -> p (a c)"),
                                                        sc_a[:, bass.ds(t + j, 1)], sc_b[:, bass.ds(t + j, 1)], ALU.mult, ALU.add)
                            ins.then_inc(S["ht_ready"].sem, 1)
                            dve.tensor_tensor(acc[s][:, :, :], tok[:, bass.ds(t, CT), :], res[:, bass.ds(t, CT), :],
                                              ALU.add).then_inc(S["base"].sem, 1)
                            w(dve, "h_full", i, s + 1)
                            dve.tensor_copy(hh[s][:, :], hv[s][:, :]).then_inc(S["h_high"].sem, 1)
                            w(dve, "h_high", i, s + 1)
                            dve.tensor_tensor(hl[s][:, :], hv[s][:, :], hh[s][:, :].bitcast(F32), ALU.subtract).then_inc(S["h_low"].sem, 1)
                            for k in range(UPS):
                                g = UPS * s + k
                                w(dve, "gelu", i, g + 1)
                                dve.tensor_copy(gh[s][:, k, :], gv[k % 2][:, :]).then_inc(S["g_high"].sem, 1)
                                w(dve, "g_high", i, g + 1)
                                dve.tensor_tensor(gl[s][:, k, :], gv[k % 2][:, :], gh[s][:, k, :].bitcast(F32),
                                                  ALU.subtract).then_inc(S["g_low"].sem, 1)
                            w(dve, "down", i, s + 1)
                            w(dve, "base_ready", i, s + 1)
                            dve.tensor_tensor(acc[s][:, :, :], downb[s][:, :].rearrange("p (j c) -> p j c", c=P),
                                              acc[s][:, :, :], ALU.add).then_inc(S["t1"].sem, 1)
                            w(dve, "t1", i, s + 1)
                            for j in range(CT):
                                ins = dve.bn_stats(tbn[:, j, :], acc[s][:, j, :])
                            step(ins)
                            step(dve.tensor_copy(bst[:, bass.ds(t, CT), :], tbn[:, :, :]))
                            w(dve, "t1_kept", i, s + 1)
                        assert count[0] == S["vec"].each
                    dve.drain()
        if dbg is not None and last_phase == 3:
            with nc.Block() as block, nc.semaphore("dbgs") as ds:
                @block.sync
                def _(sp):
                    sp.dma_start(out_t, tok[:, :, :]).then_inc(ds, 16)
                    sp.wait_ge(ds, 16)
            return

        norm_scales(False)

        gate = sb("gate", [P, TILES, EXPERTS])
        gv2 = sb("gv2", [P, TILES, 2])
        with ExitStack() as ph:
            ht = [sb(f"rht{s}", [P, CT, P], scope=ph) for s in range(2)]
            hc = [sb(f"rhc{s}", [P, CHUNK], scope=ph) for s in range(2)]
            prob = sb("prob", [P, TILES, EXPERTS], scope=ph)
            best = sb("best", [P, TILES, EXPERTS], scope=ph)
            bidx = sb("bidx", [P, TILES, EXPERTS], mybir.dt.uint32, scope=ph)
            bidf = sb("bidf", [P, TILES, 2], scope=ph)
            one = sb("one", [P, TILES, EXPERTS], scope=ph)
            rmax = sb("rmax", [P, TILES], scope=ph)
            rsum = sb("rsum", [P, TILES], scope=ph)
            NB = 2
            S = {name: Signal(sem("r_" + name, ph), each) for name, each in {
                "ht_ready": NB, "turned": NB, "hc_ready": NB, "logit": NB, "copied": NB}.items()}
            chain, expd = sem("r_chain", ph), sem("r_expd", ph)

            def w(eng, name, i, n):
                eng.wait_ge(S[name].sem, S[name].at(i, n))

            with nc.Block() as block:
                @block.tensor
                def _(pe):
                    with pe.Fori(0, TOK // CHUNK // NB) as i:
                        for s in range(NB):
                            w(pe, "ht_ready", i, s + 1)
                            w(pe, "hc_ready", i, s)
                            for j in range(CT):
                                ins = pe.transpose(banks[s][:, j * P:(j + 1) * P], ht[s][:, j, :], ident)
                            ins.then_inc(S["turned"].sem, 1)
                            w(pe, "hc_ready", i, s + 1)
                            w(pe, "copied", i, s)
                            for j in range(CT):
                                ins = pe.matmul(banks[2 + s][:, j * EXPERTS:(j + 1) * EXPERTS], hc[s][:, j * P:(j + 1) * P],
                                                routerT[:, :], start=True, stop=True)
                            ins.then_inc(S["logit"].sem, 1)

                @block.scalar
                def _(act):
                    with act.Fori(0, TOK // CHUNK // NB) as i:
                        for s in range(NB):
                            w(act, "turned", i, s + 1)
                            w(act, "logit", i, s)
                            act.activation(hc[s][:, :], banks[s][:, :], ACT.Copy).then_inc(S["hc_ready"].sem, 1)
                    act.wait_ge(chain, 2)
                    act.activation(prob[:, :, :], prob[:, :, :], ACT.Exp).then_inc(expd, 1)

                @block.vector
                def _(dve):
                    with dve.Fori(0, TOK // CHUNK // NB) as i:
                        for s in range(NB):
                            t = (i * NB + s) * CT
                            for j in range(CT):
                                ins = dve.tensor_scalar(ht[s][:, j, :], tok[:, bass.ds(t + j, 1), :].rearrange("p a c -> p (a c)"),
                                                        sc_a[:, bass.ds(t + j, 1)], sc_b[:, bass.ds(t + j, 1)], ALU.mult, ALU.add)
                            ins.then_inc(S["ht_ready"].sem, 1)
                            w(dve, "ht_ready", i, s + 1)
                            dve.tensor_copy(res[:, bass.ds(t, CT), :], ht[s][:, :, :])
                            w(dve, "logit", i, s + 1)
                            dve.tensor_copy(prob[:, bass.ds(t, CT), :], banks[2 + s][:, 0:CT * EXPERTS].rearrange("p (j e) -> p j e", e=EXPERTS)
                                            ).then_inc(S["copied"].sem, 1)
                    dve.drain()
                    n = [0]

                    def step(ins):
                        ins.then_inc(chain, 1)
                        n[0] += 1
                        dve.wait_ge(chain, n[0])

                    def each(v):
                        return v.rearrange("p (t a) -> p t a", a=1).to_broadcast([P, TILES, EXPERTS])
                    step(dve.tensor_reduce(rmax[:, :], prob[:, :, :], AX.X, ALU.max))
                    step(dve.tensor_tensor(prob[:, :, :], prob[:, :, :], each(rmax[:, :]), ALU.subtract))
                    dve.wait_ge(expd, 1)
                    step(dve.tensor_reduce(rsum[:, :], prob[:, :, :], AX.X, ALU.add))
                    step(dve.reciprocal(rsum[:, :], rsum[:, :]))
                    step(dve.tensor_tensor(prob[:, :, :], prob[:, :, :], each(rsum[:, :]), ALU.mult))
                    for t in range(TILES):
                        ins = dve.max(best[:, t, :], prob[:, t, :])
                    step(ins)
                    for t in range(TILES):
                        ins = dve.max_index(bidx[:, t, :], best[:, t, :], prob[:, t, :])
                    step(ins)
                    step(dve.tensor_copy(bidf[:, :, :], bidx[:, :, 0:2]))
                    step(dve.tensor_tensor(rsum[:, :], best[:, :, 0], best[:, :, 1], ALU.add))
                    step(dve.tensor_scalar(rsum[:, :], rsum[:, :], 1e-9, None, ALU.add))
                    step(dve.reciprocal(rsum[:, :], rsum[:, :]))
                    step(dve.tensor_tensor(gv2[:, :, :], best[:, :, 0:2],
                                           rsum[:, :].rearrange("p (t a) -> p t a", a=1).to_broadcast([P, TILES, 2]), ALU.mult))
                    iota = cst[:, C_IOTA:C_IOTA + EXPERTS].rearrange("p (a e) -> p a e", a=1).to_broadcast([P, TILES, EXPERTS])
                    for k in range(2):
                        step(dve.tensor_tensor(one[:, :, :], iota, each(bidf[:, :, k]), ALU.is_equal))
                        dst = gate if k == 0 else one
                        step(dve.tensor_tensor(dst[:, :, :], one[:, :, :], each(gv2[:, :, k]), ALU.mult))
                    step(dve.tensor_tensor(gate[:, :, :], gate[:, :, :], one[:, :, :], ALU.add))
                    dve.drain()

        with ExitStack() as ph:
            xs = sb("xs", [P, CT, P], scope=ph)
            gs = sb("gs", [P, CT, EXPERTS], scope=ph)
            xc = sb("xc", [P, CHUNK], scope=ph)
            gc = sb("gc", [EXPERTS, CHUNK], scope=ph)
            xg = [sb(f"xg{r}", [P, CHUNK], scope=ph) for r in range(2)]
            sl = [sb(f"sl{r}", [P, CHUNK], scope=ph) for r in range(2)]
            hm = [sb(f"hm{r}", [P, CHUNK], scope=ph) for r in range(2)]
            yc = sb("yc", [P, CHUNK], scope=ph)
            yt = sb("yt", [P, CT, P], scope=ph)
            K = len(HT)
            N = EXPERTS * K
            S = {name: Signal(sem("e_" + name, ph), each) for name, each in {
                "xs_ready": 1, "turned": 1, "xc_ready": 2, "gb": EXPERTS, "xg_ready": EXPERTS, "h1": N, "h3": N, "silu": N, "hm_ready": N,
                "y": N, "yc_ready": 1, "y_turned": 1, "out_ready": 1, "stored": 16}.items()}

            def w(eng, name, i, n):
                eng.wait_ge(S[name].sem, S[name].at(i, n))

            tb, gb, yb = banks[0], banks[1], banks[2]
            h1b, h3b, y2b = banks[3:5], banks[5:7], banks[7]
            with nc.Block() as block:
                @block.tensor
                def _(pe):
                    with pe.Fori(0, TOK // CHUNK) as i:
                        w(pe, "xs_ready", i, 1)
                        for j in range(CT):
                            pe.transpose(tb[:, j * P:(j + 1) * P], xs[:, j, :], ident)
                            ins = pe.transpose(gb[0:EXPERTS, j * P:(j + 1) * P], gs[:, j, :], ident)
                        ins.then_inc(S["turned"].sem, 1)
                        w(pe, "xc_ready", i, 2)

                        def down(g):
                            e, k = divmod(g, K)
                            w(pe, "hm_ready", i, g + 1)
                            m = HT[k][1]
                            pe.matmul(yb[:, :], w2T[0:m, e, k, :], hm[g % 2][0:m, :], start=(g == 0), stop=(g == N - 1)).then_inc(S["y"].sem, 1)
                        for e in range(EXPERTS):
                            w(pe, "xg_ready", i, e)
                            pe.matmul(gb[:, :], cst[0:EXPERTS, C_GATE + e * P:C_GATE + (e + 1) * P], gc[:, :], start=True, stop=True
                                      ).then_inc(S["gb"].sem, 1)
                            w(pe, "xg_ready", i, e + 1)
                            for k in range(K):
                                g = e * K + k
                                a, m = HT[k]
                                if g >= 1:
                                    w(pe, "hm_ready", i, g - 1)
                                pe.matmul(h1b[g % 2][0:m, :], w1T[:, e * HID + a:e * HID + a + m], xc[:, :], start=True, stop=True).then_inc(S["h1"].sem, 1)
                                pe.matmul(h3b[g % 2][0:m, :], w3T[:, e * HID + a:e * HID + a + m], xg[e % 2][:, :], start=True, stop=True).then_inc(S["h3"].sem, 1)
                                if g >= 1:
                                    down(g - 1)
                        down(N - 1)
                        w(pe, "yc_ready", i, 1)
                        for j in range(CT):
                            ins = pe.transpose(y2b[:, j * P:(j + 1) * P], yc[:, j * P:(j + 1) * P], ident)
                        ins.then_inc(S["y_turned"].sem, 1)

                @block.scalar
                def _(act):
                    with act.Fori(0, TOK // CHUNK) as i:
                        w(act, "turned", i, 1)
                        act.activation(xc[:, :], tb[:, :], ACT.Copy).then_inc(S["xc_ready"].sem, 1)
                        act.activation(gc[:, :], gb[0:EXPERTS, :], ACT.Copy).then_inc(S["xc_ready"].sem, 1)
                        for g in range(N):
                            m = HT[g % K][1]
                            w(act, "h1", i, g + 1)
                            if g >= 2:
                                w(act, "hm_ready", i, g - 1)
                            act.activation(sl[g % 2][0:m, :], h1b[g % 2][0:m, :], ACT.Silu).then_inc(S["silu"].sem, 1)
                        w(act, "y", i, N)
                        act.activation(yc[:, :], yb[:, :], ACT.Copy).then_inc(S["yc_ready"].sem, 1)

                @block.vector
                def _(dve):
                    with dve.Fori(0, TOK // CHUNK) as i:
                        dve.tensor_copy(gs[:, :, :], gate[:, bass.ds(i * CT, CT), :])
                        dve.tensor_copy(xs[:, :, :], res[:, bass.ds(i * CT, CT), :]).then_inc(S["xs_ready"].sem, 1)
                        w(dve, "xc_ready", i, 2)
                        for e in range(EXPERTS):
                            w(dve, "gb", i, e + 1)
                            dve.tensor_tensor(xg[e % 2][:, :], gb[:, :], xc[:, :], ALU.mult).then_inc(S["xg_ready"].sem, 1)
                            for k in range(K):
                                g = e * K + k
                                m = HT[k][1]
                                w(dve, "silu", i, g + 1)
                                w(dve, "h3", i, g + 1)
                                if g >= 2:
                                    w(dve, "y", i, g - 1)
                                dve.tensor_tensor(hm[g % 2][0:m, :], h3b[g % 2][0:m, :], sl[g % 2][0:m, :], ALU.mult).then_inc(S["hm_ready"].sem, 1)
                        w(dve, "y_turned", i, 1)
                        w(dve, "stored", i, 0)
                        dve.tensor_tensor(yt[:, :, :], y2b[:, :].rearrange("p (j c) -> p j c", c=P), tok[:, bass.ds(i * CT, CT), :],
                                          ALU.add).then_inc(S["out_ready"].sem, 1)

                @block.sync
                def _(sp):
                    for c in range(TOK // CHUNK):
                        sp.wait_ge(S["out_ready"].sem, c + 1)
                        sp.dma_start(out_t[:, c * CT:(c + 1) * CT, :], yt[:, :, :]).then_inc(S["stored"].sem, 16)
                    sp.wait_ge(S["stored"].sem, 16 * TOK // CHUNK)


_INPUTS = ["x", "L0_conv_W1", "L0_conv_b1", "L0_conv_W2", "L0_conv_b2", "L1_attn_norm1_g", "L1_attn_norm1_b",
           "L1_attn_Wq", "L1_attn_Wkv", "L1_attn_Wproj", "L1_attn_bproj", "L1_attn_norm2_g", "L1_attn_norm2_b",
           "L1_attn_W1", "L1_attn_b1", "L1_attn_W2", "L1_attn_b2", "L1_ffn_router_w", "L1_ffn_w1", "L1_ffn_w2", "L1_ffn_w3"]


def kernel(**inputs):
    import concourse.bacc as _bacc
    from concourse.bass_utils import run_bass_kernel_spmd as _run

    nc = _bacc.Bacc("TRN2", target_bir_lowering=False, num_devices=1)
    arrays, args = {}, []
    for name in _INPUTS:
        a = np.ascontiguousarray(inputs[name])
        arrays[f"in_{name}"] = a
        args.append(nc.dram_tensor(f"in_{name}", a.shape, mybir.dt.from_np(a.dtype), kind="ExternalInput").ap())
    arrays["in_consts"] = constants()
    args.append(nc.dram_tensor("in_consts", (P, C_END), F32, kind="ExternalInput").ap())
    args.append(nc.dram_tensor("out", (BATCH, SIDE, SIDE, P), F32, kind="ExternalOutput").ap())
    conv_attn_moe(nc, *args)
    r = _run(nc, [arrays], core_ids=[0])
    return r.results[0]["out"]
```

```python
from contextlib import ExitStack

import numpy as np

import concourse.bass as bass
from concourse import mybir

F32 = mybir.dt.float32
F32R = mybir.dt.float32r
BF16 = mybir.dt.bfloat16
ALU = mybir.AluOpType
ACT = mybir.ActivationFunctionType
AX = mybir.AxisListType

P = 128
BATCH, SIDE = 8, 32
PIX = SIDE * SIDE
TOK = BATCH * PIX
TILES = TOK // P
BT = PIX // P
CHUNK = 512
CT = CHUNK // P
TAPS, GROUPS, GCH = 9, 8, 16
RED = P // 4
HEADS, HD, WIN = 8, 16, 32
SPAN = P + 2 * WIN
MLP = 512
EXPERTS, HID = 8, 341
HT = [(k * P, min(P, HID - k * P)) for k in range((HID + P - 1) // P)]
HTP = HT[:-1] + [(HT[-1][0], HT[-1][1] + HID % 2)]
PADI = SIDE + 2
NEG = -1.0e30

C_ID, C_GN, C_HEAD, C_MASK = 0, P, 2 * P, 3 * P
C_HI, C_LO = C_MASK + 3 * SPAN, C_MASK + 3 * SPAN + 1
C_IOTA = C_LO + 1
C_GATE = C_IOTA + EXPERTS
C_UPPER = C_GATE
C_ONES = C_UPPER + P
COLS = 144
C_COL = C_ONES + P
C_NAME = C_COL + COLS
C_SPARE = C_NAME + 2 * TILES
C_END = C_SPARE + COLS
C_ALL = C_END + TAPS * P
ER = 8
SLOTS = 2 * TILES + EXPERTS
HIDP = HID + HID % 2


def constants():
    c = np.zeros((P, C_ALL), np.float32)
    p = np.arange(P)
    c[p, C_ID + p] = 1.0
    c[:, C_GN:C_GN + P] = (p[:, None] // 4 == p[None, :] // 4) * 0.25
    for t in range(TAPS):
        c[p, C_END + t * P + (t * P + p) // TAPS] = 1.0
    head = p // HD
    c[:, C_HEAD:C_HEAD + P] = (head[:, None] == head[None, :]) & (head[:, None] > 0)
    key = np.arange(SPAN)[None, :] // WIN
    query = p[:, None] // WIN
    near = (key >= query) & (key <= query + 2)
    for n, inside in enumerate((key >= 1, key >= 0, key < SPAN // WIN - 1)):
        c[:, C_MASK + n * SPAN:C_MASK + (n + 1) * SPAN] = np.where(near & inside, 0.0, NEG)
    c[:, C_HI] = (p < 2 * RED) | (p == 3 * RED)
    c[:, C_LO] = ((p >= 2 * RED) & (p < 3 * RED)) | (p == 3 * RED + 1)
    c[:, C_IOTA:C_IOTA + EXPERTS] = np.arange(EXPERTS)[None, :]
    c[:, C_UPPER:C_UPPER + P] = p[:, None] < p[None, :]
    c[:, C_ONES:C_ONES + P] = 1.0
    c[:, C_COL:C_COL + COLS] = np.arange(COLS)
    tile, choice = np.divmod(np.arange(2 * TILES), 2)
    c[:, C_NAME:C_NAME + 2 * TILES] = P * (1 + TILES * choice + tile)[None, :] + p[:, None]
    c[:, C_SPARE:C_SPARE + COLS] = (np.arange(COLS) % ER - (ER - 1))[None, :] * P + p[:, None]
    return c


class Signal:

    def __init__(self, sem, each):
        self.sem, self.each = sem, each

    def at(self, i, n):
        return i * self.each + n


def conv_attn_moe(nc, x, w_red, b_red, w_tap, b_tap, n1g, n1b, wq, wkv, wproj, bproj,
                  n2g, n2b, w_up, b_up, w_down, b_down, router, w1, w2, w3, consts, normed, mixed, out,
                  last_phase=9, dbg=None):
    x_t = x.rearrange("b h w c -> (b h w) c").rearrange("(n p) c -> p n c", p=P)
    normed_t = normed.rearrange("(n p) c -> p n c", p=P)
    out_t = out.rearrange("b h w c -> (b h w) c").rearrange("(n p) c -> p n c", p=P)

    with ExitStack() as ctx:
        def sb(name, shape, dt=F32, scope=ctx):
            return scope.enter_context(nc.sbuf_tensor(name, shape, dt))

        def ps(name, shape, scope=ctx):
            return scope.enter_context(nc.psum_tensor(name, shape, F32))

        def sem(name, scope=ctx):
            return scope.enter_context(nc.semaphore(name))

        cst = sb("cst", [P, C_END])
        ident = cst[:, C_ID:C_ID + P]
        eps5 = sb("eps5", [P, 1])
        tok = sb("tok", [P, TILES, P])
        res = sb("res", [P, TILES, P])
        bst = sb("bst", [P, TILES, 6])
        sc_a = sb("sc_a", [P, TILES])
        sc_b = sb("sc_b", [P, TILES])
        sc_c = sb("sc_c", [P, TILES])
        sc_d = sb("sc_d", [P, TILES])
        col = sb("col", [P, 12])
        N1G, N1B, N2G, N2B, BRED, BUP = 0, 1, 2, 3, 4, 5
        bproj_row = sb("bproj_row", [P, P])
        bdown_row = sb("bdown_row", [P, P])
        w_redT = sb("w_redT", [P, 3 * RED])
        w_taps = sb("w_taps", [P, TAPS * P], F32R)
        wqkvT = sb("wqkvT", [P, 2 * P])
        wkeyT = sb("wkeyT", [P, P])
        wprojT = sb("wprojT", [P, P])
        upH = sb("upH", [P, MLP], F32R)
        upL = sb("upL", [P, MLP], F32R)
        downT = sb("downT", [P, CT, P])
        routerT = sb("routerT", [P, EXPERTS])
        w1H, w1L, w3H, w3L = [sb(n, [P, EXPERTS * HIDP], F32R) for n in ("w1H", "w1L", "w3H", "w3L")]
        w2T = sb("w2T", [P, EXPERTS * len(HT) * P])
        w2v = w2T[:, :].rearrange("p (e k c) -> p e k c", e=EXPERTS, c=P)
        banks = [ps(f"bank{n}", [P, CHUNK]) for n in range(8)]

        with ExitStack() as ph:
            raw1 = sb("raw1", [P, EXPERTS, len(HT), P], scope=ph)
            raw3 = sb("raw3", [P, EXPERTS, len(HT), P], scope=ph)
            raw2 = sb("raw2", [P, EXPERTS, HID], scope=ph)
            rawq = sb("rawq", [P, 3, P], scope=ph)
            rawu = sb("rawu", [P, CT, P], scope=ph)
            rawd = sb("rawd", [P, MLP], scope=ph)
            rawr = sb("rawr", [EXPERTS, P], scope=ph)
            rawt = sb("rawt", [P, TAPS * GROUPS], scope=ph)
            hi_t = sb("hi_t", [P, TAPS * GROUPS], F32R, scope=ph)
            lo_t = sb("lo_t", [P, TAPS * GROUPS], F32, scope=ph)
            cleared = sem("cleared", ph)
            loaded = sem("loaded", ph)
            turned = sem("turned", ph)
            high = sem("high", ph)
            emptied = sem("emptied", ph)
            tap_step = sem("tap_step", ph)
            vec_done = sem("vec_done", ph)
            groups = []
            for raw, dst, low in ((raw1, w1H, w1L), (raw3, w3H, w3L)):
                for e in range(EXPERTS):
                    groups.append(([(raw[0:m, e, k, :], m, P, a) for k, (a, m) in enumerate(HTP)],
                                   [((P, 0, HIDP), dst[:, e * HIDP:(e + 1) * HIDP], low[:, e * HIDP:(e + 1) * HIDP])]))
            for e in range(EXPERTS):
                tail = HT[-1][1]
                groups.append(([(raw2[:, e, a:a + m], P, m, k * P) for k, (a, m) in enumerate(HT)],
                               [((P, 0, 2 * P), w2v[:, e, 0:2, :], None),
                                ((tail, 2 * P, 3 * P), w2v[0:tail, e, 2, :], None)]))
            groups.append(([(rawq[:, k, :], P, P, k * P) for k in range(3)],
                           [((P, 0, 2 * P), wqkvT[:, :], None), ((P, 2 * P, 3 * P), wprojT[:, :], None),
                            ((P, 0, HD), wkeyT[:, 0:HD], None), ((P, P + HD, 2 * P), wkeyT[:, HD:P], None)]))
            groups.append(([(rawu[:, k, :], P, P, k * P) for k in range(CT)],
                           [((P, 0, MLP), upH[:, :], upL[:, :])]))
            groups.append(([(rawd[:, k * P:(k + 1) * P], P, P, k * P) for k in range(CT)],
                           [((P, 0, 2 * P), downT[:, 0:2, :], None), ((P, 2 * P, MLP), downT[:, 2:, :], None)]))
            groups.append(([(rawr[:, :], EXPERTS, P, 0)], [((P, 0, EXPERTS // 2), routerT[:, 0:EXPERTS // 2], None), ((P, EXPERTS // 2, EXPERTS), routerT[:, EXPERTS // 2:], None)]))

            with nc.Block() as block:
                @block.vector
                def _(dve):
                    for raw in (raw1, raw3):
                        dve.memset(raw[:, :, 2, :], 0.0)
            with nc.Block() as block:
                @block.sync
                def _(sp):
                    sp.dma_start(cst[:, :], consts[:, 0:C_END]).then_inc(loaded, 16)
                    for e in range(EXPERTS):
                        for raw, w in ((raw1, w1), (raw3, w3)):
                            sp.dma_start(raw[:, e, 0:2, :], w[e, 0:2 * P, :].rearrange("(k p) c -> p k c", p=P)).then_inc(loaded, 16)
                            sp.dma_start(raw[0:HT[2][1], e, 2, :], w[e, 2 * P:HID, :]).then_inc(loaded, 16)
                    sp.dma_start(raw2[:, :, :], w2.rearrange("e c h -> c e h")).then_inc(loaded, 16)
                    for k, w in enumerate((wq, wkv, wproj)):
                        sp.dma_start(rawq[:, k, :], w).then_inc(loaded, 16)
                    sp.dma_start(rawu[:, :, :], w_up.rearrange("(k p) c -> p k c", p=P)).then_inc(loaded, 16)
                    sp.dma_start(rawd[:, :], w_down).then_inc(loaded, 16)
                    sp.dma_start(rawr[:, :], router).then_inc(loaded, 16)

                @block.scalar
                def _(act):
                    with nc.allow_non_contiguous_dma(reason="vectors with one value per partition"):
                        for n, v in ((N1G, n1g), (N1B, n1b), (N2G, n2g), (N2B, n2b)):
                            act.dma_start(col[:, n:n + 1], v.rearrange("(p a) -> p a", a=1)).then_inc(loaded, 16)
                        for k in range(3):
                            act.dma_start(col[k * RED:(k + 1) * RED, BRED:BRED + 1], b_red.rearrange("(p a) -> p a", a=1)).then_inc(loaded, 16)
                        act.dma_start(col[:, BUP:BUP + CT], b_up.rearrange("(k p) -> p k", p=P)).then_inc(loaded, 16)
                    act.dma_start(bproj_row[:, :], bproj.rearrange("(a c) -> a c", a=1).to_broadcast([P, P])).then_inc(loaded, 16)
                    act.dma_start(bdown_row[:, :], b_down.rearrange("(a c) -> a c", a=1).to_broadcast([P, P])).then_inc(loaded, 16)
                    for k in range(3):
                        act.dma_start(w_redT[:, k * RED:(k + 1) * RED], w_red).then_inc(loaded, 16)
                    act.wait_ge(cleared, 1)
                    for k in range(3):
                        act.dma_start(rawt[k * RED:(k + 1) * RED, :], w_tap).then_inc(loaded, 16)
                    for k in range(2):
                        act.dma_start(rawt[3 * RED + k:3 * RED + k + 1, :], b_tap.rearrange("(a e) -> a e", a=1)).then_inc(loaded, 16)
                    for g, (_, pieces) in enumerate(groups):
                        act.wait_ge(turned, g + 1)
                        for (rows, a, b), dst, low in pieces[:None if pieces[-1][2] is not None else -1]:
                            ins = nc.scalar.activation(dst, banks[g % 8][0:rows, a:b] if len(dst.shape) == 2 else
                                                       banks[g % 8][0:rows, a:b].rearrange("p (k c) -> p k c", c=P), ACT.Copy)
                        ins.then_inc(high, 1)

                n_loads = 1 + 4 * EXPERTS + 1 + 3 + 3 + 4 + 3 + 1 + 2 + 3 + 3 + 2

                @block.tensor
                def _(pe):
                    pe.wait_ge(loaded, 16 * n_loads)
                    for g, (turns, pieces) in enumerate(groups):
                        if g >= 8:
                            pe.wait_ge(emptied, g - 7)
                        for src, rows, cols, at in turns:
                            ins = pe.transpose(banks[g % 8][0:cols, at:at + rows], src, ident[0:rows, 0:rows])
                        ins.then_inc(turned, 1)

                @block.vector
                def _(dve):
                    dve.memset(rawt[:, :], 0.0).then_inc(cleared, 1)
                    dve.memset(eps5[:, :], 1e-5)
                    dve.wait_ge(loaded, 16 * n_loads)
                    dve.tensor_copy(hi_t[:, :], rawt[:, :]).then_inc(tap_step, 1)
                    dve.wait_ge(tap_step, 1)
                    dve.tensor_tensor(lo_t[:, :], rawt[:, :], hi_t[:, :].bitcast(F32), ALU.subtract).then_inc(tap_step, 1)
                    dve.wait_ge(tap_step, 2)
                    dve.tensor_scalar(lo_t[:, :], lo_t[:, :], cst[:, C_LO:C_LO + 1], None, ALU.mult).then_inc(tap_step, 1)
                    dve.wait_ge(tap_step, 3)
                    dve.scalar_tensor_tensor(rawt[:, :], hi_t[:, :].bitcast(F32), cst[:, C_HI:C_HI + 1], lo_t[:, :],
                                             ALU.mult, ALU.add).then_inc(tap_step, 1)
                    dve.wait_ge(tap_step, 4)
                    dve.tensor_copy(w_taps[:, :].rearrange("p (g c k) -> p g c k", g=GROUPS, k=TAPS),
                                    rawt[:, :].rearrange("p (g a k) -> p g a k", g=GROUPS, a=1)
                                    .to_broadcast([P, GROUPS, GCH, TAPS]))
                    for g, (_, pieces) in enumerate(groups):
                        dve.wait_ge(high, g + 1)
                        (rows, a, b), dst, low = pieces[-1]
                        src = banks[g % 8][0:rows, a:b]
                        if len(dst.shape) == 3:
                            src = src.rearrange("p (k c) -> p k c", c=P)
                        if low is not None:
                            dve.tensor_tensor(low, src, dst.bitcast(F32), ALU.subtract).then_inc(emptied, 1)
                        else:
                            dve.tensor_copy(dst, src).then_inc(emptied, 1)
        if last_phase < 1:
            return

        with ExitStack() as ph:
            HALF = 2
            STEPS = HALF * TAPS
            stage = [sb(f"stage{s}", [P, BT, P], scope=ph) for s in range(2)]
            norm = [sb(f"norm{s}", [P, PADI, PADI], scope=ph) for s in range(2)]
            redu = [[sb(f"redu{s}{h}", [P, CHUNK], F32R, scope=ph) for h in range(HALF)] for s in range(2)]
            PR, TR, LAG = 6, 2, 5
            high_ = [sb(f"high{s}", [P, CHUNK], F32R, scope=ph) for s in range(PR)]
            low_ = [sb(f"low{s}", [P, CHUNK], F32R, scope=ph) for s in range(PR)]
            whole = [g % 6 == 5 for g in range(STEPS)]
            SPLIT = STEPS - sum(whole)
            nth_split = [sum(not w_ for w_ in whole[:g]) for g in range(STEPS)]
            sel = res[:, 0:TAPS, :]
            conv_cm = [res[:, TAPS + h * CT:TAPS + (h + 1) * CT, :].rearrange("p j c -> p (j c)") for h in range(HALF)]
            at = TAPS + HALF * CT
            prod = [res[:, at + r * CT:at + (r + 1) * CT, :].rearrange("p j c -> p (j c)") for r in range(PR)]
            sel_r = sb("sel_r", [P, TAPS * P], F32R, scope=ph)
            bnst = sb("bnst", [P, HALF, 6], scope=ph)
            cstat = sb("cstat", [P, 1], scope=ph)
            dev4 = sb("dev4", [P, HALF, 2], scope=ph)
            gmean = sb("gmean", [P, 1], scope=ph)
            cvar = sb("cvar", [P, 1], scope=ph)
            gvar = sb("gvar", [P, 1], scope=ph)
            gsd = sb("gsd", [P, 1], scope=ph)
            grstd = sb("grstd", [P, 1], scope=ph)
            gshift = sb("gshift", [P, 1], scope=ph)
            S = {name: sem("c_" + name, ph) for name in
                 ("bordered", "x_kept", "x_turned", "cmean", "cvar", "gmean", "gvar", "gsd_set", "gsd", "chain", "gvec", "normed",
                  "reduced", "redu_high", "redu_ready", "taps", "products", "highs", "lows", "prod_used", "conv_kept", "conv_turned", "t0", "sel_loaded", "sel_ready")}
            x_loaded = [sem(f"x_loaded{s}", ph) for s in range(2)]
            T0_AT = (1, LAG + 4)
            CHAIN = 6

            def w(eng, name, count):
                if not isinstance(count, int) or count > 0:
                    eng.wait_ge(S[name], count)

            def images(eng, step):
                for n in (-1, 0):
                    step(n, n % 2, lambda d: 0 <= n + d)
                with eng.Fori(0, (BATCH - 2) // 2) as i:
                    for s in range(2):
                        step(i * 2 + s + 1, 1 - s, lambda d: True)
                for n in (BATCH - 1, BATCH):
                    step(n, n % 2, lambda d: n + d < BATCH)

            xcm, tapb, convb, backb, misc = banks[0:2], banks[2:4], banks[4:6], banks[6], banks[7]
            with nc.Block() as block:
                @block.sync
                def _(sp):
                    sp.dma_start(sel, consts[:, C_END:C_ALL].rearrange("p (t c) -> p t c", c=P)).then_inc(S["sel_loaded"], 16)
                    for b in range(BATCH):
                        if b >= 2:
                            sp.wait_ge(S["x_turned"], b - 1)
                            sp.wait_ge(S["x_kept"], b - 1)
                        sp.dma_start(stage[b % 2][:, :, :], x_t[:, b * BT:(b + 1) * BT, :]).then_inc(x_loaded[b % 2], 16)

                @block.tensor
                def _(pe):
                    def step(n, s, has):
                        def sums(n, s, g):
                            h, t = divmod(g, TAPS)
                            if whole[g]:
                                w(pe, "products", n * STEPS + g + 1)
                            else:
                                w(pe, "lows", n * SPLIT + nth_split[g] + 1)
                            if t == 0:
                                w(pe, "conv_kept", HALF * (n - 1) + h + 1)
                            select, r = sel_r[:, t * P:(t + 1) * P], g % PR
                            if whole[g]:
                                ins = pe.matmul(convb[h][:, :], select.bitcast(F32), prod[r], start=(t == 0), stop=(t == TAPS - 1))
                            else:
                                pe.matmul(convb[h][:, :], select, high_[r][:, :], start=(t == 0), stop=False)
                                ins = pe.matmul(convb[h][:, :], select, low_[r][:, :], start=False, stop=(t == TAPS - 1))
                            ins.then_inc(S["prod_used"], 1)

                        def turn_back(n, h):
                            w(pe, "conv_kept", HALF * n + h + 1)
                            w(pe, "t0", HALF * n + h)
                            for j in range(CT):
                                ins = pe.transpose(backb[:, j * P:(j + 1) * P], conv_cm[h][:, j * P:(j + 1) * P], ident)
                            ins.then_inc(S["conv_turned"], 1)

                        def turn():
                            pe.wait_ge(x_loaded[1 - s], (n + s) * 8 + 16)
                            w(pe, "redu_ready", HALF * (n + 1))
                            for h in range(HALF):
                                for j in range(CT):
                                    ins = pe.transpose(xcm[h][:, j * P:(j + 1) * P], stage[1 - s][:, h * CT + j, :], ident)
                            ins.then_inc(S["x_turned"], 1)

                        def average(of, value, result):
                            w(pe, of, n + 2)
                            pe.matmul(misc[:, 0:1], cst[:, C_GN:C_GN + P], value[:, :], start=True, stop=True).then_inc(S[result], 1)

                        def reduce(h):
                            w(pe, "normed", HALF * (n + 2))
                            pe.matmul(xcm[h][0:3 * RED, :], w_redT[:, :], norm[1 - s][:, 1 + 16 * h:17 + 16 * h, 1:1 + SIDE],
                                      start=True, stop=True).then_inc(S["reduced"], 1)

                        norm_parts = {0: turn, 3: lambda: average("cmean", cstat, "gmean"),
                                      9: lambda: average("cvar", cvar, "gvar"),
                                      15: lambda: reduce(0), 16: lambda: reduce(1)}
                        for g in range(STEPS):
                            if has(0):
                                w(pe, "redu_ready", HALF * n + g // TAPS + 1)
                                w(pe, "products", n * STEPS + g - TR + 1)
                                t = g % TAPS
                                pe.matmul(tapb[g % TR][:, :], w_taps[:, t * P:(t + 1) * P], redu[s][g // TAPS][:, :],
                                          start=True, stop=True).then_inc(S["taps"], 1)
                            if has(1) and g in norm_parts:
                                norm_parts[g]()
                            if g >= LAG and has(0):
                                sums(n, s, g - LAG)
                            elif g < LAG and has(-1):
                                sums(n - 1, 1 - s, STEPS + g - LAG)
                            if g == TAPS - 1 + LAG + 2 and has(0):
                                turn_back(n, 0)
                            if g == LAG + 1 and has(-1):
                                turn_back(n - 1, 1)
                    pe.wait_ge(S["sel_ready"], 1)
                    images(pe, step)

                @block.scalar
                def _(act):
                    act.preload_act_table(ACT.Sqrt)

                    def step(n, s, has):
                        def keep_x():
                            act.wait_ge(x_loaded[1 - s], (n + s) * 8 + 16)
                            act.activation(tok[:, bass.ds((n + 1) * BT, BT), :], stage[1 - s][:, :, :], ACT.Copy).then_inc(S["x_kept"], 1)

                        def deviation():
                            w(act, "gsd_set", n + 2)
                            act.activation(gsd[:, :], gvar[:, :], ACT.Sqrt, bias=eps5[:, 0:1]).then_inc(S["gsd"], 1)

                        def normalise(h):
                            w(act, "gvec", n + 2)
                            act.activation(norm[1 - s][:, 1 + 16 * h:17 + 16 * h, 1:1 + SIDE],
                                           xcm[h][:, :].rearrange("p (h w) -> p h w", w=SIDE), ACT.Identity,
                                           bias=gshift[:, 0:1], scale=grstd[:, 0:1]).then_inc(S["normed"], 1)

                        def reduced_high(h):
                            w(act, "reduced", HALF * (n + 1) + h + 1)
                            act.activation(redu[1 - s][h][0:3 * RED, :], xcm[h][0:3 * RED, :], ACT.Identity,
                                           bias=col[0:3 * RED, BRED:BRED + 1]).then_inc(S["redu_high"], 1)

                        def keep_conv(n, h):
                            w(act, "prod_used", n * STEPS + (h + 1) * TAPS)
                            w(act, "conv_turned", HALF * (n - 1) + h + 1)
                            act.activation(conv_cm[h], convb[h][:, :], ACT.Copy).then_inc(S["conv_kept"], 1)

                        norm_parts = {2: keep_x, 10: deviation, 12: lambda: normalise(0), 13: lambda: normalise(1),
                                      16: lambda: reduced_high(0), 17: lambda: reduced_high(1)}
                        for g in range(STEPS):
                            if has(0) and not whole[g]:
                                w(act, "products", n * STEPS + g + 1)
                                w(act, "prod_used", n * STEPS + g - PR + 1)
                                act.activation(high_[g % PR][:, :], prod[g % PR], ACT.Copy).then_inc(S["highs"], 1)
                            if has(1) and g in norm_parts:
                                norm_parts[g]()
                            if g == TAPS - 1 + LAG and has(0):
                                keep_conv(n, 0)
                            if g == LAG - 1 and has(-1):
                                keep_conv(n - 1, 1)
                    act.wait_ge(S["bordered"], 1)
                    images(act, step)

                @block.gpsimd
                def _(pool):
                    def step(n, s, has):
                        for g in range(STEPS):
                            if has(0) and not whole[g]:
                                w(pool, "highs", n * SPLIT + nth_split[g] + 1)
                                pool.tensor_tensor(low_[g % PR][:, :], prod[g % PR], high_[g % PR][:, :].bitcast(F32),
                                                   ALU.subtract).then_inc(S["lows"], 1)
                    images(pool, step)

                @block.vector
                def _(dve):
                    for s in range(2):
                        dve.memset(norm[s][:, :, :], 0.0)
                        for h in range(HALF):
                            dve.memset(redu[s][h][3 * RED:P, :].bitcast(F32), 1.0)
                    dve.drain()
                    dve.sem_inc(S["bordered"], 1)
                    dve.wait_ge(S["sel_loaded"], 16)
                    dve.tensor_copy(sel_r[:, :], sel.rearrange("p t c -> p (t c)")).then_inc(S["sel_ready"], 1)

                    def step(n, s, has):
                        def link(ins):
                            ins.then_inc(S["chain"], 1)

                        def linked(k):
                            w(dve, "chain", CHAIN * (n + 1) + k)

                        def stats():
                            w(dve, "x_turned", n + 2)
                            for h in range(HALF):
                                ins = dve.bn_stats(bnst[:, h, :], xcm[h][:, :])
                            link(ins)

                        def channel_means():
                            linked(1)
                            dve.tensor_reduce(cstat[:, :], bnst[:, :, 1::3], AX.XY, ALU.add).then_inc(S["cmean"], 1)

                        def group_mean():
                            w(dve, "gmean", n + 2)
                            link(dve.tensor_scalar(gmean[:, :], misc[:, 0:1], 0.25, None, ALU.mult))

                        def deviations():
                            linked(2)
                            link(dve.tensor_scalar(dev4[:, :, :], bnst[:, :, 1::3], gmean[:, 0:1], None, ALU.subtract))

                        def squares():
                            linked(3)
                            link(dve.tensor_tensor(dev4[:, :, :], dev4[:, :, :], dev4[:, :, :], ALU.mult))

                        def variances():
                            linked(4)
                            link(dve.scalar_tensor_tensor(dev4[:, :, :], bnst[:, :, 2::3], 2.0 * HALF / PIX, dev4[:, :, :], ALU.mult, ALU.add))

                        def channel_variances():
                            linked(5)
                            dve.tensor_reduce(cvar[:, :], dev4[:, :, :], AX.XY, ALU.add).then_inc(S["cvar"], 1)

                        def group_variance():
                            w(dve, "gvar", n + 2)
                            dve.tensor_scalar(gvar[:, :], misc[:, 0:1], 0.25, None, ALU.mult).then_inc(S["gsd_set"], 1)

                        def scale():
                            w(dve, "gsd", n + 2)
                            w(dve, "normed", HALF * (n + 1))
                            link(dve.reciprocal(grstd[:, :], gsd[:, :]))

                        def shift():
                            linked(6)
                            dve.scalar_tensor_tensor(gshift[:, :], gmean[:, :], -1.0, grstd[:, :], ALU.mult, ALU.mult).then_inc(S["gvec"], 1)

                        def low_part(h):
                            w(dve, "redu_high", HALF * (n + 1) + h + 1)
                            r = slice(RED, 2 * RED)
                            dve.scalar_tensor_tensor(redu[1 - s][h][r, :], xcm[h][r, :], col[r, BRED:BRED + 1],
                                                     redu[1 - s][h][r, :].bitcast(F32), ALU.add, ALU.subtract).then_inc(S["redu_ready"], 1)

                        def t0(n, h):
                            w(dve, "conv_turned", HALF * n + h + 1)
                            tiles = tok[:, bass.ds(n * BT + h * CT, CT), :]
                            dve.tensor_tensor(tiles, backb[:, :].rearrange("p (j c) -> p j c", c=P), tiles, ALU.add).then_inc(S["t0"], 1)

                        def t0_stats(n, h, j):
                            t = n * BT + h * CT + j
                            dve.bn_stats(bst[:, bass.ds(t, 1), :].rearrange("p a k -> p (a k)"),
                                         tok[:, bass.ds(t, 1), :].rearrange("p a c -> p (a c)"))

                        norm_parts = {1: stats, 2: channel_means, 4: group_mean, 5: deviations, 6: squares, 7: variances,
                                      8: channel_variances, 10: group_variance, 11: scale, 12: shift, 17: lambda: low_part(0)}
                        for g in range(STEPS + 1):
                            if has(1) and g in norm_parts:
                                norm_parts[g]()
                            if g == T0_AT[0] and has(-1):
                                t0(n - 1, 0)
                            if g == T0_AT[1] and has(-1):
                                t0(n - 1, 1)
                            if g == T0_AT[0] + 1 and has(-1):
                                w(dve, "t0", HALF * n - 1)
                            if g == T0_AT[1] + 1 and has(-1):
                                w(dve, "t0", HALF * n)
                            if has(0) and g < STEPS:
                                h, t = divmod(g, TAPS)
                                w(dve, "taps", n * STEPS + g + 1)
                                w(dve, "prod_used", n * STEPS + g - PR + 1)
                                dy, dx = divmod(t, 3)
                                dve.tensor_tensor(prod[g % PR].rearrange("p (h w) -> p h w", w=SIDE),
                                                  tapb[g % TR][:, :].rearrange("p (h w) -> p h w", w=SIDE),
                                                  norm[s][:, 16 * h + dy:16 * h + dy + 16, dx:dx + SIDE],
                                                  ALU.mult).then_inc(S["products"], 1)
                            if g == T0_AT[0] + 1 and has(-1):
                                for j in range(CT):
                                    t0_stats(n - 1, 0, j)
                            if g == T0_AT[1] + 1 and has(-1):
                                for j in range(CT):
                                    t0_stats(n - 1, 1, j)
                        if has(1):
                            low_part(1)
                    images(dve, step)
                    dve.drain()
        if dbg is not None and last_phase == 1:
            with nc.Block() as block, nc.semaphore("dbgs") as ds:
                @block.sync
                def _(sp):
                    sp.dma_start(out_t, tok[:, :, :]).then_inc(ds, 16)
                    sp.wait_ge(ds, 16)
            return

        def norm_scales(first, n=[0]):
            n[0] += 1
            tag = f"_{n[0]}"
            with ExitStack() as ph:
                sd = sb("sd" + tag, [P, TILES], scope=ph)
                v2 = sb("v2" + tag, [P, TILES], scope=ph)
                step, rooted = sem("step" + tag, ph), sem("rooted" + tag, ph)
                mean = sb("mean" + tag, [P, TILES], scope=ph)
                var = sb("var" + tag, [P, TILES], scope=ph)
                half = sb("half" + tag, [P, TILES], scope=ph)
                folded = sem("folded" + tag, ph)
                with nc.Block() as block:
                    @block.scalar
                    def _(act):
                        act.wait_ge(folded, 7)
                        nc.scalar.activation(sd[:, :], var[:, :], ACT.Sqrt, bias=eps5[:, 0:1]).then_inc(rooted, 1)
                        if first:
                            act.wait_ge(step, 4)
                            nc.scalar.activation(sd[:, :], v2[:, :], ACT.Sqrt, bias=eps5[:, 0:1]).then_inc(rooted, 1)

                    @block.vector
                    def _(dve):
                        me, mo = bst[:, :, 1], bst[:, :, 4]
                        fold = [
                            lambda: dve.tensor_tensor(mean[:, :], me, mo, ALU.add),
                            lambda: dve.tensor_tensor(half[:, :], me, mo, ALU.subtract),
                            lambda: dve.tensor_tensor(var[:, :], bst[:, :, 2], bst[:, :, 5], ALU.add),
                            lambda: dve.tensor_scalar(mean[:, :], mean[:, :], 0.5, None, ALU.mult),
                            lambda: dve.scalar_tensor_tensor(half[:, :], half[:, :], 0.25, half[:, :], ALU.mult, ALU.mult),
                            lambda: dve.tensor_scalar(var[:, :], var[:, :], 1.0 / P, None, ALU.mult),
                            lambda: dve.tensor_tensor(var[:, :], var[:, :], half[:, :], ALU.add),
                        ]
                        for n, part in enumerate(fold):
                            part().then_inc(folded, 1)
                            dve.wait_ge(folded, n + 1)
                        dve.wait_ge(rooted, 1)
                        dve.reciprocal(sc_a[:, :], sd[:, :]).then_inc(step, 1)
                        dve.wait_ge(step, 1)
                        dve.scalar_tensor_tensor(sc_b[:, :], mean[:, :], -1.0, sc_a[:, :], ALU.mult, ALU.mult).then_inc(step, 1)
                        if first:
                            dve.tensor_tensor(v2[:, :], var[:, :], sc_a[:, :], ALU.mult).then_inc(step, 1)
                            dve.wait_ge(step, 3)
                            dve.tensor_tensor(v2[:, :], v2[:, :], sc_a[:, :], ALU.mult).then_inc(step, 1)
                            dve.wait_ge(rooted, 2)
                            dve.reciprocal(sc_c[:, :], sd[:, :]).then_inc(step, 1)
                            dve.wait_ge(step, 5)
                            dve.tensor_tensor(sc_c[:, :], sc_c[:, :], sc_a[:, :], ALU.mult).then_inc(step, 1)
                            dve.wait_ge(step, 6)
                            dve.scalar_tensor_tensor(sc_d[:, :], mean[:, :], -1.0, sc_c[:, :], ALU.mult, ALU.mult).then_inc(step, 1)

        norm_scales(True)

        with ExitStack() as ph:
            ht = [sb(f"ht{s}", [P, BT, P], scope=ph) for s in range(2)]
            hcm = [sb(f"hcm{s}", [P, PIX + 2 * WIN], scope=ph) for s in range(2)]
            u = [sb(f"u{s}", [P, BT, P], scope=ph) for s in range(2)]
            kvt = sb("kvt", [P, BT, P], scope=ph)
            qs = sb("qs", [P, BT, P], scope=ph)
            qcm = sb("qcm", [P, PIX], scope=ph)
            ek = sb("ek", [P, PIX], scope=ph)
            ekt = sb("ekt", [P, BT, P], scope=ph)
            q0 = sb("q0", [HD, PIX], scope=ph)
            k0 = sb("k0", [HD, PIX + 2 * WIN], scope=ph)
            va = sb("va", [P, BT, HD], scope=ph)
            vb = sb("vb", [SPAN - P, BT, HD], scope=ph)
            sm = [sb(f"sm{m}", [P, 2, SPAN], scope=ph) for m in range(2)]
            pta = qs
            ptb = [t[0:SPAN - P, :, :] for t in ht]
            ctxs = sb("ctxs", [P, P], scope=ph)
            acm = ek
            qmax = sb("qmax", [P, 2 * HEADS], scope=ph)
            qsum = sb("qsum", [P, BT * HEADS], scope=ph)
            kmax = sb("kmax", [P, 2], scope=ph)
            nkmax = sb("nkmax", [P, 1], scope=ph)
            ksum = sb("ksum", [P, 2], scope=ph)
            kinv = sb("kinv", [P, 1], scope=ph)
            nmax = sb("nmax", [P, BT], scope=ph)
            lsum = sb("lsum", [P, BT], scope=ph)
            linv = sb("linv", [P, BT], scope=ph)
            tbn = sb("rbn", [P, BT, 6], scope=ph)
            NB, JOBS = 2, 28
            J_HT, J_QKV, J_KEY, J_K0, J_V, J_S, J_EKT, J_QST, J_CTX, J_PT, J_OUT, J_Y = 0, 2, 6, 8, 10, 11, 15, 17, 19, 20, 24, 26
            BY_ACT = [0, 1, 6, 7, 8, 9, 10, 15, 16, 17, 18, 20, 21, 22, 23, 24, 25]
            BY_DVE = [2, 3, 4, 5, 11, 12, 13, 14, 19, 26, 27]
            V_STEPS = 200
            S = {name: Signal(sem(name, ph), each) for name, each in {
                "done": NB * JOBS, "act_read": NB * len(BY_ACT), "dve_read": NB * len(BY_DVE),
                "ht_ready": 2 * NB, "hcm_ready": 2 * NB, "kv_ready": 4 * NB, "kmax_ready": NB, "ek_ready": NB,
                "u_raw": NB, "u_ready": NB, "u_free": NB, "q_shift": 4 * NB, "q_exp": 4 * NB, "qs_ready": 4 * NB,
                "s_shift": 4 * NB, "s_exp": 4 * NB, "s_ready": 4 * NB, "ctx_ready": NB,
                "vec": NB * 23}.items()}

            def w(eng, name, i, n):
                eng.wait_ge(S[name].sem, S[name].at(i, n))

            def bank(s, k):
                return banks[(s * JOBS + k) % 8]

            def read_out(eng, i, s, k):
                g = s * JOBS + k - 8
                i_, g = (i, g + NB * JOBS) if g < 0 else (i + 1, g)
                s_, k_ = divmod(g, JOBS)
                name, order = ("act_read", BY_ACT) if k_ in BY_ACT else ("dve_read", BY_DVE)
                w(eng, name, i_, s_ * len(order) + order.index(k_) + 1)

            with nc.Block() as block:
                @block.tensor
                def _(pe):
                    with pe.Fori(0, BATCH // NB) as i:
                        for s in range(NB):
                            def job_done(ins):
                                ins.then_inc(S["done"].sem, 1)

                            for n in range(2):
                                read_out(pe, i, s, J_HT + n)
                                w(pe, "ht_ready", i, 2 * s + n + 1)
                                for j in range(CT):
                                    ins = pe.transpose(bank(s, J_HT + n)[:, j * P:(j + 1) * P], ht[s][:, n * CT + j, :], ident)
                                job_done(ins)
                            for m in range(4):
                                w(pe, "hcm_ready", i, 2 * s + m // 2 + 1)
                                read_out(pe, i, s, J_QKV + m)
                                for h in range(2):
                                    a = WIN + (2 * m + h) * P
                                    ins = pe.matmul(bank(s, J_QKV + m)[:, h * 2 * P:(h + 1) * 2 * P], hcm[s][:, a:a + P], wqkvT[:, :],
                                                    start=True, stop=True)
                                job_done(ins)
                            for n in range(2):
                                read_out(pe, i, s, J_KEY + n)
                                a = WIN + n * CHUNK
                                job_done(pe.matmul(bank(s, J_KEY + n)[:, :], wkeyT[:, :], hcm[s][:, a:a + CHUNK], start=True, stop=True))
                            for n in range(2):
                                read_out(pe, i, s, J_K0 + n)
                                a = WIN + n * CHUNK
                                job_done(pe.matmul(bank(s, J_K0 + n)[0:HD, :], wqkvT[:, P:P + HD], hcm[s][:, a:a + CHUNK], start=True, stop=True))
                            read_out(pe, i, s, J_V)
                            for j in range(BT):
                                pe.matmul(bank(s, J_V)[:, j * 2 * HD:j * 2 * HD + HD], hcm[s][:, j * P:(j + 1) * P],
                                          wqkvT[:, P:P + HD], start=True, stop=True)
                                ins = pe.matmul(bank(s, J_V)[0:SPAN - P, j * 2 * HD + HD:(j + 1) * 2 * HD],
                                                hcm[s][:, (j + 1) * P:j * P + SPAN], wqkvT[:, P:P + HD], start=True, stop=True)
                            job_done(ins)
                            w(pe, "act_read", i + 1, s * len(BY_ACT) + BY_ACT.index(J_K0 + 1) + 1)
                            for m in range(4):
                                read_out(pe, i, s, J_S + m)
                                for h in range(2):
                                    j = 2 * m + h
                                    ins = pe.matmul(bank(s, J_S + m)[:, h * SPAN:(h + 1) * SPAN], q0[:, j * P:(j + 1) * P],
                                                    k0[:, j * P:j * P + SPAN], start=True, stop=True)
                                job_done(ins)
                            for n in range(2):
                                w(pe, "ek_ready", i, s + 1)
                                read_out(pe, i, s, J_EKT + n)
                                for j in range(CT):
                                    a = (n * CT + j) * P
                                    ins = pe.transpose(bank(s, J_EKT + n)[:, j * P:(j + 1) * P], ek[:, a:a + P], ident)
                                job_done(ins)
                            for n in range(2):
                                w(pe, "qs_ready", i, 4 * s + 2 * n + 2)
                                read_out(pe, i, s, J_QST + n)
                                for j in range(CT):
                                    ins = pe.transpose(bank(s, J_QST + n)[:, j * P:(j + 1) * P], qs[:, n * CT + j, :], ident)
                                job_done(ins)
                            w(pe, "act_read", i + 1, s * len(BY_ACT) + BY_ACT.index(J_EKT + 1) + 1)
                            w(pe, "kv_ready", i, 4 * s + 4)
                            read_out(pe, i, s, J_CTX)
                            for j in range(BT):
                                ins = pe.matmul(bank(s, J_CTX)[:, 0:P], ekt[:, j, :], kvt[:, j, :], start=(j == 0), stop=(j == BT - 1))
                            job_done(ins)
                            for m in range(4):
                                w(pe, "s_ready", i, 4 * s + m + 1)
                                read_out(pe, i, s, J_PT + m)
                                for h in range(2):
                                    a = 2 * h * P
                                    pe.transpose(bank(s, J_PT + m)[:, a:a + P], sm[m % 2][:, h, 0:P], ident)
                                    ins = pe.transpose(bank(s, J_PT + m)[0:SPAN - P, a + P:a + 2 * P], sm[m % 2][:, h, P:SPAN], ident)
                                job_done(ins)
                            for n in range(2):
                                w(pe, "ctx_ready", i, s + 1)
                                w(pe, "act_read", i + 1, s * len(BY_ACT) + BY_ACT.index(J_PT + 2 * n + 1) + 1)
                                read_out(pe, i, s, J_OUT + n)
                                pe.matmul(bank(s, J_OUT + n)[:, :], ctxs[:, :], qcm[:, n * CHUNK:(n + 1) * CHUNK],
                                          start=True, stop=False, skip_group_check=True)
                                for t in range(CT):
                                    j = n * CT + t
                                    o = bank(s, J_OUT + n)[0:HD, t * P:(t + 1) * P]
                                    pe.matmul(o, va[:, j, :], pta[:, j, :], start=False, stop=False, skip_group_check=True)
                                    ins = pe.matmul(o, vb[:, j, :], ptb[s][:, j, :], start=False, stop=True, skip_group_check=True)
                                job_done(ins)
                            for n in range(2):
                                w(pe, "act_read", i + 1, s * len(BY_ACT) + BY_ACT.index(J_OUT + n) + 1)
                                read_out(pe, i, s, J_Y + n)
                                for t in range(CT):
                                    j = n * CT + t
                                    ins = pe.matmul(bank(s, J_Y + n)[:, t * P:(t + 1) * P], acm[:, j * P:(j + 1) * P], wprojT[:, :],
                                                    start=True, stop=True)
                                job_done(ins)

                def pt_out(act, i, s, m, job, read):
                    job(J_PT + m)
                    pv = bank(s, J_PT + m)[:, :].rearrange("p (h k c) -> p h k c", h=2, k=2)
                    act.activation(pta[:, 2 * m:2 * m + 2, :], pv[:, :, 0, :], ACT.Copy)
                    read(act.activation(ptb[s][:, 2 * m:2 * m + 2, :], pv[0:SPAN - P, :, 1, :], ACT.Copy))

                @block.scalar
                def _(act):
                    act.sem_inc(S["act_read"].sem, S["act_read"].each)
                    with act.Fori(0, BATCH // NB) as i:
                        for s in range(NB):
                            def job(k):
                                w(act, "done", i, s * JOBS + k + 1)

                            def read(ins):
                                ins.then_inc(S["act_read"].sem, 1)

                            for j in range(BT):
                                t = (i * NB + s) * BT + j
                                ins = act.activation(u[s][:, j, :], tok[:, bass.ds(t, 1), :].rearrange("p a c -> p (a c)"),
                                                     ACT.Identity, bias=sc_b[:, bass.ds(t, 1)], scale=sc_a[:, bass.ds(t, 1)])
                            ins.then_inc(S["u_raw"].sem, 1)
                            for n in range(2):
                                job(J_HT + n)
                                ins = act.activation(hcm[s][:, WIN + n * CHUNK:WIN + (n + 1) * CHUNK], bank(s, J_HT + n)[:, :], ACT.Identity,
                                                     bias=col[:, N1B:N1B + 1], scale=col[:, N1G:N1G + 1])
                                read(ins)
                                act.wait_ge(S["act_read"].sem, S["act_read"].at(i + 1, s * len(BY_ACT) + n + 1))
                                act.sem_inc(S["hcm_ready"].sem, 1)
                            for m in range(4):
                                job(J_QKV + m)
                                if m == 0:
                                    w(act, "done", i, s * JOBS)
                                act.activation(kvt[:, 2 * m:2 * m + 2, :],
                                               bank(s, J_QKV + m)[:, :].rearrange("p (h c) -> p h c", h=2)[:, :, P:2 * P],
                                               ACT.Copy).then_inc(S["kv_ready"].sem, 1)
                            w(act, "kmax_ready", i, s + 1)
                            for n in range(2):
                                job(J_KEY + n)
                                act.activation(q0[:, n * CHUNK:(n + 1) * CHUNK], bank(s, J_KEY + n)[0:HD, :], ACT.Copy)
                                read(act.activation(ek[:, n * CHUNK:(n + 1) * CHUNK], bank(s, J_KEY + n)[:, :], ACT.Exp,
                                                    bias=nkmax[:, 0:1], accum_out=ksum[:, n:n + 1]))
                            act.wait_ge(S["act_read"].sem, S["act_read"].at(i + 1, s * len(BY_ACT) + BY_ACT.index(J_KEY + 1) + 1))
                            act.sem_inc(S["ek_ready"].sem, 1)
                            for n in range(2):
                                job(J_K0 + n)
                                read(act.activation(k0[:, WIN + n * CHUNK:WIN + (n + 1) * CHUNK], bank(s, J_K0 + n)[0:HD, :], ACT.Copy))
                            job(J_V)
                            vv = bank(s, J_V)[:, 0:BT * 2 * HD].rearrange("p (j k e) -> p j k e", j=BT, k=2)
                            act.activation(va[:, :, :], vv[:, :, 0, :], ACT.Copy)
                            read(act.activation(vb[:, :, :], vv[0:SPAN - P, :, 1, :], ACT.Copy))
                            for m in range(4):
                                w(act, "q_shift", i, 4 * s + m + 1)
                                act.activation(qs[:, 2 * m:2 * m + 2, :], qs[:, 2 * m:2 * m + 2, :], ACT.Exp).then_inc(S["q_exp"].sem, 1)
                            for n in range(2):
                                job(J_EKT + n)
                                read(act.activation(ekt[:, n * CT:(n + 1) * CT, :], bank(s, J_EKT + n)[:, :].rearrange("p (j c) -> p j c", c=P), ACT.Copy))
                            for n in range(2):
                                job(J_QST + n)
                                read(act.activation(qcm[:, n * CHUNK:(n + 1) * CHUNK], bank(s, J_QST + n)[:, :], ACT.Copy))
                            for m in range(4):
                                w(act, "s_shift", i, 4 * s + m + 1)
                                for h in range(2):
                                    j = 2 * m + h
                                    ins = act.activation(sm[m % 2][:, h, :], sm[m % 2][:, h, :], ACT.Exp, bias=nmax[:, j:j + 1],
                                                         accum_out=lsum[:, j:j + 1])
                                ins.then_inc(S["s_exp"].sem, 1)
                                if m >= 1:
                                    pt_out(act, i, s, m - 1, job, read)
                            pt_out(act, i, s, 3, job, read)
                            for n in range(2):
                                job(J_OUT + n)
                                read(act.activation(acm[:, n * CHUNK:(n + 1) * CHUNK], bank(s, J_OUT + n)[:, :], ACT.Copy))
                            act.wait_ge(S["dve_read"].sem, S["dve_read"].at(i + 1, (s + 1) * len(BY_DVE)))
                            act.activation(res[:, bass.ds((i * NB + s) * BT, BT), :], u[s][:, :, :], ACT.Copy).then_inc(S["u_free"].sem, 1)
                            w(act, "u_free", i, s + 1)

                @block.gpsimd
                def _(pool):
                    with pool.Fori(0, BATCH // NB) as i:
                        for s in range(NB):
                            w(pool, "u_raw", i, s + 1)
                            pool.tensor_tensor(u[s][:, :, :], u[s][:, :, :],
                                               bproj_row[:, :].rearrange("p (a c) -> p a c", a=1).to_broadcast([P, BT, P]),
                                               ALU.add).then_inc(S["u_ready"].sem, 1)

                @block.vector
                def _(dve):
                    for s in range(2):
                        dve.memset(hcm[s][:, :], 0.0)
                    dve.memset(k0[:, :], 0.0)
                    dve.drain()
                    dve.sem_inc(S["dve_read"].sem, S["dve_read"].each)
                    with dve.Fori(0, BATCH // NB) as i:
                        count = [0]

                        def step(ins):
                            ins.then_inc(S["vec"].sem, 1)
                            count[0] += 1
                            w(dve, "vec", i, count[0])

                        for s in range(NB):
                            def job(k):
                                w(dve, "done", i, s * JOBS + k + 1)

                            def read(ins):
                                ins.then_inc(S["dve_read"].sem, 1)

                            for j in range(BT):
                                t = (i * NB + s) * BT + j
                                ins = dve.tensor_scalar(ht[s][:, j, :], tok[:, bass.ds(t, 1), :].rearrange("p a c -> p (a c)"),
                                                        sc_c[:, bass.ds(t, 1)], sc_d[:, bass.ds(t, 1)], ALU.mult, ALU.add)
                                if j % CT == CT - 1:
                                    ins.then_inc(S["ht_ready"].sem, 1)
                            for m in range(4):
                                w(dve, "kv_ready", i, 4 * s + m + 1)
                                q4 = bank(s, J_QKV + m)[:, :].rearrange("p (h c) -> p h c", h=2)[:, :, 0:P].rearrange("p h (g d) -> p h g d", d=HD)
                                step(dve.tensor_reduce(qmax[:, :].rearrange("p (h g) -> p h g", h=2), q4, AX.X, ALU.max))
                                ins = dve.tensor_tensor(qs[:, 2 * m:2 * m + 2, :].rearrange("p h (g d) -> p h g d", d=HD), q4,
                                                        qmax[:, :].rearrange("p (h g a) -> p h g a", h=2, a=1).to_broadcast([P, 2, HEADS, HD]),
                                                        ALU.subtract)
                                read(ins)
                                dve.wait_ge(S["dve_read"].sem, S["dve_read"].at(i + 1, s * len(BY_DVE) + m + 1))
                                dve.sem_inc(S["q_shift"].sem, 1)
                            for n in range(2):
                                job(J_KEY + n)
                                ins = dve.tensor_reduce(kmax[:, n:n + 1], bank(s, J_KEY + n)[:, :], AX.X, ALU.max)
                            step(ins)
                            dve.tensor_reduce(nkmax[:, :], kmax[:, :], AX.X, ALU.max, negate=True).then_inc(S["kmax_ready"].sem, 1)

                            def scores_in(m):
                                job(J_S + m)
                                for h in range(2):
                                    j = 2 * m + h
                                    kind = 0 if j == 0 else 2 if j == BT - 1 else 1
                                    ins = dve.scalar_tensor_tensor(sm[m % 2][:, h, :], bank(s, J_S + m)[:, h * SPAN:(h + 1) * SPAN], HD ** -0.5,
                                                                   cst[:, C_MASK + kind * SPAN:C_MASK + (kind + 1) * SPAN], ALU.mult, ALU.add)
                                read(ins)
                                dve.wait_ge(S["dve_read"].sem, S["dve_read"].at(i + 1, s * len(BY_DVE) + 4 + m + 1))
                                dve.tensor_reduce(nmax[:, 2 * m:2 * m + 2], sm[m % 2][:, :, :], AX.X, ALU.max, negate=True).then_inc(S["s_shift"].sem, 1)

                            def scores_out(m):
                                w(dve, "s_exp", i, 4 * s + m + 1)
                                step(dve.reciprocal(linv[:, 2 * m:2 * m + 2], lsum[:, 2 * m:2 * m + 2]))
                                for h in range(2):
                                    ins = dve.tensor_scalar(sm[m % 2][:, h, :], sm[m % 2][:, h, :], linv[:, 2 * m + h:2 * m + h + 1], None, ALU.mult)
                                ins.then_inc(S["s_ready"].sem, 1)

                            def q_out(m):
                                w(dve, "q_exp", i, 4 * s + m + 1)
                                q4 = qs[:, 2 * m:2 * m + 2, :].rearrange("p h (g d) -> p h g d", d=HD)
                                r = qsum[:, 2 * m * HEADS:(2 * m + 2) * HEADS]
                                step(dve.tensor_reduce(r.rearrange("p (h g) -> p h g", h=2), q4, AX.X, ALU.add))
                                step(dve.reciprocal(r, r))
                                dve.tensor_tensor(q4, q4, r.rearrange("p (h g a) -> p h g a", h=2, a=1).to_broadcast([P, 2, HEADS, HD]),
                                                  ALU.mult).then_inc(S["qs_ready"].sem, 1)

                            scores_in(0)
                            scores_in(1)
                            for m in range(4):
                                q_out(m)
                            w(dve, "ek_ready", i, s + 1)
                            step(dve.tensor_tensor(kinv[:, :], ksum[:, 0:1], ksum[:, 1:2], ALU.add))
                            step(dve.reciprocal(kinv[:, :], kinv[:, :]))
                            step(dve.tensor_scalar(kinv[:, :], kinv[:, :], HD ** -0.5, None, ALU.mult))
                            scores_out(0)
                            scores_out(1)
                            for m in range(2, 4):
                                job(J_PT + m - 2)
                                if m == 2:
                                    job(J_CTX)
                                    ins = dve.scalar_tensor_tensor(ctxs[:, :], bank(s, J_CTX)[:, 0:P], kinv[:, 0:1], cst[:, C_HEAD:C_HEAD + P],
                                                                   ALU.mult, ALU.mult)
                                    step(ins)
                                    dve.sem_inc(S["ctx_ready"].sem, 1)
                                scores_in(m)
                                scores_out(m)
                            dve.sem_inc(S["dve_read"].sem, 1)
                            w(dve, "u_ready", i, s + 1)
                            for n in range(2):
                                job(J_Y + n)
                                read(dve.tensor_tensor(u[s][:, n * CT:(n + 1) * CT, :], bank(s, J_Y + n)[:, :].rearrange("p (j c) -> p j c", c=P),
                                                       u[s][:, n * CT:(n + 1) * CT, :], ALU.add))
                                dve.wait_ge(S["dve_read"].sem, S["dve_read"].at(i + 1, s * len(BY_DVE) + 9 + n + 1))
                                for j in range(CT):
                                    ins = dve.bn_stats(tbn[:, n * CT + j, :], u[s][:, n * CT + j, :])
                            step(ins)
                            step(dve.tensor_copy(bst[:, bass.ds((i * NB + s) * BT, BT), :], tbn[:, :, :]))
                        assert count[0] == S["vec"].each, count
                    dve.drain()
        if dbg is not None and last_phase == 2:
            with nc.Block() as block, nc.semaphore("dbgs") as ds:
                @block.sync
                def _(sp):
                    sp.dma_start(out_t, res[:, :, :]).then_inc(ds, 16)
                    sp.wait_ge(ds, 16)
            return

        norm_scales(False)

        with ExitStack() as ph:
            CHUNKS, UPS = TOK // CHUNK, MLP // P
            ht = [sb(f"mht{s}", [P, CT, P], scope=ph) for s in range(2)]
            hv = [sb(f"mhv{s}", [P, CHUNK], scope=ph) for s in range(2)]
            hh = [sb(f"mhh{s}", [P, CHUNK], F32R, scope=ph) for s in range(2)]
            hl = [sb(f"mhl{s}", [P, CHUNK], F32R, scope=ph) for s in range(2)]
            gv = [sb(f"mgv{s}", [P, UPS, CHUNK], scope=ph) for s in range(2)]
            acc = [sb(f"macc{s}", [P, CT, P], scope=ph) for s in range(2)]
            tbn = [sb(f"mbn{s}", [P, CT, 6], scope=ph) for s in range(2)]
            S = {name: sem("m_" + name, ph) for name in
                 ("ht_ready", "ht_turned", "h_full", "h_high", "h_low", "up", "gelu", "down", "base", "base_ready", "t1",
                  "stats", "t1_kept")}

            def w(eng, name, count):
                if not isinstance(count, int) or count > 0:
                    eng.wait_ge(S[name], count)

            def steps(eng, step):
                for n in range(-3, 2):
                    step(n, n % 2, lambda d: 0 <= n + d < CHUNKS)
                with eng.Fori(1, (CHUNKS - 4) // 2) as i:
                    for s in range(2):
                        step(i * 2 + s, s, lambda d: True)
                for n in range(2 * ((CHUNKS - 4) // 2), CHUNKS + 1):
                    step(n, n % 2, lambda d: 0 <= n + d < CHUNKS)

            turnb, upb, downb = banks[0:2], banks[2:6], banks[6:8]
            with nc.Block() as block:
                @block.tensor
                def _(pe):
                    def step(n, s, has):
                        if has(2):
                            w(pe, "ht_ready", n + 3)
                            w(pe, "h_full", n + 1)
                            for j in range(CT):
                                ins = pe.transpose(turnb[s][:, j * P:(j + 1) * P], ht[s][:, j, :], ident)
                            ins.then_inc(S["ht_turned"], 1)
                        if has(1):
                            w(pe, "h_low", n + 2)
                            for k in range(UPS):
                                w(pe, "gelu", UPS * n + k + 1)
                                c = slice(k * P, (k + 1) * P)
                                pe.matmul(upb[k][:, :], upH[:, c], hh[1 - s][:, :], start=True, stop=False)
                                pe.matmul(upb[k][:, :], upH[:, c], hl[1 - s][:, :], start=False, stop=False)
                                pe.matmul(upb[k][:, :], upL[:, c], hh[1 - s][:, :], start=False, stop=True).then_inc(S["up"], 1)
                        if has(0):
                            w(pe, "t1", n - 1)
                            w(pe, "gelu", UPS * (n + 1))
                            for j in range(CT):
                                c = slice(j * P, (j + 1) * P)
                                for k in range(UPS):
                                    ins = pe.matmul(downb[s][:, c], gv[s][:, k, c], downT[:, k, :], start=(k == 0), stop=(k == UPS - 1))
                            ins.then_inc(S["down"], 1)
                    steps(pe, step)

                @block.scalar
                def _(act):
                    act.preload_act_table(ACT.Gelu)

                    def step(n, s, has):
                        if has(2):
                            w(act, "ht_turned", n + 3)
                            w(act, "h_low", n + 1)
                            act.activation(hv[s][:, :], turnb[s][:, :], ACT.Identity, bias=col[:, N2B:N2B + 1],
                                           scale=col[:, N2G:N2G + 1]).then_inc(S["h_full"], 1)
                        for k in range(UPS):
                            if has(1):
                                w(act, "up", UPS * (n + 1) + k + 1)
                                if k == 0:
                                    w(act, "down", n)
                                act.activation(gv[1 - s][:, k, :], upb[k][:, :], ACT.Gelu,
                                               bias=col[:, BUP + k:BUP + k + 1]).then_inc(S["gelu"], 1)
                            if k == 0 and has(-1):
                                w(act, "t1", n)
                                act.activation(tok[:, bass.ds((n - 1) * CT, CT), :], acc[1 - s][:, :, :], ACT.Copy
                                               ).then_inc(S["t1_kept"], 1)
                    steps(act, step)

                @block.gpsimd
                def _(pool):
                    def step(n, s, has):
                        if has(0):
                            w(pool, "base", n + 1)
                            pool.tensor_tensor(acc[s][:, :, :], acc[s][:, :, :],
                                               bdown_row[:, :].rearrange("p (a c) -> p a c", a=1).to_broadcast([P, CT, P]),
                                               ALU.add).then_inc(S["base_ready"], 1)
                    steps(pool, step)

                @block.vector
                def _(dve):
                    def step(n, s, has):
                        if has(-1):
                            w(dve, "down", n)
                            w(dve, "base_ready", n)
                            a = acc[1 - s]
                            dve.tensor_tensor(a[:, :, :], downb[1 - s][:, :].rearrange("p (j c) -> p j c", c=P),
                                              a[:, :, :], ALU.add).then_inc(S["t1"], 1)
                        if has(2):
                            w(dve, "h_full", n + 3)
                            w(dve, "up", UPS * (n + 1))
                            dve.tensor_copy(hh[s][:, :], hv[s][:, :]).then_inc(S["h_high"], 1)
                        if has(-1):
                            w(dve, "t1", n)
                            for j in range(CT):
                                ins = dve.bn_stats(tbn[1 - s][:, j, :], a[:, j, :])
                            ins.then_inc(S["stats"], 1)
                        if has(2):
                            w(dve, "h_high", n + 3)
                            dve.tensor_tensor(hl[s][:, :], hv[s][:, :], hh[s][:, :].bitcast(F32), ALU.subtract).then_inc(S["h_low"], 1)
                        if has(0):
                            w(dve, "t1_kept", n - 1)
                            dve.tensor_tensor(acc[s][:, :, :], tok[:, bass.ds(n * CT, CT), :], res[:, bass.ds(n * CT, CT), :],
                                              ALU.add).then_inc(S["base"], 1)
                        if has(3):
                            w(dve, "ht_turned", n + 2)
                            for j in range(CT):
                                t = (n + 3) * CT + j
                                ins = dve.tensor_scalar(ht[1 - s][:, j, :], res[:, bass.ds(t, 1), :].rearrange("p a c -> p (a c)"),
                                                        sc_a[:, bass.ds(t, 1)], sc_b[:, bass.ds(t, 1)], ALU.mult, ALU.add)
                            ins.then_inc(S["ht_ready"], 1)
                        if has(-1):
                            w(dve, "stats", n)
                            dve.tensor_copy(bst[:, bass.ds((n - 1) * CT, CT), :], tbn[1 - s][:, :, :])
                    steps(dve, step)
                    dve.drain()
        if dbg is not None and last_phase == 3:
            with nc.Block() as block, nc.semaphore("dbgs") as ds:
                @block.sync
                def _(sp):
                    sp.dma_start(out_t, tok[:, :, :]).then_inc(ds, 16)
                    sp.wait_ge(ds, 16)
            return

        norm_scales(False)

        gates = sb("gates", [P, TILES, 2])
        to_load = sb("to_load", [P, COLS], mybir.dt.uint32)
        to_store = sb("to_store", [P, COLS], mybir.dt.uint32)
        expert = sb("expert", [P, COLS], mybir.dt.int32)
        with ExitStack() as ph:
            NB = 4
            ht = [sb(f"rht{s}", [P, CT, P], scope=ph) for s in range(NB)]
            hc = [sb(f"rhc{s}", [P, CHUNK], scope=ph) for s in range(2)]
            prob = sb("prob", [P, TILES, EXPERTS], scope=ph)
            best = sb("best", [P, TILES, EXPERTS], scope=ph)
            bidx = sb("bidx", [P, TILES, EXPERTS], mybir.dt.uint32, scope=ph)
            bidf = sb("bidf", [P, TILES, 2], scope=ph)
            one = [sb(f"one{k}", [P, TILES, EXPERTS], scope=ph) for k in range(2)]
            chosen = sb("chosen", [P, TILES, EXPERTS], scope=ph)
            rank = sb("rank", [P, TILES, EXPERTS], scope=ph)
            cum = [sb(f"cum{k}", [P, TILES, EXPERTS], scope=ph) for k in range(2)]
            rmax = sb("rmax", [P, TILES], scope=ph)
            rsum = sb("rsum", [P, TILES], scope=ph)
            size = [sb(f"size{k}", [P, EXPERTS], scope=ph) for k in range(3)]
            whole8 = sb("whole8", [P, EXPERTS], mybir.dt.int32, scope=ph)
            slot = sb("slot", [P, TILES, 2], scope=ph)
            slot_hi = sb("slot_hi", [P, TILES, 2], scope=ph)
            slot_i = sb("slot_i", [P, TILES, 2], mybir.dt.int32, scope=ph)
            tab = sb("tab", [P, COLS], scope=ph)
            tmp = [sb(f"tmp{k}", [P, COLS], scope=ph) for k in range(2)]
            RING = 8
            is_lo = [sb(f"is_lo{r}", [P, P], scope=ph) for r in range(RING)]
            is_hi = [sb(f"is_hi{r}", [P, COLS], scope=ph) for r in range(RING)]
            kept = [sem(f"r_kept{s}", ph) for s in range(NB)]
            S = {name: Signal(sem("r_" + name, ph), each) for name, each in {
                "ht_ready": NB, "turned": NB, "hc_ready": NB, "logit": NB, 
                "hot": RING, "hot_used": RING}.items()}
            chain, expd, counted, tabled = sem("r_chain", ph), sem("r_expd", ph), sem("r_counted", ph), sem("r_tabled", ph)
            to_count, to_exp = sem("r_to_count", ph), sem("r_to_exp", ph)

            def w(eng, name, i, n):
                eng.wait_ge(S[name].sem, S[name].at(i, n))

            def logits_out(dve, c):
                dve.wait_ge(S["logit"].sem, c + 1)
                dve.tensor_copy(prob[:, c * CT:(c + 1) * CT, :], banks[2 + c % NB][:, 0:CT * EXPERTS].rearrange("p (j e) -> p j e", e=EXPERTS))

            with nc.Block() as block:
                @block.sync
                def _(sp):
                    for c in range(TOK // CHUNK):
                        sp.wait_ge(S["ht_ready"].sem, c + 1)
                        sp.dma_start(normed_t[:, c * CT:(c + 1) * CT, :], ht[c % NB][:, :, :]).then_inc(kept[c % NB], 16)
                    for s in range(NB):
                        sp.wait_ge(kept[s], 16 * (TOK // CHUNK // NB))

                @block.tensor
                def _(pe):
                    with pe.Fori(0, TOK // CHUNK // NB) as i:
                        for s in range(NB):
                            w(pe, "ht_ready", i, s + 1)
                            for j in range(CT):
                                ins = pe.transpose(banks[s % 2][:, j * P:(j + 1) * P], ht[s][:, j, :], ident)
                            ins.then_inc(S["turned"].sem, 1)
                            w(pe, "hc_ready", i, s + 1)
                            for j in range(CT):
                                ins = pe.matmul(banks[2 + s][:, j * EXPERTS:(j + 1) * EXPERTS], hc[s % 2][:, j * P:(j + 1) * P],
                                                routerT[:, :], start=True, stop=True)
                            ins.then_inc(S["logit"].sem, 1)
                    pe.wait_ge(to_count, 1)
                    m = chosen[:, :, :].rearrange("p t e -> p (t e)")
                    pe.matmul(banks[4][:, :], cst[:, C_UPPER:C_UPPER + P], m, start=True, stop=True)
                    pe.matmul(banks[5][:, :], cst[:, C_ONES:C_ONES + P], m, start=True, stop=True).then_inc(counted, 1)
                    with pe.Fori(0, 2 * TILES // RING) as i:
                        for r in range(RING):
                            w(pe, "hot", i, r + 1)
                            pe.matmul(banks[6][:, 0:COLS], is_lo[r][:, :], is_hi[r][:, :], start=False, stop=True, skip_group_check=True).then_inc(S["hot_used"].sem, 1)

                @block.scalar
                def _(act):
                    act.preload_act_table(ACT.Exp)
                    with act.Fori(0, TOK // CHUNK // NB) as i:
                        for s in range(NB):
                            w(act, "turned", i, s + 1)
                            act.activation(hc[s % 2][:, :], banks[s % 2][:, :], ACT.Copy).then_inc(S["hc_ready"].sem, 1)
                    act.wait_ge(to_exp, 1)
                    act.activation(prob[:, :, :], prob[:, :, :], ACT.Exp).then_inc(expd, 1)

                @block.vector
                def _(dve):
                    for c in range(TOK // CHUNK):
                        s = c % NB
                        t = c * CT
                        if c >= NB:
                            dve.wait_ge(kept[s], 16 * (c // NB))
                            dve.wait_ge(S["turned"].sem, c - NB + 1)
                        for j in range(CT):
                            ins = dve.tensor_scalar(ht[s][:, j, :], tok[:, t + j, :], sc_a[:, t + j:t + j + 1], sc_b[:, t + j:t + j + 1],
                                                    ALU.mult, ALU.add)
                        ins.then_inc(S["ht_ready"].sem, 1)
                        if c >= 2:
                            logits_out(dve, c - 2)
                    for c in (TOK // CHUNK - 2, TOK // CHUNK - 1):
                        logits_out(dve, c)
                    dve.drain()
                    n = [0]

                    def step(ins):
                        ins.then_inc(chain, 1)
                        n[0] += 1
                        dve.wait_ge(chain, n[0])

                    def each(v):
                        return v.rearrange("p (t a) -> p t a", a=1).to_broadcast([P, TILES, EXPERTS])

                    def over(v):
                        return v.rearrange("p (a e) -> p a e", a=1).to_broadcast([P, TILES, EXPERTS])
                    step(dve.tensor_reduce(rmax[:, :], prob[:, :, :], AX.X, ALU.max))
                    dve.tensor_tensor(prob[:, :, :], prob[:, :, :], each(rmax[:, :]), ALU.subtract).then_inc(to_exp, 1)
                    dve.wait_ge(expd, 1)
                    step(dve.tensor_reduce(rsum[:, :], prob[:, :, :], AX.X, ALU.add))
                    step(dve.reciprocal(rsum[:, :], rsum[:, :]))
                    step(dve.tensor_tensor(prob[:, :, :], prob[:, :, :], each(rsum[:, :]), ALU.mult))
                    for t in range(TILES):
                        ins = dve.max(best[:, t, :], prob[:, t, :])
                    step(ins)
                    for t in range(TILES):
                        ins = dve.max_index(bidx[:, t, :], best[:, t, :], prob[:, t, :])
                    step(ins)
                    step(dve.tensor_copy(bidf[:, :, :], bidx[:, :, 0:2]))
                    iota = over(cst[:, C_IOTA:C_IOTA + EXPERTS])
                    for k in range(2):
                        ins = dve.tensor_tensor(one[k][:, :, :], iota, each(bidf[:, :, k]), ALU.is_equal)
                    step(ins)
                    dve.tensor_tensor(chosen[:, :, :], one[0][:, :, :], one[1][:, :, :], ALU.add).then_inc(to_count, 1)
                    step(dve.tensor_tensor(rsum[:, :], best[:, :, 0], best[:, :, 1], ALU.add))
                    step(dve.tensor_scalar(rsum[:, :], rsum[:, :], 1e-9, None, ALU.add))
                    step(dve.reciprocal(rsum[:, :], rsum[:, :]))
                    dve.tensor_tensor(gates[:, :, :], best[:, :, 0:2],
                                      rsum[:, :].rearrange("p (t a) -> p t a", a=1).to_broadcast([P, TILES, 2]), ALU.mult)
                    dve.memset(banks[6][:, :], 0.0)
                    dve.wait_ge(counted, 1)
                    total = banks[5][:, :].rearrange("p (t e) -> p t e", e=EXPERTS)
                    step(dve.tensor_copy(cum[0][:, :, :], total))
                    a, d = 0, 1
                    while d < TILES:
                        dve.tensor_copy(cum[1 - a][:, 0:d, :], cum[a][:, 0:d, :])
                        step(dve.tensor_tensor(cum[1 - a][:, d:, :], cum[a][:, d:, :], cum[a][:, :TILES - d, :], ALU.add))
                        a, d = 1 - a, 2 * d
                    step(dve.tensor_scalar(size[0][:, :], cum[a][:, TILES - 1, :], 1.0 / P, (P - 1.0) / P - 0.5 + 0.5 / P, ALU.mult, ALU.add))
                    step(dve.tensor_copy(whole8[:, :], size[0][:, :]))
                    step(dve.tensor_copy(size[0][:, :], whole8[:, :]))
                    step(dve.tensor_copy(size[2][:, :], size[0][:, :]))
                    b, d = 2, 1
                    while d < EXPERTS:
                        c = 1 if b == 2 else 2
                        dve.tensor_copy(size[c][:, 0:d], size[b][:, 0:d])
                        step(dve.tensor_tensor(size[c][:, d:], size[b][:, d:], size[b][:, :EXPERTS - d], ALU.add))
                        b, d = c, 2 * d
                    ends = size[b]
                    step(dve.memset(tmp[0][:, :], 0.0))
                    for e in range(EXPERTS - 1):
                        step(dve.scalar_tensor_tensor(tmp[0][:, :], cst[:, C_COL:C_COL + COLS], ends[:, e:e + 1], tmp[0][:, :],
                                                      ALU.is_ge, ALU.add))
                    dve.tensor_copy(expert[:, :], tmp[0][:, :])
                    step(dve.tensor_tensor(size[0][:, :], ends[:, :], size[0][:, :], ALU.subtract))
                    step(dve.tensor_scalar(size[0][:, :], size[0][:, :], float(P), None, ALU.mult))
                    step(dve.tensor_tensor(cum[a][:, :, :], cum[a][:, :, :], total, ALU.subtract))
                    step(dve.tensor_tensor(rank[:, :, :], cum[a][:, :, :], banks[4][:, :].rearrange("p (t e) -> p t e", e=EXPERTS), ALU.add))
                    step(dve.tensor_tensor(rank[:, :, :], rank[:, :, :], over(size[0][:, :]), ALU.add))
                    for k in range(2):
                        ins = dve.tensor_tensor(one[k][:, :, :], one[k][:, :, :], rank[:, :, :], ALU.mult)
                    step(ins)
                    for k in range(2):
                        ins = dve.tensor_reduce(slot[:, :, k], one[k][:, :, :], AX.X, ALU.add)
                    step(ins)
                    step(dve.tensor_scalar(slot_hi[:, :, :], slot[:, :, :], 1.0 / P, 0.5 / P - 0.5, ALU.mult, ALU.add))
                    step(dve.tensor_copy(slot_i[:, :, :], slot_hi[:, :, :]))
                    step(dve.tensor_copy(slot_hi[:, :, :], slot_i[:, :, :]))
                    step(dve.scalar_tensor_tensor(slot[:, :, :], slot_hi[:, :, :], -float(P), slot[:, :, :], ALU.mult, ALU.add))
                    lo = slot[:, :, :].rearrange("p t k -> p (t k)")
                    hi = slot_hi[:, :, :].rearrange("p t k -> p (t k)")
                    dve.sem_inc(S["hot_used"].sem, RING)
                    with dve.Fori(0, 2 * TILES // RING) as i:
                        for r in range(RING):
                            w(dve, "hot_used", i, r + 1)
                            q = i * RING + r
                            dve.tensor_scalar(is_lo[r][:, :], cst[:, C_COL:C_COL + P], lo[:, bass.ds(q, 1)], None, ALU.is_equal)
                            dve.tensor_scalar(is_hi[r][:, :], cst[:, C_COL:C_COL + COLS], hi[:, bass.ds(q, 1)], cst[:, bass.ds(C_NAME + q, 1)],
                                              ALU.is_equal, ALU.mult).then_inc(S["hot"].sem, 1)
                    dve.wait_ge(S["hot_used"].sem, S["hot_used"].at(2 * TILES // RING, RING))
                    step(dve.tensor_copy(tab[:, :], banks[6][:, 0:COLS]))
                    step(dve.tensor_scalar(tmp[0][:, :], tab[:, :], TOK + P - 0.5, -float(TOK), ALU.is_gt, ALU.mult))
                    step(dve.tensor_tensor(tmp[0][:, :], tmp[0][:, :], tab[:, :], ALU.add))
                    dve.tensor_scalar(to_load[:, :], tmp[0][:, :], -float(P), 0.0, ALU.add, ALU.max)
                    step(dve.scalar_tensor_tensor(tmp[1][:, :], tab[:, :], 0.5, cst[:, C_SPARE:C_SPARE + COLS], ALU.is_lt, ALU.mult))
                    step(dve.tensor_tensor(tmp[1][:, :], tmp[1][:, :], tab[:, :], ALU.add))
                    step(dve.tensor_scalar(to_store[:, :], tmp[1][:, :], float((ER - 1) * P), None, ALU.add))

        with ExitStack() as ph:
            R = ER
            LEAD, LATE = 8, 2
            xg = [sb(f"xg{r}", [P, P], scope=ph) for r in range(R)]
            lidx = [sb(f"lidx{r}", [P, 1], mybir.dt.uint32, scope=ph) for r in range(R)]
            sidx = [sb(f"sidx{r}", [P, 1], mybir.dt.uint32, scope=ph) for r in range(R)]
            xh = [sb(f"xh{r}", [P, P], F32R, scope=ph) for r in range(2)]
            xl = [sb(f"xl{r}", [P, P], F32R, scope=ph) for r in range(2)]
            sl = [sb(f"sl{r}", [P, HIDP], scope=ph) for r in range(2)]
            hm = [sb(f"hm{r}", [P, HIDP], scope=ph) for r in range(2)]
            hmt = [sb(f"hmt{r}", [P, len(HT), P], scope=ph) for r in range(2)]
            yt = [sb(f"yt{r}", [P, P], scope=ph) for r in range(R)]
            S = {name: Signal(sem("e_" + name, ph), R) for name in
                 ("x_turned", "x_high", "x_low", "h1", "h3", "silu", "silu_used", "h_ready", "h_turned", "ht_ready", "y", "y_ready", "y_free",
                  "row_picked", "place_picked")}
            gathered = [sem(f"gathered{r}", ph) for r in range(R)]
            scattered = [sem(f"scattered{r}", ph) for r in range(R)]
            issued = sem("issued", ph)
            xb, hb, yb = banks[0], banks[1], banks[2:4]
            h1b, h3b = banks[4:6], banks[6:8]

            def w(eng, name, n):
                eng.wait_ge(S[name].sem, n + 1)

            with nc.Block() as block:
                @block.gpsimd
                def _(pool):
                    def fetch(n, r):
                        w(pool, "row_picked", n)
                        pool.sem_inc(issued, 1)
                        pool.indirect_dma_start(xg[r][:, :], None, normed, bass.IndirectOffsetOnAxis(lidx[r][:, :], 0)
                                                ).then_inc(gathered[r], 16)

                    def scatter(i, s, has_free=True):
                        n = i * R + s - LATE
                        r = (s - LATE) % R
                        if has_free:
                            f = s - LATE - 3
                            pool.wait_ge(scattered[f % R], 16 * (i + f // R + 1))
                            pool.sem_inc(S["y_free"].sem, 1)
                        w(pool, "place_picked", n)
                        w(pool, "y_ready", n)
                        pool.sem_inc(issued, 1)
                        pool.indirect_dma_start(mixed, bass.IndirectOffsetOnAxis(sidx[r][:, :], 0), yt[r][:, :], None
                                                ).then_inc(scattered[r], 16)

                    def turn(i, s):
                        n = i * R + s
                        if not isinstance(n, int) or n >= LATE:
                            scatter(i, s, not isinstance(n, int) or n >= LATE + 3)
                        fetch(n + LEAD, (s + LEAD) % R)

                    pool.sem_inc(S["y_free"].sem, R)
                    for n in range(LEAD):
                        fetch(n, n % R)
                    for s in range(R):
                        turn(0, s)
                    with pool.Fori(1, SLOTS // R) as i:
                        for s in range(R):
                            turn(i, s)
                    for s in range(LATE):
                        scatter(SLOTS // R, s)
                    for r in range(R):
                        pool.wait_ge(scattered[r], 16 * (SLOTS // R))
                        pool.wait_ge(gathered[r], 16 * ((SLOTS + LEAD - r + R - 1) // R))

                @block.tensor
                def _(pe):
                    def turn_x(n, r, count):
                        pe.wait_ge(gathered[r], 16 * count)
                        if not (isinstance(n, int) and n == 0):
                            w(pe, "x_low", n - 1)
                        pe.transpose(xb[:, 0:P], xg[r][:, :], ident).then_inc(S["x_turned"].sem, 1)

                    def front(n, e, r, ahead):
                        w(pe, "x_low", n)
                        if ahead:
                            w(pe, "silu", n - 2)
                        o1, o3 = h1b[r % 2][:, 0:HIDP], h3b[r % 2][:, 0:HIDP]
                        for o, wh, wl, name in ((o1, w1H, w1L, "h1"), (o3, w3H, w3L, "h3")):
                            if name == "h3" and ahead:
                                w(pe, "h_ready", n - 2)
                            a = bass.ds(e * HIDP, HIDP)
                            pe.matmul(o, xh[r % 2][:, :], wh[:, a], start=True, stop=False)
                            pe.matmul(o, xl[r % 2][:, :], wh[:, a], start=False, stop=False)
                            pe.matmul(o, xh[r % 2][:, :], wl[:, a], start=False, stop=True).then_inc(S[name].sem, 1)

                    def turn_h(n, r, ahead):
                        w(pe, "h_ready", n)
                        if ahead:
                            w(pe, "ht_ready", n - 1)
                        for k, (a, m) in enumerate(HT):
                            ins = pe.transpose(hb[0:m, k * P:(k + 1) * P], hm[r % 2][:, a:a + m], ident)
                        ins.then_inc(S["h_turned"].sem, 1)

                    def back(n, e, r):
                        w(pe, "ht_ready", n)
                        for k, (a, m) in enumerate(HT):
                            c = bass.ds((e * len(HT) + k) * P, P)
                            ins = pe.matmul(yb[r % 2][:, 0:P], hmt[r % 2][0:m, k, :], w2T[0:m, c], start=(k == 0), stop=(k == len(HT) - 1))
                        ins.then_inc(S["y"].sem, 1)

                    def expert_of(n):
                        col_ = expert[0:1, n:n + 1] if isinstance(n, int) else expert[0:1, bass.ds(n, 1)]
                        return pe.value_load(col_, min_val=0, max_val=EXPERTS - 1)

                    turn_x(0, 0, 1)
                    turn_x(1, 1, 1)
                    turn_x(2, 2, 1)
                    front(0, expert_of(0), 0, False)
                    front(1, expert_of(1), 1, False)
                    turn_h(0, 0, False)
                    with pe.Fori(0, SLOTS // R) as i:
                        _, e = nc.values_load_multi_w_load_instructions(expert[0:1, bass.ds(i * R, R + 2)], [mybir.EngineType.PE],
                                                                        min_val=0, max_val=EXPERTS - 1)
                        for s in range(R):
                            n = i * R + s
                            turn_x(n + 3, (s + 3) % R, i + 1 + (s + 3) // R)
                            front(n + 2, e[s + 2], s + 2, True)
                            turn_h(n + 1, s + 1, True)
                            back(n, e[s], s)

                @block.scalar
                def _(act):
                    def split_x(n, r):
                        w(act, "x_turned", n)
                        act.activation(xh[r % 2][:, :], xb[:, 0:P], ACT.Copy).then_inc(S["x_high"].sem, 1)

                    def silu(n, r):
                        w(act, "h1", n)
                        act.activation(sl[r % 2][:, :], h1b[r % 2][:, 0:HIDP], ACT.Silu).then_inc(S["silu"].sem, 1)

                    act.preload_act_table(ACT.Silu)
                    split_x(0, 0)
                    split_x(1, 1)
                    act.wait_ge(S["h3"].sem, 1)
                    split_x(2, 2)
                    silu(0, 0)
                    silu(1, 1)
                    with act.Fori(0, SLOTS // R) as i:
                        for s in range(R):
                            n = i * R + s
                            act.wait_ge(S["h3"].sem, n + 2)
                            split_x(n + 3, s + 3)
                            w(act, "h_ready", n)
                            silu(n + 2, s + 2)
                            w(act, "y", n)
                            w(act, "y_free", n)
                            act.activation(yt[s][:, :], yb[s % 2][:, 0:P], ACT.Copy).then_inc(S["y_ready"].sem, 1)

                @block.vector
                def _(dve):
                    def split_x(n, r):
                        w(dve, "x_high", n)
                        dve.tensor_tensor(xl[r % 2][:, :], xb[:, 0:P], xh[r % 2][:, :].bitcast(F32), ALU.subtract).then_inc(S["x_low"].sem, 1)

                    def gate_h(n, r):
                        w(dve, "silu", n)
                        w(dve, "h3", n)
                        dve.tensor_tensor(hm[r % 2][:, :], h3b[r % 2][:, 0:HIDP], sl[r % 2][:, :], ALU.mult).then_inc(S["h_ready"].sem, 1)

                    def keep_h(n, r):
                        w(dve, "h_turned", n)
                        dve.tensor_copy(hmt[r % 2][:, 0:2, :], hb[:, 0:2 * P].rearrange("p (k c) -> p k c", c=P))
                        dve.tensor_copy(hmt[r % 2][0:HT[2][1], 2, :], hb[0:HT[2][1], 2 * P:3 * P]).then_inc(S["ht_ready"].sem, 1)

                    def pick_rows(n, r):
                        dve.tensor_copy(lidx[r][:, :], to_load[:, bass.ds(n, 1)]).then_inc(S["row_picked"].sem, 1)

                    for n in range(LEAD):
                        pick_rows(n, n)
                    split_x(0, 0)
                    split_x(1, 1)
                    split_x(2, 2)
                    gate_h(0, 0)
                    gate_h(1, 1)
                    keep_h(0, 0)
                    with dve.Fori(0, SLOTS // R) as i:
                        for s in range(R):
                            n = i * R + s
                            split_x(n + 3, s + 3)
                            w(dve, "h_turned", n)
                            gate_h(n + 2, s + 2)
                            keep_h(n + 1, s + 1)
                            pick_rows(n + LEAD, (s + LEAD) % R)
                            w(dve, "y_free", n)
                            dve.tensor_copy(sidx[s][:, :], to_store[:, bass.ds(n, 1)]).then_inc(S["place_picked"].sem, 1)

        with ExitStack() as ph:
            R, CHUNKS = 4, TOK // CHUNK
            y = [sb(f"y{r}", [P, 2, CT, P], scope=ph) for r in range(R)]
            arrived = [sem(f"arrived{r}", ph) for r in range(R)]
            stored = [sem(f"stored{r}", ph) for r in range(R)]
            scaled, first, both = sem("scaled", ph), sem("first", ph), sem("both", ph)
            mixed_t = mixed.rearrange("(n p) c -> p n c", p=P)
            with nc.Block() as block:
                @block.sync
                def _(sp):
                    for c in range(CHUNKS):
                        if c >= R:
                            sp.wait_ge(both, c - R + 1)
                        for k in range(2):
                            a = ER + k * TILES + c * CT
                            sp.dma_start(y[c % R][:, k, :, :], mixed_t[:, a:a + CT, :]).then_inc(arrived[c % R], 16)

                @block.scalar
                def _(act):
                    def store(c):
                        act.wait_ge(both, c + 1)
                        act.dma_start(out_t[:, c * CT:(c + 1) * CT, :], tok[:, c * CT:(c + 1) * CT, :]).then_inc(stored[c % R], 16)

                    for c in range(CHUNKS):
                        r = c % R
                        act.wait_ge(arrived[r], 32 * (c // R + 1))
                        for j in range(CT):
                            ins = act.activation(y[r][:, 1, j, :], y[r][:, 1, j, :], ACT.Identity, scale=gates[:, c * CT + j, 1:2])
                        ins.then_inc(scaled, 1)
                        if c >= 2:
                            store(c - 2)
                    for c in (CHUNKS - 2, CHUNKS - 1):
                        store(c)
                    for r in range(R):
                        act.wait_ge(stored[r], 16 * (CHUNKS // R))

                @block.vector
                def _(dve):
                    for c in range(CHUNKS):
                        r = c % R
                        dve.wait_ge(arrived[r], 32 * (c // R + 1))
                        for j in range(CT):
                            t = c * CT + j
                            ins = dve.scalar_tensor_tensor(tok[:, t, :], y[r][:, 0, j, :], gates[:, t, 0:1], tok[:, t, :],
                                                           ALU.mult, ALU.add)
                        ins.then_inc(first, 1)

                @block.gpsimd
                def _(pool):
                    for c in range(CHUNKS):
                        pool.wait_ge(first, c + 1)
                        pool.wait_ge(scaled, c + 1)
                        t1 = tok[:, c * CT:(c + 1) * CT, :]
                        pool.tensor_tensor(t1, t1, y[c % R][:, 1, :, :], ALU.add).then_inc(both, 1)


_INPUTS = ["x", "L0_conv_W1", "L0_conv_b1", "L0_conv_W2", "L0_conv_b2", "L1_attn_norm1_g", "L1_attn_norm1_b",
           "L1_attn_Wq", "L1_attn_Wkv", "L1_attn_Wproj", "L1_attn_bproj", "L1_attn_norm2_g", "L1_attn_norm2_b",
           "L1_attn_W1", "L1_attn_b1", "L1_attn_W2", "L1_attn_b2", "L1_ffn_router_w", "L1_ffn_w1", "L1_ffn_w2", "L1_ffn_w3"]


def kernel(**inputs):
    import concourse.bacc as _bacc
    from concourse.bass_utils import run_bass_kernel_spmd as _run

    nc = _bacc.Bacc("TRN2", target_bir_lowering=False, num_devices=1)
    arrays, args = {}, []
    for name in _INPUTS:
        a = np.ascontiguousarray(inputs[name])
        arrays[f"in_{name}"] = a
        args.append(nc.dram_tensor(f"in_{name}", a.shape, mybir.dt.from_np(a.dtype), kind="ExternalInput").ap())
    arrays["in_consts"] = constants()
    args.append(nc.dram_tensor("in_consts", (P, C_ALL), F32, kind="ExternalInput").ap())
    args.append(nc.dram_tensor("normed", (TOK, P), F32, kind="Internal").ap())
    args.append(nc.dram_tensor("mixed", (ER * P + 2 * TOK, P), F32, kind="Internal").ap())
    args.append(nc.dram_tensor("out", (BATCH, SIDE, SIDE, P), F32, kind="ExternalOutput").ap())
    conv_attn_moe(nc, *args)
    r = _run(nc, [arrays], core_ids=[0])
    return r.results[0]["out"]
```

```python
from contextlib import ExitStack

import numpy as np

import concourse.bass as bass
from concourse import mybir

F32 = mybir.dt.float32
F32R = mybir.dt.float32r
ALU = mybir.AluOpType
ACT = mybir.ActivationFunctionType
AX = mybir.AxisListType

P = 128
BATCH, SIDE = 8, 32
PIX = SIDE * SIDE
TOK = BATCH * PIX
TILES = TOK // P
BT = PIX // P
CHUNK = 512
CT = CHUNK // P
TAPS, GROUPS, GCH = 9, 8, 16
RED = P // 4
HEADS, HD, WIN = 8, 16, 32
SPAN = P + 2 * WIN
MLP = 512
EXPERTS, HID = 8, 341
HT = [(k * P, min(P, HID - k * P)) for k in range((HID + P - 1) // P)]
HTP = HT[:-1] + [(HT[-1][0], HT[-1][1] + HID % 2)]
PADI = SIDE + 2
NEG = -1.0e30

C_ID, C_GN, C_HEAD, C_MASK = 0, P, 2 * P, 3 * P
C_HI, C_LO = C_MASK + 3 * SPAN, C_MASK + 3 * SPAN + 1
C_IOTA = C_LO + 1
C_UPPER = C_IOTA + EXPERTS
C_ONES = C_UPPER + P
COLS = 144
C_COL = C_ONES + P
C_NAME = C_COL + COLS
C_SPARE = C_NAME + 2 * TILES
C_END = C_SPARE + COLS
C_ALL = C_END + TAPS * P
ER = 8
SLOTS = 2 * TILES + EXPERTS
HIDP = HID + HID % 2


def constants():
    c = np.zeros((P, C_ALL), np.float32)
    p = np.arange(P)
    c[p, C_ID + p] = 1.0
    c[:, C_GN:C_GN + P] = (p[:, None] // 4 == p[None, :] // 4) * 0.25
    for t in range(TAPS):
        c[p, C_END + t * P + (t * P + p) // TAPS] = 1.0
    head = p // HD
    c[:, C_HEAD:C_HEAD + P] = (head[:, None] == head[None, :]) & (head[:, None] > 0)
    key = np.arange(SPAN)[None, :] // WIN
    query = p[:, None] // WIN
    near = (key >= query) & (key <= query + 2)
    for n, inside in enumerate((key >= 1, key >= 0, key < SPAN // WIN - 1)):
        c[:, C_MASK + n * SPAN:C_MASK + (n + 1) * SPAN] = np.where(near & inside, 0.0, NEG)
    c[:, C_HI] = (p < 2 * RED) | (p == 3 * RED)
    c[:, C_LO] = ((p >= 2 * RED) & (p < 3 * RED)) | (p == 3 * RED + 1)
    c[:, C_IOTA:C_IOTA + EXPERTS] = np.arange(EXPERTS)[None, :]
    c[:, C_UPPER:C_UPPER + P] = p[:, None] < p[None, :]
    c[:, C_ONES:C_ONES + P] = 1.0
    c[:, C_COL:C_COL + COLS] = np.arange(COLS)
    tile, choice = np.divmod(np.arange(2 * TILES), 2)
    c[:, C_NAME:C_NAME + 2 * TILES] = P * (1 + TILES * choice + tile)[None, :] + p[:, None]
    c[:, C_SPARE:C_SPARE + COLS] = (np.arange(COLS) % ER - (ER - 1))[None, :] * P + p[:, None]
    return c


class Signal:

    def __init__(self, sem, each):
        self.sem, self.each = sem, each

    def at(self, i, n):
        return i * self.each + n


def conv_attn_moe(nc, x, w_red, b_red, w_tap, b_tap, n1g, n1b, wq, wkv, wproj, bproj,
                  n2g, n2b, w_up, b_up, w_down, b_down, router, w1, w2, w3, consts, normed, mixed, out):
    x_t = x.rearrange("b h w c -> (b h w) c").rearrange("(n p) c -> p n c", p=P)
    normed_t = normed.rearrange("(n p) c -> p n c", p=P)
    out_t = out.rearrange("b h w c -> (b h w) c").rearrange("(n p) c -> p n c", p=P)

    with ExitStack() as ctx:
        def sb(name, shape, dt=F32, scope=ctx):
            return scope.enter_context(nc.sbuf_tensor(name, shape, dt))

        def ps(name, shape, scope=ctx):
            return scope.enter_context(nc.psum_tensor(name, shape, F32))

        def sem(name, scope=ctx):
            return scope.enter_context(nc.semaphore(name))

        cst = sb("cst", [P, C_END])
        ident = cst[:, C_ID:C_ID + P]
        eps5 = sb("eps5", [P, 1])
        tok = sb("tok", [P, TILES, P])
        res = sb("res", [P, TILES, P])
        bst = sb("bst", [P, TILES, 6])
        sc_a = sb("sc_a", [P, TILES])
        sc_b = sb("sc_b", [P, TILES])
        sc_c = sb("sc_c", [P, TILES])
        sc_d = sb("sc_d", [P, TILES])
        col = sb("col", [P, 12])
        N1G, N1B, N2G, N2B, BRED, BUP = 0, 1, 2, 3, 4, 5
        bproj_row = sb("bproj_row", [P, P])
        bdown_row = sb("bdown_row", [P, P])
        w_redT = sb("w_redT", [P, 3 * RED])
        w_taps = sb("w_taps", [P, TAPS * P], F32R)
        wqkvT = sb("wqkvT", [P, 2 * P])
        wkeyT = sb("wkeyT", [P, P])
        wprojT = sb("wprojT", [P, P])
        upH = sb("upH", [P, MLP], F32R)
        upL = sb("upL", [P, MLP], F32R)
        downT = sb("downT", [P, CT, P])
        routerT = sb("routerT", [P, EXPERTS])
        w1H, w1L, w3H, w3L = [sb(n, [P, EXPERTS * HIDP], F32R) for n in ("w1H", "w1L", "w3H", "w3L")]
        w2T = sb("w2T", [P, EXPERTS * len(HT) * P])
        w2v = w2T[:, :].rearrange("p (e k c) -> p e k c", e=EXPERTS, c=P)
        banks = [ps(f"bank{n}", [P, CHUNK]) for n in range(8)]

        with ExitStack() as ph:
            rawq = sb("rawq", [P, 3, P], scope=ph)
            rawu = sb("rawu", [P, CT, P], scope=ph)
            rawd = sb("rawd", [P, MLP], scope=ph)
            rawr = sb("rawr", [EXPERTS, P], scope=ph)
            rawt = sb("rawt", [P, TAPS * GROUPS], scope=ph)
            hi_t = sb("hi_t", [P, TAPS * GROUPS], F32R, scope=ph)
            lo_t = sb("lo_t", [P, TAPS * GROUPS], F32, scope=ph)
            cleared = sem("cleared", ph)
            loaded = sem("loaded", ph)
            turned = sem("turned", ph)
            high = sem("high", ph)
            emptied = sem("emptied", ph)
            tap_step = sem("tap_step", ph)
            vec_done = sem("vec_done", ph)
            groups = []
            groups.append(([(rawq[:, k, :], P, P, k * P) for k in range(3)],
                           [((P, 0, 2 * P), wqkvT[:, :], None), ((P, 2 * P, 3 * P), wprojT[:, :], None),
                            ((P, 0, HD), wkeyT[:, 0:HD], None), ((P, P + HD, 2 * P), wkeyT[:, HD:P], None)]))
            groups.append(([(rawu[:, k, :], P, P, k * P) for k in range(CT)],
                           [((P, 0, MLP), upH[:, :], upL[:, :])]))
            groups.append(([(rawd[:, k * P:(k + 1) * P], P, P, k * P) for k in range(CT)],
                           [((P, 0, 2 * P), downT[:, 0:2, :], None), ((P, 2 * P, MLP), downT[:, 2:, :], None)]))
            groups.append(([(rawr[:, :], EXPERTS, P, 0)], [((P, 0, EXPERTS // 2), routerT[:, 0:EXPERTS // 2], None),
                                                           ((P, EXPERTS // 2, EXPERTS), routerT[:, EXPERTS // 2:], None)]))

            with nc.Block() as block:
                @block.sync
                def _(sp):
                    sp.dma_start(cst[:, :], consts[:, 0:C_END]).then_inc(loaded, 16)
                    for k, w in enumerate((wq, wkv, wproj)):
                        sp.dma_start(rawq[:, k, :], w).then_inc(loaded, 16)
                    sp.dma_start(rawu[:, :, :], w_up.rearrange("(k p) c -> p k c", p=P)).then_inc(loaded, 16)
                    sp.dma_start(rawd[:, :], w_down).then_inc(loaded, 16)
                    sp.dma_start(rawr[:, :], router).then_inc(loaded, 16)

                @block.scalar
                def _(act):
                    with nc.allow_non_contiguous_dma(reason="vectors with one value per partition"):
                        for n, v in ((N1G, n1g), (N1B, n1b), (N2G, n2g), (N2B, n2b)):
                            act.dma_start(col[:, n:n + 1], v.rearrange("(p a) -> p a", a=1)).then_inc(loaded, 16)
                        for k in range(3):
                            act.dma_start(col[k * RED:(k + 1) * RED, BRED:BRED + 1], b_red.rearrange("(p a) -> p a", a=1)).then_inc(loaded, 16)
                        act.dma_start(col[:, BUP:BUP + CT], b_up.rearrange("(k p) -> p k", p=P)).then_inc(loaded, 16)
                    act.dma_start(bproj_row[:, :], bproj.rearrange("(a c) -> a c", a=1).to_broadcast([P, P])).then_inc(loaded, 16)
                    act.dma_start(bdown_row[:, :], b_down.rearrange("(a c) -> a c", a=1).to_broadcast([P, P])).then_inc(loaded, 16)
                    for k in range(3):
                        act.dma_start(w_redT[:, k * RED:(k + 1) * RED], w_red).then_inc(loaded, 16)
                    act.wait_ge(cleared, 1)
                    for k in range(3):
                        act.dma_start(rawt[k * RED:(k + 1) * RED, :], w_tap).then_inc(loaded, 16)
                    for k in range(2):
                        act.dma_start(rawt[3 * RED + k:3 * RED + k + 1, :], b_tap.rearrange("(a e) -> a e", a=1)).then_inc(loaded, 16)
                    for g, (_, pieces) in enumerate(groups):
                        act.wait_ge(turned, g + 1)
                        for (rows, a, b), dst, low in pieces[:None if pieces[-1][2] is not None else -1]:
                            ins = nc.scalar.activation(dst, banks[g % 8][0:rows, a:b] if len(dst.shape) == 2 else
                                                       banks[g % 8][0:rows, a:b].rearrange("p (k c) -> p k c", c=P), ACT.Copy)
                        ins.then_inc(high, 1)

                n_loads = 1 + 3 + 3 + 4 + 3 + 1 + 2 + 3 + 3 + 2

                @block.tensor
                def _(pe):
                    pe.wait_ge(loaded, 16 * n_loads)
                    for g, (turns, pieces) in enumerate(groups):
                        if g >= 8:
                            pe.wait_ge(emptied, g - 7)
                        for src, rows, cols, at in turns:
                            ins = pe.transpose(banks[g % 8][0:cols, at:at + rows], src, ident[0:rows, 0:rows])
                        ins.then_inc(turned, 1)

                @block.vector
                def _(dve):
                    dve.memset(rawt[:, :], 0.0).then_inc(cleared, 1)
                    dve.memset(eps5[:, :], 1e-5)
                    dve.wait_ge(loaded, 16 * n_loads)
                    dve.tensor_copy(hi_t[:, :], rawt[:, :]).then_inc(tap_step, 1)
                    dve.wait_ge(tap_step, 1)
                    dve.tensor_tensor(lo_t[:, :], rawt[:, :], hi_t[:, :].bitcast(F32), ALU.subtract).then_inc(tap_step, 1)
                    dve.wait_ge(tap_step, 2)
                    dve.tensor_scalar(lo_t[:, :], lo_t[:, :], cst[:, C_LO:C_LO + 1], None, ALU.mult).then_inc(tap_step, 1)
                    dve.wait_ge(tap_step, 3)
                    dve.scalar_tensor_tensor(rawt[:, :], hi_t[:, :].bitcast(F32), cst[:, C_HI:C_HI + 1], lo_t[:, :],
                                             ALU.mult, ALU.add).then_inc(tap_step, 1)
                    dve.wait_ge(tap_step, 4)
                    dve.tensor_copy(w_taps[:, :].rearrange("p (g c k) -> p g c k", g=GROUPS, k=TAPS),
                                    rawt[:, :].rearrange("p (g a k) -> p g a k", g=GROUPS, a=1)
                                    .to_broadcast([P, GROUPS, GCH, TAPS]))
                    for g, (_, pieces) in enumerate(groups):
                        dve.wait_ge(high, g + 1)
                        (rows, a, b), dst, low = pieces[-1]
                        src = banks[g % 8][0:rows, a:b]
                        if len(dst.shape) == 3:
                            src = src.rearrange("p (k c) -> p k c", c=P)
                        if low is not None:
                            dve.tensor_tensor(low, src, dst.bitcast(F32), ALU.subtract).then_inc(emptied, 1)
                        else:
                            dve.tensor_copy(dst, src).then_inc(emptied, 1)

        with ExitStack() as ph:
            HALF = 2
            STEPS = HALF * TAPS
            stage = [sb(f"stage{s}", [P, BT, P], scope=ph) for s in range(2)]
            norm = [sb(f"norm{s}", [P, PADI, PADI], scope=ph) for s in range(2)]
            redu = [[sb(f"redu{s}{h}", [P, CHUNK], F32R, scope=ph) for h in range(HALF)] for s in range(2)]
            PR, TR, LAG = 6, 2, 5
            high_ = [sb(f"high{s}", [P, CHUNK], F32R, scope=ph) for s in range(PR)]
            low_ = [sb(f"low{s}", [P, CHUNK], F32R, scope=ph) for s in range(PR)]
            whole = [g in (7, 13) for g in range(STEPS)]
            SPLIT = STEPS - sum(whole)
            nth_split = [sum(not w_ for w_ in whole[:g]) for g in range(STEPS)]
            sel = res[:, 0:TAPS, :]
            conv_cm = [res[:, TAPS + h * CT:TAPS + (h + 1) * CT, :].rearrange("p j c -> p (j c)") for h in range(HALF)]
            at = TAPS + HALF * CT
            prod = [res[:, at + r * CT:at + (r + 1) * CT, :].rearrange("p j c -> p (j c)") for r in range(PR)]
            sel_r = sb("sel_r", [P, TAPS * P], F32R, scope=ph)
            bnst = sb("bnst", [P, HALF, 6], scope=ph)
            cstat = sb("cstat", [P, 1], scope=ph)
            dev4 = sb("dev4", [P, HALF, 2], scope=ph)
            gmean = sb("gmean", [P, 1], scope=ph)
            cvar = sb("cvar", [P, 1], scope=ph)
            gvar = sb("gvar", [P, 1], scope=ph)
            gsd = sb("gsd", [P, 1], scope=ph)
            grstd = sb("grstd", [P, 1], scope=ph)
            gshift = sb("gshift", [P, 1], scope=ph)
            S = {name: sem("c_" + name, ph) for name in
                 ("bordered", "x_kept", "x_turned", "cmean", "cvar", "gmean", "gvar", "gsd_set", "gsd", "chain", "gvec", "normed",
                  "reduced", "redu_high", "redu_ready", "taps", "products", "highs", "lows", "prod_used",
                  "conv_kept", "conv_turned", "t0", "sel_loaded", "sel_ready")}
            x_loaded = [sem(f"x_loaded{s}", ph) for s in range(2)]
            T0_AT = (1, LAG + 5)
            CHAIN = 6

            def w(eng, name, count):
                if not isinstance(count, int) or count > 0:
                    eng.wait_ge(S[name], count)

            def images(eng, step):
                for n in (-1, 0):
                    step(n, n % 2, lambda d: 0 <= n + d)
                with eng.Fori(0, (BATCH - 2) // 2) as i:
                    for s in range(2):
                        step(i * 2 + s + 1, 1 - s, lambda d: True)
                for n in (BATCH - 1, BATCH):
                    step(n, n % 2, lambda d: n + d < BATCH)

            xcm, tapb, convb, backb, misc = banks[0:2], banks[2:4], banks[4:6], banks[6], banks[7]
            with nc.Block() as block:
                @block.sync
                def _(sp):
                    sp.dma_start(sel, consts[:, C_END:C_ALL].rearrange("p (t c) -> p t c", c=P)).then_inc(S["sel_loaded"], 16)
                    for b in range(BATCH):
                        if b >= 2:
                            sp.wait_ge(S["x_turned"], b - 1)
                            sp.wait_ge(S["x_kept"], b - 1)
                        sp.dma_start(stage[b % 2][:, :, :], x_t[:, b * BT:(b + 1) * BT, :]).then_inc(x_loaded[b % 2], 16)

                @block.tensor
                def _(pe):
                    def step(n, s, has):
                        def sums(n, s, g):
                            h, t = divmod(g, TAPS)
                            if whole[g]:
                                w(pe, "products", n * STEPS + g + 1)
                            else:
                                w(pe, "lows", n * SPLIT + nth_split[g] + 1)
                            if t == 0:
                                w(pe, "conv_kept", HALF * (n - 1) + h + 1)
                            select, r = sel_r[:, t * P:(t + 1) * P], g % PR
                            if whole[g]:
                                ins = pe.matmul(convb[h][:, :], select.bitcast(F32), prod[r], start=(t == 0), stop=(t == TAPS - 1))
                            else:
                                pe.matmul(convb[h][:, :], select, high_[r][:, :], start=(t == 0), stop=False)
                                ins = pe.matmul(convb[h][:, :], select, low_[r][:, :], start=False, stop=(t == TAPS - 1))
                            ins.then_inc(S["prod_used"], 1)

                        def turn_back(n, h):
                            w(pe, "conv_kept", HALF * n + h + 1)
                            w(pe, "t0", HALF * n + h)
                            for j in range(CT):
                                ins = pe.transpose(backb[:, j * P:(j + 1) * P], conv_cm[h][:, j * P:(j + 1) * P], ident)
                            ins.then_inc(S["conv_turned"], 1)

                        def turn():
                            pe.wait_ge(x_loaded[1 - s], (n + s) * 8 + 16)
                            w(pe, "redu_ready", HALF * (n + 1))
                            for h in range(HALF):
                                for j in range(CT):
                                    ins = pe.transpose(xcm[h][:, j * P:(j + 1) * P], stage[1 - s][:, h * CT + j, :], ident)
                            ins.then_inc(S["x_turned"], 1)

                        def average(of, value, result):
                            w(pe, of, n + 2)
                            pe.matmul(misc[:, 0:1], cst[:, C_GN:C_GN + P], value[:, :], start=True, stop=True).then_inc(S[result], 1)

                        def reduce(h):
                            w(pe, "normed", HALF * (n + 2))
                            pe.matmul(xcm[h][0:3 * RED, :], w_redT[:, :], norm[1 - s][:, 1 + 16 * h:17 + 16 * h, 1:1 + SIDE],
                                      start=True, stop=True).then_inc(S["reduced"], 1)

                        norm_parts = {0: turn, 4: lambda: average("cmean", cstat, "gmean"),
                                      7: lambda: average("cvar", cvar, "gvar"),
                                      13: lambda: reduce(0), 14: lambda: reduce(1)}
                        for g in range(STEPS):
                            if has(0):
                                w(pe, "redu_ready", HALF * n + g // TAPS + 1)
                                w(pe, "products", n * STEPS + g - TR + 1)
                                t = g % TAPS
                                pe.matmul(tapb[g % TR][:, :], w_taps[:, t * P:(t + 1) * P], redu[s][g // TAPS][:, :],
                                          start=True, stop=True).then_inc(S["taps"], 1)
                            if has(1) and g in norm_parts:
                                norm_parts[g]()
                            if g >= LAG and has(0):
                                sums(n, s, g - LAG)
                            elif g < LAG and has(-1):
                                sums(n - 1, 1 - s, STEPS + g - LAG)
                            if g == TAPS - 1 + LAG + 2 and has(0):
                                turn_back(n, 0)
                            if g == LAG + 1 and has(-1):
                                turn_back(n - 1, 1)
                    pe.wait_ge(S["sel_ready"], 1)
                    images(pe, step)

                @block.scalar
                def _(act):
                    act.preload_act_table(ACT.Sqrt)

                    def step(n, s, has):
                        def keep_x():
                            act.wait_ge(x_loaded[1 - s], (n + s) * 8 + 16)
                            act.activation(tok[:, bass.ds((n + 1) * BT, BT), :], stage[1 - s][:, :, :], ACT.Copy).then_inc(S["x_kept"], 1)

                        def deviation():
                            w(act, "gsd_set", n + 2)
                            act.activation(gsd[:, :], gvar[:, :], ACT.Sqrt, bias=eps5[:, 0:1]).then_inc(S["gsd"], 1)

                        def normalise(h):
                            w(act, "gvec", n + 2)
                            act.activation(norm[1 - s][:, 1 + 16 * h:17 + 16 * h, 1:1 + SIDE],
                                           xcm[h][:, :].rearrange("p (h w) -> p h w", w=SIDE), ACT.Identity,
                                           bias=gshift[:, 0:1], scale=grstd[:, 0:1]).then_inc(S["normed"], 1)

                        def reduced_high(h):
                            w(act, "reduced", HALF * (n + 1) + h + 1)
                            act.activation(redu[1 - s][h][0:3 * RED, :], xcm[h][0:3 * RED, :], ACT.Identity,
                                           bias=col[0:3 * RED, BRED:BRED + 1]).then_inc(S["redu_high"], 1)

                        def keep_conv(n, h):
                            w(act, "prod_used", n * STEPS + (h + 1) * TAPS)
                            w(act, "conv_turned", HALF * (n - 1) + h + 1)
                            act.activation(conv_cm[h], convb[h][:, :], ACT.Copy).then_inc(S["conv_kept"], 1)

                        norm_parts = {2: keep_x, 7: deviation, 9: lambda: normalise(0), 10: lambda: normalise(1),
                                      13: lambda: reduced_high(0), 14: lambda: reduced_high(1)}
                        for g in range(STEPS):
                            if has(0) and not whole[g]:
                                w(act, "products", n * STEPS + g + 1)
                                w(act, "prod_used", n * STEPS + g - PR + 1)
                                act.activation(high_[g % PR][:, :], prod[g % PR], ACT.Copy).then_inc(S["highs"], 1)
                            if has(1) and g in norm_parts:
                                norm_parts[g]()
                            if g == TAPS - 1 + LAG and has(0):
                                keep_conv(n, 0)
                            if g == LAG - 1 and has(-1):
                                keep_conv(n - 1, 1)
                    act.wait_ge(S["bordered"], 1)
                    images(act, step)

                @block.gpsimd
                def _(pool):
                    def step(n, s, has):
                        for g in range(STEPS):
                            if has(0) and not whole[g]:
                                w(pool, "highs", n * SPLIT + nth_split[g] + 1)
                                pool.tensor_tensor(low_[g % PR][:, :], prod[g % PR], high_[g % PR][:, :].bitcast(F32),
                                                   ALU.subtract).then_inc(S["lows"], 1)
                    images(pool, step)

                @block.vector
                def _(dve):
                    for s in range(2):
                        dve.memset(norm[s][:, :, :], 0.0)
                        for h in range(HALF):
                            dve.memset(redu[s][h][3 * RED:P, :].bitcast(F32), 1.0)
                    dve.drain()
                    dve.sem_inc(S["bordered"], 1)
                    dve.wait_ge(S["sel_loaded"], 16)
                    dve.tensor_copy(sel_r[:, :], sel.rearrange("p t c -> p (t c)")).then_inc(S["sel_ready"], 1)

                    def step(n, s, has):
                        def link(ins):
                            ins.then_inc(S["chain"], 1)

                        def linked(k):
                            w(dve, "chain", CHAIN * (n + 1) + k)

                        def stats():
                            w(dve, "x_turned", n + 2)
                            for h in range(HALF):
                                ins = dve.bn_stats(bnst[:, h, :], xcm[h][:, :])
                            link(ins)

                        def channel_means():
                            linked(1)
                            dve.tensor_reduce(cstat[:, :], bnst[:, :, 1::3], AX.XY, ALU.add).then_inc(S["cmean"], 1)

                        def group_mean():
                            w(dve, "gmean", n + 2)
                            link(dve.tensor_scalar(gmean[:, :], misc[:, 0:1], 0.25, None, ALU.mult))

                        def deviations():
                            linked(2)
                            link(dve.tensor_scalar(dev4[:, :, :], bnst[:, :, 1::3], gmean[:, 0:1], None, ALU.subtract))

                        def squares():
                            linked(3)
                            link(dve.tensor_tensor(dev4[:, :, :], dev4[:, :, :], dev4[:, :, :], ALU.mult))

                        def variances():
                            linked(4)
                            link(dve.scalar_tensor_tensor(dev4[:, :, :], bnst[:, :, 2::3], 2.0 * HALF / PIX, dev4[:, :, :], ALU.mult, ALU.add))

                        def channel_variances():
                            linked(5)
                            dve.tensor_reduce(cvar[:, :], dev4[:, :, :], AX.XY, ALU.add).then_inc(S["cvar"], 1)

                        def group_variance():
                            w(dve, "gvar", n + 2)
                            dve.tensor_scalar(gvar[:, :], misc[:, 0:1], 0.25, None, ALU.mult).then_inc(S["gsd_set"], 1)

                        def scale():
                            w(dve, "gsd", n + 2)
                            w(dve, "normed", HALF * (n + 1))
                            link(dve.reciprocal(grstd[:, :], gsd[:, :]))

                        def shift():
                            linked(6)
                            dve.scalar_tensor_tensor(gshift[:, :], gmean[:, :], -1.0, grstd[:, :], ALU.mult, ALU.mult).then_inc(S["gvec"], 1)

                        def low_part(h):
                            w(dve, "redu_high", HALF * (n + 1) + h + 1)
                            r = slice(RED, 2 * RED)
                            dve.scalar_tensor_tensor(redu[1 - s][h][r, :], xcm[h][r, :], col[r, BRED:BRED + 1],
                                                     redu[1 - s][h][r, :].bitcast(F32), ALU.add, ALU.subtract).then_inc(S["redu_ready"], 1)

                        def t0(n, h):
                            w(dve, "conv_turned", HALF * n + h + 1)
                            tiles = tok[:, bass.ds(n * BT + h * CT, CT), :]
                            dve.tensor_tensor(tiles, backb[:, :].rearrange("p (j c) -> p j c", c=P), tiles, ALU.add).then_inc(S["t0"], 1)

                        def t0_stats(n, h, j):
                            t = n * BT + h * CT + j
                            dve.bn_stats(bst[:, bass.ds(t, 1), :].rearrange("p a k -> p (a k)"),
                                         tok[:, bass.ds(t, 1), :].rearrange("p a c -> p (a c)"))

                        norm_parts = {1: [stats], 2: [channel_means], 5: [group_mean], 6: [deviations, squares, variances, channel_variances],
                                      7: [group_variance], 8: [scale, shift],
                                      15: [lambda: low_part(0)], 16: [lambda: low_part(1)]}
                        for g in range(STEPS + 1):
                            if has(1):
                                for part in norm_parts.get(g, []):
                                    part()
                            if g == T0_AT[0] and has(-1):
                                t0(n - 1, 0)
                            if g == T0_AT[1] and has(-1):
                                t0(n - 1, 1)
                            if g == T0_AT[0] + 1 and has(-1):
                                w(dve, "t0", HALF * n - 1)
                            if g == T0_AT[1] + 1 and has(-1):
                                w(dve, "t0", HALF * n)
                            if has(0) and g < STEPS:
                                h, t = divmod(g, TAPS)
                                w(dve, "taps", n * STEPS + g + 1)
                                w(dve, "prod_used", n * STEPS + g - PR + 1)
                                dy, dx = divmod(t, 3)
                                dve.tensor_tensor(prod[g % PR].rearrange("p (h w) -> p h w", w=SIDE),
                                                  tapb[g % TR][:, :].rearrange("p (h w) -> p h w", w=SIDE),
                                                  norm[s][:, 16 * h + dy:16 * h + dy + 16, dx:dx + SIDE],
                                                  ALU.mult).then_inc(S["products"], 1)
                            if g == T0_AT[0] + 1 and has(-1):
                                for j in range(CT):
                                    t0_stats(n - 1, 0, j)
                            if g == T0_AT[1] + 1 and has(-1):
                                for j in range(CT):
                                    t0_stats(n - 1, 1, j)
                    images(dve, step)
                    dve.drain()

        def norm_scales(first, tag):
            with ExitStack() as ph:
                sd = sb("sd" + tag, [P, TILES], scope=ph)
                v2 = sb("v2" + tag, [P, TILES], scope=ph)
                step, rooted = sem("step" + tag, ph), sem("rooted" + tag, ph)
                mean = sb("mean" + tag, [P, TILES], scope=ph)
                var = sb("var" + tag, [P, TILES], scope=ph)
                half = sb("half" + tag, [P, TILES], scope=ph)
                folded = sem("folded" + tag, ph)
                with nc.Block() as block:
                    @block.scalar
                    def _(act):
                        act.wait_ge(folded, 7)
                        nc.scalar.activation(sd[:, :], var[:, :], ACT.Sqrt, bias=eps5[:, 0:1]).then_inc(rooted, 1)
                        if first:
                            act.wait_ge(step, 4)
                            nc.scalar.activation(sd[:, :], v2[:, :], ACT.Sqrt, bias=eps5[:, 0:1]).then_inc(rooted, 1)

                    @block.vector
                    def _(dve):
                        me, mo = bst[:, :, 1], bst[:, :, 4]
                        fold = [
                            lambda: dve.tensor_tensor(mean[:, :], me, mo, ALU.add),
                            lambda: dve.tensor_tensor(half[:, :], me, mo, ALU.subtract),
                            lambda: dve.tensor_tensor(var[:, :], bst[:, :, 2], bst[:, :, 5], ALU.add),
                            lambda: dve.tensor_scalar(mean[:, :], mean[:, :], 0.5, None, ALU.mult),
                            lambda: dve.scalar_tensor_tensor(half[:, :], half[:, :], 0.25, half[:, :], ALU.mult, ALU.mult),
                            lambda: dve.tensor_scalar(var[:, :], var[:, :], 1.0 / P, None, ALU.mult),
                            lambda: dve.tensor_tensor(var[:, :], var[:, :], half[:, :], ALU.add),
                        ]
                        for n, part in enumerate(fold):
                            part().then_inc(folded, 1)
                            dve.wait_ge(folded, n + 1)
                        dve.wait_ge(rooted, 1)
                        dve.reciprocal(sc_a[:, :], sd[:, :]).then_inc(step, 1)
                        dve.wait_ge(step, 1)
                        dve.scalar_tensor_tensor(sc_b[:, :], mean[:, :], -1.0, sc_a[:, :], ALU.mult, ALU.mult).then_inc(step, 1)
                        if first:
                            dve.tensor_tensor(v2[:, :], var[:, :], sc_a[:, :], ALU.mult).then_inc(step, 1)
                            dve.wait_ge(step, 3)
                            dve.tensor_tensor(v2[:, :], v2[:, :], sc_a[:, :], ALU.mult).then_inc(step, 1)
                            dve.wait_ge(rooted, 2)
                            dve.reciprocal(sc_c[:, :], sd[:, :]).then_inc(step, 1)
                            dve.wait_ge(step, 5)
                            dve.tensor_tensor(sc_c[:, :], sc_c[:, :], sc_a[:, :], ALU.mult).then_inc(step, 1)
                            dve.wait_ge(step, 6)
                            dve.scalar_tensor_tensor(sc_d[:, :], mean[:, :], -1.0, sc_c[:, :], ALU.mult, ALU.mult).then_inc(step, 1)

        norm_scales(True, "_1")

        with ExitStack() as ph:
            ht = [sb(f"ht{s}", [P, BT, P], scope=ph) for s in range(2)]
            hcm = sb("hcm", [P, PIX + 2 * WIN], scope=ph)
            u = [sb(f"u{s}", [P, BT, P], scope=ph) for s in range(2)]
            kvt = sb("kvt", [P, BT, P], scope=ph)
            qs = sb("qs", [P, BT, P], scope=ph)
            qcm = sb("qcm", [P, PIX], scope=ph)
            ek = sb("ek", [P, PIX], scope=ph)
            ekt = sb("ekt", [P, BT, P], scope=ph)
            q0 = sb("q0", [HD, PIX], scope=ph)
            k0 = sb("k0", [HD, PIX + 2 * WIN], scope=ph)
            va = [sb(f"va{s}", [P, BT, HD], scope=ph) for s in range(2)]
            vb = [sb(f"vb{s}", [SPAN - P, BT, HD], scope=ph) for s in range(2)]
            sm = [sb(f"sm{m}", [P, 2, SPAN], scope=ph) for m in range(2)]
            pta = sb("pta", [P, BT, P], scope=ph)
            ptb = sb("ptb", [SPAN - P, BT, P], scope=ph)
            ctxs = sb("ctxs", [P, P], scope=ph)
            acm = res[:, (BATCH - 1) * BT:BATCH * BT, :].rearrange("p j c -> p (j c)")
            qmax = sb("qmax", [P, 4, 2 * HEADS], scope=ph)
            qsum = sb("qsum", [P, BT * HEADS], scope=ph)
            kmax = sb("kmax", [P, 2], scope=ph)
            nkmax = sb("nkmax", [P, 1], scope=ph)
            ksum = sb("ksum", [P, 2], scope=ph)
            kinv = sb("kinv", [P, 1], scope=ph)
            nmax = sb("nmax", [P, BT], scope=ph)
            lsum = sb("lsum", [P, BT], scope=ph)
            linv = sb("linv", [P, BT], scope=ph)
            tbn = sb("rbn", [P, BT, 6], scope=ph)

            ORDER = [(1, "S0"), (1, "S1"), (1, "EKT0"), (1, "EKT1"), (0, "HT0"), (0, "HT1"), (1, "QST0"), (1, "QST1"),
                     (1, "CTX"), (0, "QKV0"), (1, "S2"), (1, "PT0"), (0, "QKV1"), (1, "S3"), (0, "QKV2"), (1, "PT1"),
                     (0, "QKV3"), (0, "KEY0"), (1, "PT2"), (0, "KEY1"), (0, "K00"), (1, "PT3"), (0, "K01"), (0, "V"),
                     (1, "OUT0"), (1, "OUT1"), (1, "Y0"), (1, "Y1")]
            JOBS = [[name for part, name in ORDER if part == which] for which in range(2)]
            BY_ACT = [["HT0", "HT1", "K00", "K01", "KEY0", "KEY1", "V"],
                      ["EKT0", "EKT1", "QST0", "QST1", "PT0", "PT1", "PT2", "PT3", "OUT0", "OUT1"]]
            BY_DVE = [["QKV0", "QKV1", "QKV2", "QKV3"], ["S0", "S1", "CTX", "S2", "S3", "Y0", "Y1"]]
            LINKS = (16, 4)
            S = {name: sem("a_" + name, ph) for name in
                 ("done0", "done1", "act_read0", "act_read1", "dve_read0", "dve_read1", "bordered",
                  "ht_ready", "kv_ready", "kmax_ready", "u_raw", "u_ready", "u_kept", "q_exp", "qs_ready",
                  "s_shift", "s_exp", "s_ready", "stats", "link0", "link1")}

            def w(eng, name, count):
                if not isinstance(count, int) or count > 0:
                    eng.wait_ge(S[name], count)

            def images(eng, step):
                for n in (-2, -1, 0):
                    step(n, n % 2, lambda d: 0 <= n + d)
                with eng.Fori(0, (BATCH - 4) // 2) as i:
                    for s in range(2):
                        step(i * 2 + s + 1, 1 - s, lambda d: True)
                for n in range(BATCH - 3, BATCH + 1):
                    step(n, n % 2, lambda d: 0 <= n + d < BATCH)

            def bank(s, name):
                return banks[(s * len(ORDER) + [k for _, k in ORDER].index(name)) % 8]

            def done(eng, part, image, name):
                w(eng, f"done{part}", len(JOBS[part]) * image + JOBS[part].index(name) + 1)

            def was_read(eng, part, image, name):
                who, order = ("act_read", BY_ACT[part]) if name in BY_ACT[part] else ("dve_read", BY_DVE[part])
                w(eng, f"{who}{part}", len(order) * image + order.index(name) + 1)

            with nc.Block() as block:
                @block.tensor
                def _(pe):
                    def step(n, s, has):
                        next_ = n + 1

                        def turn_h(name, c):
                            w(pe, "ht_ready", 2 * next_ + c + 1)
                            for j in range(CT):
                                ins = pe.transpose(bank(s, name)[:, j * P:(j + 1) * P], ht[1 - s][:, c * CT + j, :], ident)
                            return ins

                        def q_and_kv(name, m):
                            for h in range(2):
                                a = WIN + (2 * m + h) * P
                                ins = pe.matmul(bank(s, name)[:, h * 2 * P:(h + 1) * 2 * P], hcm[:, a:a + P], wqkvT[:, :],
                                                start=True, stop=True)
                            return ins

                        def keys(name, c):
                            a = WIN + c * CHUNK
                            return pe.matmul(bank(s, name)[:, :], wkeyT[:, :], hcm[:, a:a + CHUNK], start=True, stop=True)

                        def first_keys(name, c):
                            a = WIN + c * CHUNK
                            return pe.matmul(bank(s, name)[0:HD, :], wqkvT[:, P:P + HD], hcm[:, a:a + CHUNK], start=True, stop=True)

                        def values(name):
                            for j in range(BT):
                                pe.matmul(bank(s, name)[:, j * 2 * HD:j * 2 * HD + HD], hcm[:, j * P:(j + 1) * P],
                                          wqkvT[:, P:P + HD], start=True, stop=True)
                                ins = pe.matmul(bank(s, name)[0:SPAN - P, j * 2 * HD + HD:(j + 1) * 2 * HD],
                                                hcm[:, (j + 1) * P:j * P + SPAN], wqkvT[:, P:P + HD], start=True, stop=True)
                            return ins

                        def scores(name, m):
                            for h in range(2):
                                j = 2 * m + h
                                ins = pe.matmul(bank(s, name)[:, h * SPAN:(h + 1) * SPAN], q0[:, j * P:(j + 1) * P],
                                                k0[:, j * P:j * P + SPAN], start=True, stop=True)
                            return ins

                        def turn_k(name, c):
                            for j in range(CT):
                                a = (c * CT + j) * P
                                ins = pe.transpose(bank(s, name)[:, j * P:(j + 1) * P], ek[:, a:a + P], ident)
                            return ins

                        def turn_q(name, c):
                            w(pe, "qs_ready", 4 * n + 2 * c + 2)
                            for j in range(CT):
                                ins = pe.transpose(bank(s, name)[:, j * P:(j + 1) * P], qs[:, c * CT + j, :], ident)
                            return ins

                        def context(name):
                            w(pe, "kv_ready", 4 * n + 4)
                            for j in range(BT):
                                ins = pe.matmul(bank(s, name)[:, 0:P], ekt[:, j, :], kvt[:, j, :], start=(j == 0), stop=(j == BT - 1))
                            return ins

                        def turn_weights(name, m):
                            w(pe, "s_ready", 4 * n + m + 1)
                            for h in range(2):
                                a = 2 * h * P
                                pe.transpose(bank(s, name)[:, a:a + P], sm[m % 2][:, h, 0:P], ident)
                                ins = pe.transpose(bank(s, name)[0:SPAN - P, a + P:a + 2 * P], sm[m % 2][:, h, P:SPAN], ident)
                            return ins

                        def attend(name, c):
                            pe.matmul(bank(s, name)[:, :], ctxs[:, :], qcm[:, c * CHUNK:(c + 1) * CHUNK],
                                      start=True, stop=False, skip_group_check=True)
                            for t in range(CT):
                                j = c * CT + t
                                o = bank(s, name)[0:HD, t * P:(t + 1) * P]
                                pe.matmul(o, va[s][:, j, :], pta[:, j, :], start=False, stop=False, skip_group_check=True)
                                ins = pe.matmul(o, vb[s][:, j, :], ptb[:, j, :], start=False, stop=True, skip_group_check=True)
                            return ins

                        def project(name, c):
                            for t in range(CT):
                                j = c * CT + t
                                ins = pe.matmul(bank(s, name)[:, t * P:(t + 1) * P], acm[:, j * P:(j + 1) * P], wprojT[:, :],
                                                start=True, stop=True)
                            return ins

                        def job(part, name, do, *args, after):
                            if has(1 - part):
                                for earlier, image in after:
                                    if not isinstance(image, int) or 0 <= image < BATCH:
                                        was_read(pe, 0 if earlier in JOBS[0] else 1, image, earlier)
                                do(name, *args).then_inc(S[f"done{part}"], 1)

                        job(1, "S0", scores, 0, after=[("KEY1", n)])
                        job(1, "S1", scores, 1, after=[("PT3", n - 1)])
                        job(1, "EKT0", turn_k, 0, after=[("KEY1", n)])
                        job(1, "EKT1", turn_k, 1, after=[("V", n)])
                        job(0, "HT0", turn_h, 0, after=[("OUT0", n - 1)])
                        job(0, "HT1", turn_h, 1, after=[("OUT1", n - 1)])
                        job(1, "QST0", turn_q, 0, after=[("Y0", n - 1)])
                        job(1, "QST1", turn_q, 1, after=[("Y1", n - 1)])
                        job(1, "CTX", context, after=[("EKT1", n), ("S0", n)])
                        job(0, "QKV0", q_and_kv, 0, after=[("HT0", n + 1), ("S1", n)])
                        job(1, "S2", scores, 2, after=[("EKT0", n)])
                        job(1, "PT0", turn_weights, 0, after=[("EKT1", n)])
                        job(0, "QKV1", q_and_kv, 1, after=[("HT0", n + 1)])
                        job(1, "S3", scores, 3, after=[("HT1", n + 1)])
                        job(0, "QKV2", q_and_kv, 2, after=[("HT1", n + 1), ("QST0", n)])
                        job(1, "PT1", turn_weights, 1, after=[("QST1", n)])
                        job(0, "QKV3", q_and_kv, 3, after=[("HT1", n + 1), ("CTX", n)])
                        job(0, "KEY0", keys, 0, after=[("QKV0", n + 1)])
                        job(1, "PT2", turn_weights, 2, after=[("S2", n)])
                        job(0, "KEY1", keys, 1, after=[("PT0", n)])
                        job(0, "K00", first_keys, 0, after=[("QKV1", n + 1)])
                        job(1, "PT3", turn_weights, 3, after=[("S3", n)])
                        job(0, "K01", first_keys, 1, after=[("QKV2", n + 1)])
                        job(0, "V", values, after=[("PT1", n)])
                        job(1, "OUT0", attend, 0, after=[("CTX", n), ("PT1", n), ("QKV3", n + 1)])
                        job(1, "OUT1", attend, 1, after=[("PT3", n), ("KEY0", n + 1)])
                        job(1, "Y0", project, 0, after=[("OUT0", n)])
                        job(1, "Y1", project, 1, after=[("OUT1", n), ("KEY1", n + 1)])
                    images(pe, step)

                @block.scalar
                def _(act):
                    act.preload_act_table(ACT.Exp)
                    act.wait_ge(S["bordered"], 1)

                    def step(n, s, has):
                        next_ = n + 1

                        def read(part, ins):
                            ins.then_inc(S[f"act_read{part}"], 1)

                        def residual(tiles):
                            w(act, "stats", n)
                            w(act, "u_kept", n)
                            for j in tiles:
                                t = next_ * BT + j
                                ins = act.activation(u[1 - s][:, j, :], tok[:, bass.ds(t, 1), :].rearrange("p a c -> p (a c)"),
                                                     ACT.Identity, bias=sc_b[:, bass.ds(t, 1)], scale=sc_a[:, bass.ds(t, 1)])
                            ins.then_inc(S["u_raw"], 1)

                        def h_out(c):
                            done(act, 0, next_, f"HT{c}")
                            read(0, act.activation(hcm[:, WIN + c * CHUNK:WIN + (c + 1) * CHUNK], bank(s, f"HT{c}")[:, :],
                                                   ACT.Identity, bias=col[:, N1B:N1B + 1], scale=col[:, N1G:N1G + 1]))

                        def kv_out(m):
                            done(act, 0, next_, f"QKV{m}")
                            act.activation(kvt[:, 2 * m:2 * m + 2, :],
                                           bank(s, f"QKV{m}")[:, :].rearrange("p (h c) -> p h c", h=2)[:, :, P:2 * P],
                                           ACT.Copy).then_inc(S["kv_ready"], 1)

                        def key_out(c):
                            w(act, "kmax_ready", next_ + 1)
                            b = bank(s, f"KEY{c}")
                            act.activation(q0[:, c * CHUNK:(c + 1) * CHUNK], b[0:HD, :], ACT.Copy)
                            read(0, act.activation(ek[:, c * CHUNK:(c + 1) * CHUNK], b[:, :], ACT.Exp,
                                                   bias=nkmax[:, 0:1], accum_out=ksum[:, c:c + 1]))

                        def first_key_out(c):
                            done(act, 0, next_, f"K0{c}")
                            read(0, act.activation(k0[:, WIN + c * CHUNK:WIN + (c + 1) * CHUNK], bank(s, f"K0{c}")[0:HD, :], ACT.Copy))

                        def value_out():
                            done(act, 0, next_, "V")
                            vv = bank(s, "V")[:, 0:BT * 2 * HD].rearrange("p (j k e) -> p j k e", j=BT, k=2)
                            act.activation(va[1 - s][:, :, :], vv[:, :, 0, :], ACT.Copy)
                            read(0, act.activation(vb[1 - s][:, :, :], vv[0:SPAN - P, :, 1, :], ACT.Copy))

                        def q_exp(m):
                            was_read(act, 0, next_, f"QKV{m}")
                            act.activation(qs[:, 2 * m:2 * m + 2, :], qs[:, 2 * m:2 * m + 2, :], ACT.Exp).then_inc(S["q_exp"], 1)

                        def k_turned(c):
                            done(act, 1, n, f"EKT{c}")
                            read(1, act.activation(ekt[:, c * CT:(c + 1) * CT, :],
                                                   bank(s, f"EKT{c}")[:, :].rearrange("p (j c) -> p j c", c=P), ACT.Copy))

                        def q_turned(c):
                            done(act, 1, n, f"QST{c}")
                            read(1, act.activation(qcm[:, c * CHUNK:(c + 1) * CHUNK], bank(s, f"QST{c}")[:, :], ACT.Copy))

                        def weights(m):
                            w(act, "s_shift", 4 * n + m + 1)
                            for h in range(2):
                                j = 2 * m + h
                                ins = act.activation(sm[m % 2][:, h, :], sm[m % 2][:, h, :], ACT.Exp, bias=nmax[:, j:j + 1],
                                                     accum_out=lsum[:, j:j + 1])
                            ins.then_inc(S["s_exp"], 1)

                        def weights_turned(m):
                            done(act, 1, n, f"PT{m}")
                            pv = bank(s, f"PT{m}")[:, :].rearrange("p (h k c) -> p h k c", h=2, k=2)
                            act.activation(pta[:, 2 * m:2 * m + 2, :], pv[:, :, 0, :], ACT.Copy)
                            read(1, act.activation(ptb[:, 2 * m:2 * m + 2, :], pv[0:SPAN - P, :, 1, :], ACT.Copy))

                        def attention_out(c):
                            done(act, 1, n, f"OUT{c}")
                            read(1, act.activation(acm[:, c * CHUNK:(c + 1) * CHUNK], bank(s, f"OUT{c}")[:, :], ACT.Copy))

                        def keep():
                            was_read(act, 1, n - 1, "Y1")
                            act.activation(res[:, bass.ds((n - 1) * BT, BT), :], u[1 - s][:, :, :], ACT.Copy).then_inc(S["u_kept"], 1)

                        def do(part, work, *args):
                            if has(1 - part):
                                work(*args)
                        do(1, k_turned, 0)
                        do(1, k_turned, 1)
                        do(0, h_out, 0)
                        do(1, weights, 0)
                        do(0, h_out, 1)
                        do(1, weights, 1)
                        do(1, q_turned, 0)
                        do(1, q_turned, 1)
                        do(0, kv_out, 0)
                        do(2, keep)
                        do(1, weights_turned, 0)
                        do(0, kv_out, 1)
                        do(0, kv_out, 2)
                        do(1, weights, 2)
                        do(1, weights_turned, 1)
                        do(0, kv_out, 3)
                        do(1, weights, 3)
                        do(1, weights_turned, 2)
                        do(0, first_key_out, 0)
                        do(1, weights_turned, 3)
                        do(0, q_exp, 0)
                        do(0, first_key_out, 1)
                        do(0, key_out, 0)
                        do(0, key_out, 1)
                        do(0, q_exp, 1)
                        do(0, value_out)
                        do(0, q_exp, 2)
                        do(0, q_exp, 3)
                        do(1, attention_out, 0)
                        do(0, residual, range(0, CT))
                        do(1, attention_out, 1)
                        do(0, residual, range(CT, BT))
                    images(act, step)

                @block.gpsimd
                def _(pool):
                    def step(n, s, has):
                        if has(1):
                            w(pool, "u_raw", 2 * (n + 1) + 2)
                            pool.tensor_tensor(u[1 - s][:, :, :], u[1 - s][:, :, :],
                                               bproj_row[:, :].rearrange("p (a c) -> p a c", a=1).to_broadcast([P, BT, P]),
                                               ALU.add).then_inc(S["u_ready"], 1)
                    images(pool, step)

                @block.vector
                def _(dve):
                    dve.memset(hcm[:, :], 0.0)
                    dve.memset(k0[:, :], 0.0)
                    dve.drain()
                    dve.sem_inc(S["bordered"], 1)

                    def step(n, s, has):
                        next_ = n + 1
                        count = [0, 0]

                        def link(part, ins):
                            ins.then_inc(S[f"link{part}"], 1)
                            count[part] += 1
                            w(dve, f"link{part}", LINKS[part] * (n + 1 - part) + count[part])

                        def read(part, ins):
                            ins.then_inc(S[f"dve_read{part}"], 1)

                        def norm(c):
                            for j in range(c * CT, (c + 1) * CT):
                                t = (n + 2) * BT + j
                                ins = dve.tensor_scalar(ht[s][:, j, :], tok[:, bass.ds(t, 1), :].rearrange("p a c -> p (a c)"),
                                                        sc_c[:, bass.ds(t, 1)], sc_d[:, bass.ds(t, 1)], ALU.mult, ALU.add)
                            ins.then_inc(S["ht_ready"], 1)

                        def q_shift(m):
                            w(dve, "kv_ready", 4 * next_ + m + 1)
                            q4 = bank(s, f"QKV{m}")[:, :].rearrange("p (h c) -> p h c", h=2)[:, :, 0:P].rearrange("p h (g d) -> p h g d", d=HD)
                            link(0, dve.tensor_reduce(qmax[:, m, :].rearrange("p (h g) -> p h g", h=2), q4, AX.X, ALU.max))
                            read(0, dve.tensor_tensor(qs[:, 2 * m:2 * m + 2, :].rearrange("p h (g d) -> p h g d", d=HD), q4,
                                                      qmax[:, m, :].rearrange("p (h g a) -> p h g a", h=2, a=1).to_broadcast([P, 2, HEADS, HD]),
                                                      ALU.subtract))

                        def k_max():
                            for c in range(2):
                                done(dve, 0, next_, f"KEY{c}")
                                ins = dve.tensor_reduce(kmax[:, c:c + 1], bank(s, f"KEY{c}")[:, :], AX.X, ALU.max)
                            link(0, ins)
                            dve.tensor_reduce(nkmax[:, :], kmax[:, :], AX.X, ALU.max, negate=True).then_inc(S["kmax_ready"], 1)

                        def q_out(m):
                            w(dve, "q_exp", 4 * next_ + m + 1)
                            q4 = qs[:, 2 * m:2 * m + 2, :].rearrange("p h (g d) -> p h g d", d=HD)
                            r = qsum[:, 2 * m * HEADS:(2 * m + 2) * HEADS]
                            link(0, dve.tensor_reduce(r.rearrange("p (h g) -> p h g", h=2), q4, AX.X, ALU.add))
                            link(0, dve.reciprocal(r, r))
                            dve.tensor_tensor(q4, q4, r.rearrange("p (h g a) -> p h g a", h=2, a=1).to_broadcast([P, 2, HEADS, HD]),
                                              ALU.mult).then_inc(S["qs_ready"], 1)

                        def k_scale():
                            was_read(dve, 0, next_, "KEY1")
                            link(0, dve.tensor_tensor(kinv[:, :], ksum[:, 0:1], ksum[:, 1:2], ALU.add))
                            link(0, dve.reciprocal(kinv[:, :], kinv[:, :]))
                            link(0, dve.tensor_scalar(kinv[:, :], kinv[:, :], HD ** -0.5, None, ALU.mult))

                        def scores_in(m):
                            if m >= 2:
                                done(dve, 1, n, f"PT{m - 2}")
                            done(dve, 1, n, f"S{m}")
                            for h in range(2):
                                j = 2 * m + h
                                kind = 0 if j == 0 else 2 if j == BT - 1 else 1
                                ins = dve.scalar_tensor_tensor(sm[m % 2][:, h, :], bank(s, f"S{m}")[:, h * SPAN:(h + 1) * SPAN], HD ** -0.5,
                                                               cst[:, C_MASK + kind * SPAN:C_MASK + (kind + 1) * SPAN], ALU.mult, ALU.add)
                            read(1, ins)
                            was_read(dve, 1, n, f"S{m}")
                            dve.tensor_reduce(nmax[:, 2 * m:2 * m + 2], sm[m % 2][:, :, :], AX.X, ALU.max, negate=True).then_inc(S["s_shift"], 1)

                        def scores_out(m):
                            w(dve, "s_exp", 4 * n + m + 1)
                            link(1, dve.reciprocal(linv[:, 2 * m:2 * m + 2], lsum[:, 2 * m:2 * m + 2]))
                            for h in range(2):
                                ins = dve.tensor_scalar(sm[m % 2][:, h, :], sm[m % 2][:, h, :], linv[:, 2 * m + h:2 * m + h + 1], None, ALU.mult)
                            ins.then_inc(S["s_ready"], 1)

                        def context():
                            done(dve, 1, n, "CTX")
                            read(1, dve.scalar_tensor_tensor(ctxs[:, :], bank(s, "CTX")[:, 0:P], kinv[:, 0:1],
                                                             cst[:, C_HEAD:C_HEAD + P], ALU.mult, ALU.mult))

                        def add(c):
                            done(dve, 1, n, f"Y{c}")
                            w(dve, "u_ready", n + 1)
                            tiles = u[s][:, c * CT:(c + 1) * CT, :]
                            read(1, dve.tensor_tensor(tiles, bank(s, f"Y{c}")[:, :].rearrange("p (j c) -> p j c", c=P), tiles, ALU.add))

                        def stats():
                            was_read(dve, 1, n - 1, "Y1")
                            for j in range(BT):
                                ins = dve.bn_stats(tbn[:, j, :], u[1 - s][:, j, :])
                            ins.then_inc(S["stats"], 1)

                        def keep_stats():
                            w(dve, "stats", n)
                            dve.tensor_copy(bst[:, bass.ds((n - 1) * BT, BT), :], tbn[:, :, :])

                        def do(part, work, *args):
                            if has(1 - part):
                                work(*args)
                        do(1, scores_in, 0)
                        do(1, scores_in, 1)
                        do(2, stats)
                        do(1, scores_out, 0)
                        do(1, context)
                        do(1, scores_out, 1)
                        do(2, keep_stats)
                        do(1, scores_in, 2)
                        do(0, q_shift, 0)
                        do(0, q_shift, 1)
                        do(0, q_shift, 2)
                        do(1, scores_out, 2)
                        do(1, scores_in, 3)
                        do(0, q_shift, 3)
                        do(1, scores_out, 3)
                        do(0, k_max)
                        do(-1, norm, 0)
                        do(-1, norm, 1)
                        do(0, q_out, 0)
                        do(0, q_out, 1)
                        do(0, q_out, 2)
                        do(0, q_out, 3)
                        do(0, k_scale)
                        do(1, add, 0)
                        do(1, add, 1)
                    images(dve, step)
                    dve.drain()

        norm_scales(False, "_2")

        gates = sb("gates", [P, TILES, 2])
        to_load = sb("to_load", [P, COLS], mybir.dt.uint32)
        to_store = sb("to_store", [P, COLS], mybir.dt.uint32)
        expert = sb("expert", [P, COLS], mybir.dt.int32)
        late = ctx.enter_context(ExitStack())
        raw1, raw3 = [sb(f"raw{k}", [P, EXPERTS, len(HT), P], scope=late) for k in (1, 3)]
        padded, w_loaded = sem("padded", late), sem("w_loaded", late)
        W_LOADS = 4 * EXPERTS

        with ExitStack() as ph:
            CHUNKS, UPS = TOK // CHUNK, MLP // P
            ht = [sb(f"mht{s}", [P, CT, P], scope=ph) for s in range(2)]
            hv = [sb(f"mhv{s}", [P, CHUNK], scope=ph) for s in range(2)]
            hh = [sb(f"mhh{s}", [P, CHUNK], F32R, scope=ph) for s in range(2)]
            hl = [sb(f"mhl{s}", [P, CHUNK], F32R, scope=ph) for s in range(2)]
            gv = [sb(f"mgv{s}", [P, UPS, CHUNK], scope=ph) for s in range(2)]
            acc = [sb(f"macc{s}", [P, CT, P], scope=ph) for s in range(2)]
            tbn = [sb(f"mbn{s}", [P, CT, 6], scope=ph) for s in range(2)]
            S = {name: sem("m_" + name, ph) for name in
                 ("ht_ready", "ht_turned", "h_full", "h_high", "h_low", "up", "gelu", "down", "base", "base_ready", "t1",
                  "stats", "t1_kept")}

            def w(eng, name, count):
                if not isinstance(count, int) or count > 0:
                    eng.wait_ge(S[name], count)

            def steps(eng, step):
                for n in range(-3, 2):
                    step(n, n % 2, lambda d: 0 <= n + d < CHUNKS)
                with eng.Fori(1, (CHUNKS - 4) // 2) as i:
                    for s in range(2):
                        step(i * 2 + s, s, lambda d: True)
                for n in range(2 * ((CHUNKS - 4) // 2), CHUNKS + 1):
                    step(n, n % 2, lambda d: 0 <= n + d < CHUNKS)

            turnb, upb, downb = banks[0:2], banks[2:6], banks[6:8]
            with nc.Block() as block:
                @block.sync
                def _(sp):
                    sp.wait_ge(padded, 1)
                    for e in range(EXPERTS):
                        for raw, w_ in ((raw1, w1), (raw3, w3)):
                            sp.dma_start(raw[:, e, 0:2, :], w_[e, 0:2 * P, :].rearrange("(k p) c -> p k c", p=P)).then_inc(w_loaded, 16)
                            sp.dma_start(raw[0:HT[2][1], e, 2, :], w_[e, 2 * P:HID, :]).then_inc(w_loaded, 16)

                @block.tensor
                def _(pe):
                    def step(n, s, has):
                        if has(2):
                            w(pe, "ht_ready", n + 3)
                            w(pe, "h_full", n + 1)
                            for j in range(CT):
                                ins = pe.transpose(turnb[s][:, j * P:(j + 1) * P], ht[s][:, j, :], ident)
                            ins.then_inc(S["ht_turned"], 1)
                        if has(1):
                            w(pe, "h_low", n + 2)
                            for k in range(UPS):
                                w(pe, "gelu", UPS * n + k + 1)
                                c = slice(k * P, (k + 1) * P)
                                pe.matmul(upb[k][:, :], upH[:, c], hh[1 - s][:, :], start=True, stop=False)
                                pe.matmul(upb[k][:, :], upH[:, c], hl[1 - s][:, :], start=False, stop=False)
                                pe.matmul(upb[k][:, :], upL[:, c], hh[1 - s][:, :], start=False, stop=True).then_inc(S["up"], 1)
                        if has(0):
                            w(pe, "t1", n - 1)
                            w(pe, "gelu", UPS * (n + 1))
                            for j in range(CT):
                                c = slice(j * P, (j + 1) * P)
                                for k in range(UPS):
                                    ins = pe.matmul(downb[s][:, c], gv[s][:, k, c], downT[:, k, :], start=(k == 0), stop=(k == UPS - 1))
                            ins.then_inc(S["down"], 1)
                    steps(pe, step)

                @block.scalar
                def _(act):
                    act.preload_act_table(ACT.Gelu)

                    def step(n, s, has):
                        if has(2):
                            w(act, "ht_turned", n + 3)
                            w(act, "h_low", n + 1)
                            act.activation(hv[s][:, :], turnb[s][:, :], ACT.Identity, bias=col[:, N2B:N2B + 1],
                                           scale=col[:, N2G:N2G + 1]).then_inc(S["h_full"], 1)
                        for k in range(UPS):
                            if has(1):
                                w(act, "up", UPS * (n + 1) + k + 1)
                                if k == 0:
                                    w(act, "down", n)
                                act.activation(gv[1 - s][:, k, :], upb[k][:, :], ACT.Gelu,
                                               bias=col[:, BUP + k:BUP + k + 1]).then_inc(S["gelu"], 1)
                            if k == 0 and has(-1):
                                w(act, "t1", n)
                                act.activation(tok[:, bass.ds((n - 1) * CT, CT), :], acc[1 - s][:, :, :], ACT.Copy
                                               ).then_inc(S["t1_kept"], 1)
                    steps(act, step)

                @block.gpsimd
                def _(pool):
                    for raw in (raw1, raw3):
                        ins = pool.memset(raw[:, :, 2, :], 0.0)
                    ins.then_inc(padded, 1)
                    def step(n, s, has):
                        if has(0):
                            w(pool, "base", n + 1)
                            pool.tensor_tensor(acc[s][:, :, :], acc[s][:, :, :],
                                               bdown_row[:, :].rearrange("p (a c) -> p a c", a=1).to_broadcast([P, CT, P]),
                                               ALU.add).then_inc(S["base_ready"], 1)
                    steps(pool, step)

                @block.vector
                def _(dve):
                    def step(n, s, has):
                        if has(-1):
                            w(dve, "down", n)
                            w(dve, "base_ready", n)
                            a = acc[1 - s]
                            dve.tensor_tensor(a[:, :, :], downb[1 - s][:, :].rearrange("p (j c) -> p j c", c=P),
                                              a[:, :, :], ALU.add).then_inc(S["t1"], 1)
                        if has(2):
                            w(dve, "h_full", n + 3)
                            w(dve, "up", UPS * (n + 1))
                            dve.tensor_copy(hh[s][:, :], hv[s][:, :]).then_inc(S["h_high"], 1)
                        if has(-1):
                            w(dve, "t1", n)
                            for j in range(CT):
                                ins = dve.bn_stats(tbn[1 - s][:, j, :], a[:, j, :])
                            ins.then_inc(S["stats"], 1)
                        if has(2):
                            w(dve, "h_high", n + 3)
                            dve.tensor_tensor(hl[s][:, :], hv[s][:, :], hh[s][:, :].bitcast(F32), ALU.subtract).then_inc(S["h_low"], 1)
                        if has(0):
                            w(dve, "t1_kept", n - 1)
                            dve.tensor_tensor(acc[s][:, :, :], tok[:, bass.ds(n * CT, CT), :], res[:, bass.ds(n * CT, CT), :],
                                              ALU.add).then_inc(S["base"], 1)
                        if has(3):
                            w(dve, "ht_turned", n + 2)
                            for j in range(CT):
                                t = (n + 3) * CT + j
                                ins = dve.tensor_scalar(ht[1 - s][:, j, :], res[:, bass.ds(t, 1), :].rearrange("p a c -> p (a c)"),
                                                        sc_a[:, bass.ds(t, 1)], sc_b[:, bass.ds(t, 1)], ALU.mult, ALU.add)
                            ins.then_inc(S["ht_ready"], 1)
                        if has(-1):
                            w(dve, "stats", n)
                            dve.tensor_copy(bst[:, bass.ds((n - 1) * CT, CT), :], tbn[1 - s][:, :, :])
                    steps(dve, step)
                    dve.drain()

        norm_scales(False, "_3")

        with ExitStack() as ph:
            NB = 4
            ht = [res[:, s * CT:(s + 1) * CT, :] for s in range(NB)]
            hc = [res[:, (NB + s) * CT:(NB + s + 1) * CT, :].rearrange("p j c -> p (j c)") for s in range(2)]
            prob = sb("prob", [P, TILES, EXPERTS], scope=ph)
            best = sb("best", [P, TILES, EXPERTS], scope=ph)
            bidx = sb("bidx", [P, TILES, EXPERTS], mybir.dt.uint32, scope=ph)
            bidf = sb("bidf", [P, TILES, 2], scope=ph)
            one = [sb(f"one{k}", [P, TILES, EXPERTS], scope=ph) for k in range(2)]
            chosen = sb("chosen", [P, TILES, EXPERTS], scope=ph)
            rank = sb("rank", [P, TILES, EXPERTS], scope=ph)
            cum = [sb(f"cum{k}", [P, TILES, EXPERTS], scope=ph) for k in range(2)]
            rmax = sb("rmax", [P, TILES], scope=ph)
            rsum = sb("rsum", [P, TILES], scope=ph)
            size = [sb(f"size{k}", [P, EXPERTS], scope=ph) for k in range(3)]
            whole8 = sb("whole8", [P, EXPERTS], mybir.dt.int32, scope=ph)
            slot = sb("slot", [P, TILES, 2], scope=ph)
            slot_hi = sb("slot_hi", [P, TILES, 2], scope=ph)
            slot_i = sb("slot_i", [P, TILES, 2], mybir.dt.int32, scope=ph)
            tab = sb("tab", [P, COLS], scope=ph)
            tmp = [sb(f"tmp{k}", [P, COLS], scope=ph) for k in range(2)]
            RING = 8
            is_lo = [sb(f"is_lo{r}", [P, P], scope=ph) for r in range(RING)]
            is_hi = [sb(f"is_hi{r}", [P, COLS], scope=ph) for r in range(RING)]
            kept = [sem(f"r_kept{s}", ph) for s in range(NB)]
            w2_loaded, w_turned, w_low, w_out, logits_read = [sem("r_" + n, ph) for n in
                                                              ("w2_loaded", "w_turned", "w_low", "w_out", "logits_read")]
            W_BANKS = 4
            at = (NB + 2) * CT
            whole_w = [res[:, at + r * len(HT):at + (r + 1) * len(HT), :].rearrange("p k c -> p (k c)")[:, 0:HIDP]
                       for r in range(W_BANKS)]
            raw2 = res[:, at + W_BANKS * len(HT):, :].rearrange("p k c -> p (k c)")[:, 0:EXPERTS * HID].rearrange("p (e h) -> p e h", h=HID)
            groups = [([(raw[0:m, e, k, :], m, P, a) for k, (a, m) in enumerate(HTP)],
                       dst[:, e * HIDP:(e + 1) * HIDP], low[:, e * HIDP:(e + 1) * HIDP])
                      for raw, dst, low in ((raw1, w1H, w1L), (raw3, w3H, w3L)) for e in range(EXPERTS)]
            groups += [([(raw2[:, e, a:a + m], P, m, k * P) for k, (a, m) in enumerate(HT)], w2v[:, e, :, :], None)
                       for e in range(EXPERTS)]
            S = {name: Signal(sem("r_" + name, ph), each) for name, each in {
                "ht_ready": NB, "turned": NB, "hc_ready": NB, "logit": NB,
                "hot": RING, "squared": RING // 2, "hot_lo": RING // 2, "hot_used": RING}.items()}
            chain, expd, counted = sem("r_chain", ph), sem("r_expd", ph), sem("r_counted", ph)
            to_count, to_exp = sem("r_to_count", ph), sem("r_to_exp", ph)

            def w(eng, name, i, n):
                eng.wait_ge(S[name].sem, S[name].at(i, n))

            def logits_out(dve, c):
                dve.wait_ge(S["logit"].sem, c + 1)
                dve.tensor_copy(prob[:, c * CT:(c + 1) * CT, :], banks[2 + c % NB][:, 0:CT * EXPERTS].rearrange("p (j e) -> p j e", e=EXPERTS))

            with nc.Block() as block:
                @block.sync
                def _(sp):
                    sp.dma_start(raw2, w2.rearrange("e c h -> c e h")).then_inc(w2_loaded, 16)
                    for c in range(TOK // CHUNK):
                        sp.wait_ge(S["ht_ready"].sem, c + 1)
                        sp.dma_start(normed_t[:, c * CT:(c + 1) * CT, :], ht[c % NB]).then_inc(kept[c % NB], 16)
                    for s in range(NB):
                        sp.wait_ge(kept[s], 16 * (TOK // CHUNK // NB))

                @block.tensor
                def _(pe):
                    def turn(n, s):
                        pe.wait_ge(S["ht_ready"].sem, n + 1)
                        for j in range(CT):
                            ins = pe.transpose(banks[s % 2][:, j * P:(j + 1) * P], ht[s][:, j, :], ident)
                        ins.then_inc(S["turned"].sem, 1)

                    def logits(n, s):
                        pe.wait_ge(S["hc_ready"].sem, n + 1)
                        for j in range(CT):
                            ins = pe.matmul(banks[2 + s][:, j * EXPERTS:(j + 1) * EXPERTS], hc[s % 2][:, j * P:(j + 1) * P],
                                            routerT[:, :], start=True, stop=True)
                        ins.then_inc(S["logit"].sem, 1)

                    turn(0, 0)
                    with pe.Fori(0, TOK // CHUNK // NB - 1) as i:
                        for s in range(NB):
                            turn(i * NB + s + 1, (s + 1) % NB)
                            logits(i * NB + s, s)
                    for s in range(NB):
                        n = TOK // CHUNK - NB + s
                        if s + 1 < NB:
                            turn(n + 1, s + 1)
                        logits(n, s)
                    pe.wait_ge(logits_read, 1)
                    pe.wait_ge(w_loaded, 16 * W_LOADS)
                    for g, (turns, _, low) in enumerate(groups):
                        if low is None:
                            pe.wait_ge(w2_loaded, 16)
                        if g >= W_BANKS:
                            pe.wait_ge(w_out, g - W_BANKS + 1)
                        for src, rows, cols, at_ in turns:
                            ins = pe.transpose(banks[g % W_BANKS][0:cols, at_:at_ + rows], src, ident[0:rows, 0:rows])
                        ins.then_inc(w_turned, 1)
                    pe.wait_ge(to_count, 1)
                    m = chosen[:, :, :].rearrange("p t e -> p (t e)")
                    pe.matmul(banks[4][:, :], cst[:, C_UPPER:C_UPPER + P], m, start=True, stop=True)
                    pe.matmul(banks[5][:, :], cst[:, C_ONES:C_ONES + P], m, start=True, stop=True).then_inc(counted, 1)
                    with pe.Fori(0, 2 * TILES // RING) as i:
                        for r in range(RING):
                            w(pe, "hot", i, r + 1)
                            if r % 2 == 0:
                                w(pe, "hot_lo", i, r // 2 + 1)
                            pe.matmul(banks[6][:, 0:COLS], is_lo[r][:, :], is_hi[r][:, :], start=False, stop=True,
                                      skip_group_check=True).then_inc(S["hot_used"].sem, 1)

                @block.scalar
                def _(act):
                    act.preload_act_table(ACT.Exp)
                    with act.Fori(0, TOK // CHUNK // NB) as i:
                        for s in range(NB):
                            w(act, "turned", i, s + 1)
                            act.activation(hc[s % 2], banks[s % 2][:, :], ACT.Copy).then_inc(S["hc_ready"].sem, 1)
                    act.wait_ge(to_exp, 1)
                    act.activation(prob[:, :, :], prob[:, :, :], ACT.Exp).then_inc(expd, 1)
                    for g, (_, dst, low) in enumerate(groups):
                        act.wait_ge(w_turned, g + 1)
                        b = banks[g % W_BANKS]
                        if low is not None:
                            if g >= W_BANKS:
                                act.wait_ge(w_low, g - W_BANKS + 1)
                            act.activation(whole_w[g % W_BANKS], b[:, 0:HIDP], ACT.Copy)
                            act.activation(dst, b[:, 0:HIDP], ACT.Copy).then_inc(w_out, 1)
                        else:
                            tail = HT[-1][1]
                            act.activation(dst[:, 0:2, :], b[:, 0:2 * P].rearrange("p (k c) -> p k c", c=P), ACT.Copy)
                            act.activation(dst[0:tail, 2, :], b[0:tail, 2 * P:3 * P], ACT.Copy).then_inc(w_out, 1)
                    lo = slot[:, :, :].rearrange("p t k -> p (t k)")
                    with act.Fori(0, 2 * TILES // RING) as i:
                        for r in range(0, RING, 2):
                            w(act, "hot_used", i, r + 1)
                            act.activation(is_lo[r][:, :], cst[:, C_COL:C_COL + P], ACT.Square, bias=lo[:, bass.ds(i * RING + r, 1)],
                                           scale=-1.0).then_inc(S["squared"].sem, 1)
                        for r in range(0, RING, 2):
                            w(act, "squared", i, r // 2 + 1)
                            act.activation(is_lo[r][:, :], is_lo[r][:, :], ACT.Relu, bias=cst[:, C_ONES:C_ONES + 1],
                                           scale=-1.0).then_inc(S["hot_lo"].sem, 1)

                @block.gpsimd
                def _(pool):
                    for g, (_, dst, low) in enumerate(groups):
                        if low is not None:
                            pool.wait_ge(w_out, g + 1)
                            pool.tensor_tensor(low, whole_w[g % W_BANKS], dst.bitcast(F32), ALU.subtract).then_inc(w_low, 1)

                @block.vector
                def _(dve):
                    for c in range(TOK // CHUNK):
                        s = c % NB
                        t = c * CT
                        if c >= NB:
                            dve.wait_ge(kept[s], 16 * (c // NB))
                            dve.wait_ge(S["turned"].sem, c - NB + 1)
                        for j in range(CT):
                            ins = dve.tensor_scalar(ht[s][:, j, :], tok[:, t + j, :], sc_a[:, t + j:t + j + 1], sc_b[:, t + j:t + j + 1],
                                                    ALU.mult, ALU.add)
                        ins.then_inc(S["ht_ready"].sem, 1)
                        if c >= 2:
                            logits_out(dve, c - 2)
                    for c in (TOK // CHUNK - 2, TOK // CHUNK - 1):
                        logits_out(dve, c)
                    dve.drain()
                    dve.sem_inc(logits_read, 1)
                    n = [0]

                    def step(ins):
                        ins.then_inc(chain, 1)
                        n[0] += 1
                        dve.wait_ge(chain, n[0])

                    def each(v):
                        return v.rearrange("p (t a) -> p t a", a=1).to_broadcast([P, TILES, EXPERTS])

                    def over(v):
                        return v.rearrange("p (a e) -> p a e", a=1).to_broadcast([P, TILES, EXPERTS])
                    step(dve.tensor_reduce(rmax[:, :], prob[:, :, :], AX.X, ALU.max))
                    dve.tensor_tensor(prob[:, :, :], prob[:, :, :], each(rmax[:, :]), ALU.subtract).then_inc(to_exp, 1)
                    dve.wait_ge(expd, 1)
                    step(dve.tensor_reduce(rsum[:, :], prob[:, :, :], AX.X, ALU.add))
                    step(dve.reciprocal(rsum[:, :], rsum[:, :]))
                    step(dve.tensor_tensor(prob[:, :, :], prob[:, :, :], each(rsum[:, :]), ALU.mult))
                    for t in range(TILES):
                        ins = dve.max(best[:, t, :], prob[:, t, :])
                    step(ins)
                    for t in range(TILES):
                        ins = dve.max_index(bidx[:, t, :], best[:, t, :], prob[:, t, :])
                    step(ins)
                    step(dve.tensor_copy(bidf[:, :, :], bidx[:, :, 0:2]))
                    iota = over(cst[:, C_IOTA:C_IOTA + EXPERTS])
                    for k in range(2):
                        ins = dve.tensor_tensor(one[k][:, :, :], iota, each(bidf[:, :, k]), ALU.is_equal)
                    step(ins)
                    dve.tensor_tensor(chosen[:, :, :], one[0][:, :, :], one[1][:, :, :], ALU.add).then_inc(to_count, 1)
                    step(dve.tensor_tensor(rsum[:, :], best[:, :, 0], best[:, :, 1], ALU.add))
                    step(dve.tensor_scalar(rsum[:, :], rsum[:, :], 1e-9, None, ALU.add))
                    step(dve.reciprocal(rsum[:, :], rsum[:, :]))
                    dve.tensor_tensor(gates[:, :, :], best[:, :, 0:2],
                                      rsum[:, :].rearrange("p (t a) -> p t a", a=1).to_broadcast([P, TILES, 2]), ALU.mult)
                    dve.memset(banks[6][:, :], 0.0)
                    dve.wait_ge(counted, 1)
                    total = banks[5][:, :].rearrange("p (t e) -> p t e", e=EXPERTS)
                    step(dve.tensor_copy(cum[0][:, :, :], total))
                    a, d = 0, 1
                    while d < TILES:
                        dve.tensor_copy(cum[1 - a][:, 0:d, :], cum[a][:, 0:d, :])
                        step(dve.tensor_tensor(cum[1 - a][:, d:, :], cum[a][:, d:, :], cum[a][:, :TILES - d, :], ALU.add))
                        a, d = 1 - a, 2 * d
                    step(dve.tensor_scalar(size[0][:, :], cum[a][:, TILES - 1, :], 1.0 / P, (P - 1.0) / P - 0.5 + 0.5 / P, ALU.mult, ALU.add))
                    step(dve.tensor_copy(whole8[:, :], size[0][:, :]))
                    step(dve.tensor_copy(size[0][:, :], whole8[:, :]))
                    step(dve.tensor_copy(size[2][:, :], size[0][:, :]))
                    b, d = 2, 1
                    while d < EXPERTS:
                        c = 1 if b == 2 else 2
                        dve.tensor_copy(size[c][:, 0:d], size[b][:, 0:d])
                        step(dve.tensor_tensor(size[c][:, d:], size[b][:, d:], size[b][:, :EXPERTS - d], ALU.add))
                        b, d = c, 2 * d
                    ends = size[b]
                    step(dve.memset(tmp[0][:, :], 0.0))
                    for e in range(EXPERTS - 1):
                        step(dve.scalar_tensor_tensor(tmp[0][:, :], cst[:, C_COL:C_COL + COLS], ends[:, e:e + 1], tmp[0][:, :],
                                                      ALU.is_ge, ALU.add))
                    dve.tensor_copy(expert[:, :], tmp[0][:, :])
                    step(dve.tensor_tensor(size[0][:, :], ends[:, :], size[0][:, :], ALU.subtract))
                    step(dve.tensor_scalar(size[0][:, :], size[0][:, :], float(P), None, ALU.mult))
                    step(dve.tensor_tensor(cum[a][:, :, :], cum[a][:, :, :], total, ALU.subtract))
                    step(dve.tensor_tensor(rank[:, :, :], cum[a][:, :, :], banks[4][:, :].rearrange("p (t e) -> p t e", e=EXPERTS), ALU.add))
                    step(dve.tensor_tensor(rank[:, :, :], rank[:, :, :], over(size[0][:, :]), ALU.add))
                    for k in range(2):
                        ins = dve.tensor_tensor(one[k][:, :, :], one[k][:, :, :], rank[:, :, :], ALU.mult)
                    step(ins)
                    for k in range(2):
                        ins = dve.tensor_reduce(slot[:, :, k], one[k][:, :, :], AX.X, ALU.add)
                    step(ins)
                    step(dve.tensor_scalar(slot_hi[:, :, :], slot[:, :, :], 1.0 / P, 0.5 / P - 0.5, ALU.mult, ALU.add))
                    step(dve.tensor_copy(slot_i[:, :, :], slot_hi[:, :, :]))
                    step(dve.tensor_copy(slot_hi[:, :, :], slot_i[:, :, :]))
                    step(dve.scalar_tensor_tensor(slot[:, :, :], slot_hi[:, :, :], -float(P), slot[:, :, :], ALU.mult, ALU.add))
                    lo = slot[:, :, :].rearrange("p t k -> p (t k)")
                    hi = slot_hi[:, :, :].rearrange("p t k -> p (t k)")
                    dve.drain()
                    dve.sem_inc(S["hot_used"].sem, RING)
                    with dve.Fori(0, 2 * TILES // RING) as i:
                        for r in range(RING):
                            w(dve, "hot_used", i, r + 1)
                            q = i * RING + r
                            if r % 2:
                                dve.tensor_scalar(is_lo[r][:, :], cst[:, C_COL:C_COL + P], lo[:, bass.ds(q, 1)], None, ALU.is_equal)
                            dve.tensor_scalar(is_hi[r][:, :], cst[:, C_COL:C_COL + COLS], hi[:, bass.ds(q, 1)], cst[:, bass.ds(C_NAME + q, 1)],
                                              ALU.is_equal, ALU.mult).then_inc(S["hot"].sem, 1)
                    dve.wait_ge(S["hot_used"].sem, S["hot_used"].at(2 * TILES // RING, RING))
                    step(dve.tensor_copy(tab[:, :], banks[6][:, 0:COLS]))
                    step(dve.tensor_scalar(tmp[0][:, :], tab[:, :], TOK + P - 0.5, -float(TOK), ALU.is_gt, ALU.mult))
                    step(dve.tensor_tensor(tmp[0][:, :], tmp[0][:, :], tab[:, :], ALU.add))
                    dve.tensor_scalar(to_load[:, :], tmp[0][:, :], -float(P), 0.0, ALU.add, ALU.max)
                    step(dve.scalar_tensor_tensor(tmp[1][:, :], tab[:, :], 0.5, cst[:, C_SPARE:C_SPARE + COLS], ALU.is_lt, ALU.mult))
                    step(dve.tensor_tensor(tmp[1][:, :], tmp[1][:, :], tab[:, :], ALU.add))
                    step(dve.tensor_scalar(to_store[:, :], tmp[1][:, :], float((ER - 1) * P), None, ALU.add))

        late.close()

        with ExitStack() as ph:
            R = ER
            LEAD, LATE = 8, 2
            xg = [sb(f"xg{r}", [P, P], scope=ph) for r in range(R)]
            lidx = [sb(f"lidx{r}", [P, 1], mybir.dt.uint32, scope=ph) for r in range(R)]
            sidx = [sb(f"sidx{r}", [P, 1], mybir.dt.uint32, scope=ph) for r in range(R)]
            xh = [sb(f"xh{r}", [P, P], F32R, scope=ph) for r in range(2)]
            xl = [sb(f"xl{r}", [P, P], F32R, scope=ph) for r in range(2)]
            sl = [sb(f"sl{r}", [P, HIDP], scope=ph) for r in range(2)]
            hm = [sb(f"hm{r}", [P, HIDP], scope=ph) for r in range(2)]
            hmt = [sb(f"hmt{r}", [P, len(HT), P], scope=ph) for r in range(2)]
            yt = [sb(f"yt{r}", [P, P], scope=ph) for r in range(R)]
            S = {name: Signal(sem("e_" + name, ph), R) for name in
                 ("x_turned", "x_high", "x_low", "h1", "h3", "silu", "h_ready", "h_turned", "ht_ready", "y", "y_ready", "y_free",
                  "row_picked", "place_picked")}
            gathered = [sem(f"gathered{r}", ph) for r in range(R)]
            scattered = [sem(f"scattered{r}", ph) for r in range(R)]
            issued = sem("issued", ph)
            xb, hb, yb = banks[0], banks[1], banks[2:4]
            h1b, h3b = banks[4:6], banks[6:8]

            def w(eng, name, n):
                eng.wait_ge(S[name].sem, n + 1)

            with nc.Block() as block:
                @block.gpsimd
                def _(pool):
                    def fetch(n, r):
                        w(pool, "row_picked", n)
                        pool.sem_inc(issued, 1)
                        pool.indirect_dma_start(xg[r][:, :], None, normed, bass.IndirectOffsetOnAxis(lidx[r][:, :], 0)
                                                ).then_inc(gathered[r], 16)

                    def scatter(i, s, has_free=True):
                        n = i * R + s - LATE
                        r = (s - LATE) % R
                        if has_free:
                            f = s - LATE - 3
                            pool.wait_ge(scattered[f % R], 16 * (i + f // R + 1))
                            pool.sem_inc(S["y_free"].sem, 1)
                        w(pool, "place_picked", n)
                        w(pool, "y_ready", n)
                        pool.sem_inc(issued, 1)
                        pool.indirect_dma_start(mixed, bass.IndirectOffsetOnAxis(sidx[r][:, :], 0), yt[r][:, :], None
                                                ).then_inc(scattered[r], 16)

                    def turn(i, s):
                        n = i * R + s
                        if not isinstance(n, int) or n >= LATE:
                            scatter(i, s, not isinstance(n, int) or n >= LATE + 3)
                        fetch(n + LEAD, (s + LEAD) % R)

                    pool.sem_inc(S["y_free"].sem, R)
                    for n in range(LEAD):
                        fetch(n, n % R)
                    for s in range(R):
                        turn(0, s)
                    with pool.Fori(1, SLOTS // R) as i:
                        for s in range(R):
                            turn(i, s)
                    for s in range(LATE):
                        scatter(SLOTS // R, s)
                    for r in range(R):
                        pool.wait_ge(scattered[r], 16 * (SLOTS // R))
                        pool.wait_ge(gathered[r], 16 * ((SLOTS + LEAD - r + R - 1) // R))

                @block.tensor
                def _(pe):
                    def turn_x(n, r, count):
                        pe.wait_ge(gathered[r], 16 * count)
                        if not (isinstance(n, int) and n == 0):
                            w(pe, "x_low", n - 1)
                        pe.transpose(xb[:, 0:P], xg[r][:, :], ident).then_inc(S["x_turned"].sem, 1)

                    def front(n, e, r, ahead):
                        w(pe, "x_low", n)
                        if ahead:
                            w(pe, "silu", n - 2)
                        o1, o3 = h1b[r % 2][:, 0:HIDP], h3b[r % 2][:, 0:HIDP]
                        for o, wh, wl, name in ((o1, w1H, w1L, "h1"), (o3, w3H, w3L, "h3")):
                            if name == "h3" and ahead:
                                w(pe, "h_ready", n - 2)
                            a = bass.ds(e * HIDP, HIDP)
                            pe.matmul(o, xh[r % 2][:, :], wh[:, a], start=True, stop=False)
                            pe.matmul(o, xl[r % 2][:, :], wh[:, a], start=False, stop=False)
                            pe.matmul(o, xh[r % 2][:, :], wl[:, a], start=False, stop=True).then_inc(S[name].sem, 1)

                    def turn_h(n, r, ahead):
                        w(pe, "h_ready", n)
                        if ahead:
                            w(pe, "ht_ready", n - 1)
                        for k, (a, m) in enumerate(HT):
                            ins = pe.transpose(hb[0:m, k * P:(k + 1) * P], hm[r % 2][:, a:a + m], ident)
                        ins.then_inc(S["h_turned"].sem, 1)

                    def back(n, e, r):
                        w(pe, "ht_ready", n)
                        for k, (a, m) in enumerate(HT):
                            c = bass.ds((e * len(HT) + k) * P, P)
                            ins = pe.matmul(yb[r % 2][:, 0:P], hmt[r % 2][0:m, k, :], w2T[0:m, c], start=(k == 0), stop=(k == len(HT) - 1))
                        ins.then_inc(S["y"].sem, 1)

                    def expert_of(n):
                        col_ = expert[0:1, n:n + 1] if isinstance(n, int) else expert[0:1, bass.ds(n, 1)]
                        return pe.value_load(col_, min_val=0, max_val=EXPERTS - 1)

                    turn_x(0, 0, 1)
                    turn_x(1, 1, 1)
                    turn_x(2, 2, 1)
                    front(0, expert_of(0), 0, False)
                    front(1, expert_of(1), 1, False)
                    turn_h(0, 0, False)
                    with pe.Fori(0, SLOTS // R) as i:
                        e = {2: expert_of(i * R + 2)}
                        for s in range(R):
                            n = i * R + s
                            turn_x(n + 3, (s + 3) % R, i + 1 + (s + 3) // R)
                            front(n + 2, e[s + 2], s + 2, True)
                            for k in ([s + 3] if s + 1 < R else []) + ([s] if s < 2 else []):
                                e[k] = expert_of(i * R + k)
                            turn_h(n + 1, s + 1, True)
                            back(n, e[s], s)

                @block.scalar
                def _(act):
                    def split_x(n, r):
                        w(act, "x_turned", n)
                        act.activation(xh[r % 2][:, :], xb[:, 0:P], ACT.Copy).then_inc(S["x_high"].sem, 1)

                    def silu(n, r):
                        w(act, "h1", n)
                        act.activation(sl[r % 2][:, :], h1b[r % 2][:, 0:HIDP], ACT.Silu).then_inc(S["silu"].sem, 1)

                    act.preload_act_table(ACT.Silu)
                    split_x(0, 0)
                    split_x(1, 1)
                    act.wait_ge(S["h3"].sem, 1)
                    split_x(2, 2)
                    silu(0, 0)
                    silu(1, 1)
                    with act.Fori(0, SLOTS // R) as i:
                        for s in range(R):
                            n = i * R + s
                            act.wait_ge(S["h3"].sem, n + 2)
                            split_x(n + 3, s + 3)
                            w(act, "h_ready", n)
                            silu(n + 2, s + 2)
                            w(act, "y", n)
                            w(act, "y_free", n)
                            act.activation(yt[s][:, :], yb[s % 2][:, 0:P], ACT.Copy).then_inc(S["y_ready"].sem, 1)

                @block.vector
                def _(dve):
                    def split_x(n, r):
                        w(dve, "x_high", n)
                        dve.tensor_tensor(xl[r % 2][:, :], xb[:, 0:P], xh[r % 2][:, :].bitcast(F32), ALU.subtract).then_inc(S["x_low"].sem, 1)

                    def gate_h(n, r):
                        w(dve, "silu", n)
                        w(dve, "h3", n)
                        dve.tensor_tensor(hm[r % 2][:, :], h3b[r % 2][:, 0:HIDP], sl[r % 2][:, :], ALU.mult).then_inc(S["h_ready"].sem, 1)

                    def keep_h(n, r):
                        w(dve, "h_turned", n)
                        dve.tensor_copy(hmt[r % 2][:, 0:2, :], hb[:, 0:2 * P].rearrange("p (k c) -> p k c", c=P))
                        dve.tensor_copy(hmt[r % 2][0:HT[2][1], 2, :], hb[0:HT[2][1], 2 * P:3 * P]).then_inc(S["ht_ready"].sem, 1)

                    def pick_rows(n, r):
                        dve.tensor_copy(lidx[r][:, :], to_load[:, bass.ds(n, 1)]).then_inc(S["row_picked"].sem, 1)

                    for n in range(LEAD):
                        pick_rows(n, n)
                    split_x(0, 0)
                    split_x(1, 1)
                    split_x(2, 2)
                    gate_h(0, 0)
                    gate_h(1, 1)
                    keep_h(0, 0)
                    with dve.Fori(0, SLOTS // R) as i:
                        for s in range(R):
                            n = i * R + s
                            split_x(n + 3, s + 3)
                            w(dve, "h_turned", n)
                            gate_h(n + 2, s + 2)
                            keep_h(n + 1, s + 1)
                            pick_rows(n + LEAD, (s + LEAD) % R)
                            w(dve, "y_free", n)
                            dve.tensor_copy(sidx[s][:, :], to_store[:, bass.ds(n, 1)]).then_inc(S["place_picked"].sem, 1)

        with ExitStack() as ph:
            R, CHUNKS = 4, TOK // CHUNK
            y = [sb(f"y{r}", [P, 2, CT, P], scope=ph) for r in range(R)]
            arrived = [sem(f"arrived{r}", ph) for r in range(R)]
            stored = [sem(f"stored{r}", ph) for r in range(R)]
            scaled, first, both = sem("scaled", ph), sem("first", ph), sem("both", ph)
            mixed_t = mixed.rearrange("(n p) c -> p n c", p=P)
            with nc.Block() as block:
                @block.sync
                def _(sp):
                    for c in range(CHUNKS):
                        if c >= R:
                            sp.wait_ge(both, c - R + 1)
                        for k in range(2):
                            a = ER + k * TILES + c * CT
                            sp.dma_start(y[c % R][:, k, :, :], mixed_t[:, a:a + CT, :]).then_inc(arrived[c % R], 16)

                @block.scalar
                def _(act):
                    def store(c):
                        act.wait_ge(both, c + 1)
                        act.dma_start(out_t[:, c * CT:(c + 1) * CT, :], tok[:, c * CT:(c + 1) * CT, :]).then_inc(stored[c % R], 16)

                    for c in range(CHUNKS):
                        r = c % R
                        act.wait_ge(arrived[r], 32 * (c // R + 1))
                        for j in range(CT):
                            ins = act.activation(y[r][:, 1, j, :], y[r][:, 1, j, :], ACT.Identity, scale=gates[:, c * CT + j, 1:2])
                        ins.then_inc(scaled, 1)
                        if c >= 2:
                            store(c - 2)
                    for c in (CHUNKS - 2, CHUNKS - 1):
                        store(c)
                    for r in range(R):
                        act.wait_ge(stored[r], 16 * (CHUNKS // R))

                @block.vector
                def _(dve):
                    for c in range(CHUNKS):
                        r = c % R
                        dve.wait_ge(arrived[r], 32 * (c // R + 1))
                        for j in range(CT):
                            t = c * CT + j
                            ins = dve.scalar_tensor_tensor(tok[:, t, :], y[r][:, 0, j, :], gates[:, t, 0:1], tok[:, t, :],
                                                           ALU.mult, ALU.add)
                        ins.then_inc(first, 1)

                @block.gpsimd
                def _(pool):
                    for c in range(CHUNKS):
                        pool.wait_ge(first, c + 1)
                        pool.wait_ge(scaled, c + 1)
                        t1 = tok[:, c * CT:(c + 1) * CT, :]
                        pool.tensor_tensor(t1, t1, y[c % R][:, 1, :, :], ALU.add).then_inc(both, 1)


_INPUTS = ["x", "L0_conv_W1", "L0_conv_b1", "L0_conv_W2", "L0_conv_b2", "L1_attn_norm1_g", "L1_attn_norm1_b",
           "L1_attn_Wq", "L1_attn_Wkv", "L1_attn_Wproj", "L1_attn_bproj", "L1_attn_norm2_g", "L1_attn_norm2_b",
           "L1_attn_W1", "L1_attn_b1", "L1_attn_W2", "L1_attn_b2", "L1_ffn_router_w", "L1_ffn_w1", "L1_ffn_w2", "L1_ffn_w3"]


def kernel(**inputs):
    import concourse.bacc as _bacc
    from concourse.bass_utils import run_bass_kernel_spmd as _run

    nc = _bacc.Bacc("TRN2", target_bir_lowering=False, num_devices=1)
    arrays, args = {}, []
    for name in _INPUTS:
        a = np.ascontiguousarray(inputs[name])
        arrays[f"in_{name}"] = a
        args.append(nc.dram_tensor(f"in_{name}", a.shape, mybir.dt.from_np(a.dtype), kind="ExternalInput").ap())
    arrays["in_consts"] = constants()
    args.append(nc.dram_tensor("in_consts", (P, C_ALL), F32, kind="ExternalInput").ap())
    args.append(nc.dram_tensor("normed", (TOK, P), F32, kind="Internal").ap())
    args.append(nc.dram_tensor("mixed", (ER * P + 2 * TOK, P), F32, kind="Internal").ap())
    args.append(nc.dram_tensor("out", (BATCH, SIDE, SIDE, P), F32, kind="ExternalOutput").ap())
    conv_attn_moe(nc, *args)
    r = _run(nc, [arrays], core_ids=[0])
    return r.results[0]["out"]
```
